# Optimizing a Trainium2 kernel written in Bass

```python
import numpy as np
import jax
import jax.numpy as jnp

def _softmax(x, axis=-1):
    return jax.nn.softmax(x, axis=axis)

def _gelu(x):
    return jax.nn.gelu(x, approximate=True)

def _silu(x):
    return jax.nn.silu(x)

def _sigmoid(x):
    return jax.nn.sigmoid(x)

def _layernorm(x, axis=-1, eps=1e-05):
    m = jnp.mean(x, axis=axis, keepdims=True)
    v = jnp.var(x, axis=axis, keepdims=True)
    return (x - m) / jnp.sqrt(v + eps)

def _scatter_add(tgt, idx, src, axis=0):
    return tgt.at[idx].add(src)

def _segment_sum(src, seg, n):
    return jax.ops.segment_sum(src, seg, n)
kernel_name = 'mk_sandwich_d2_jaxref_r8_ade8a8'

def setup_inputs(seed: int=0):
    np.random.seed(seed)
    _w = jnp.asarray

    def _L0_attn_setup():
        import math
        import jax, jax.numpy as jnp
        import numpy as np
        EPS = 1e-06
        NB_FEATURES = 32
        NUM_HEADS = 16

        def fwht(x):
            shape = x.shape
            P = shape[-1]
            h = 1
            while h < P:
                x = x.reshape(shape[:-1] + (-1, 2 * h))
                a, b = (x[..., :h], x[..., h:])
                x = jnp.concatenate([a + b, a - b], axis=-1).reshape(shape)
                h *= 2
            return x

        def apply_rope(q, k):
            C, H, L, D = q.shape
            dtype = q.dtype
            freqs = 10000.0 ** (-jnp.arange(0, D, 2, dtype=dtype) / D)
            pos = jnp.arange(L - 1, dtype=dtype)[:, None]
            ang = pos * freqs
            cos, sin = (jnp.cos(ang), jnp.sin(ang))

            def rot(t):
                ts = t[..., 1:, :]
                t1, t2 = (ts[..., 0::2], ts[..., 1::2])
                re = t1 * cos - t2 * sin
                im = t1 * sin + t2 * cos
                rs = jnp.stack([re, im], axis=-1).reshape(ts.shape)
                return jnp.concatenate([t[..., :1, :], rs], axis=-2)
            return (rot(q), rot(k))

        def sorf_phi(x, signs, scales, m):
            C, H, L, D = x.shape
            R, P = (signs.shape[1], signs.shape[-1])
            x_p = x if D == P else jnp.pad(x, ((0, 0), (0, 0), (0, 0), (0, P - D)))
            inv = 1.0 / math.sqrt(P)
            s1 = signs[None, :, :, 0, None, :]
            s2 = signs[None, :, :, 1, None, :]
            s3 = signs[None, :, :, 2, None, :]
            g = (scales * inv)[None, :, :, None, :]
            t = fwht(x_p[:, :, None, :, :] * s1) * inv
            t = fwht(t * s2) * inv
            t = fwht(t * s3) * inv
            block = t * g
            phi = block.transpose(0, 1, 3, 2, 4).reshape(C, H, L, R * P)[..., :m]
            x_norm_sq = jnp.sum(x * x, axis=-1, keepdims=True) / 2.0
            return jnp.exp(phi - x_norm_sq) / math.sqrt(m)
        key = jax.random.key(seed)
        ks = jax.random.split(key, 5)
        C, L, E = (4, 512, 128)
        H, D = (NUM_HEADS, 128 // NUM_HEADS)
        P = 64
        R = 4
        x = jax.random.normal(ks[0], (C, L, E), dtype=jnp.float32)
        w_qkv = jax.random.normal(ks[1], (3 * E, E), dtype=jnp.float32) / math.sqrt(E)
        w_out = jax.random.normal(ks[2], (E, E), dtype=jnp.float32) / math.sqrt(E)
        sorf_signs = (2.0 * jax.random.randint(ks[3], (H, R, 3, P), 0, 2) - 1.0).astype(jnp.float32)
        sorf_scales = jax.random.normal(ks[4], (H, R, P), dtype=jnp.float32)
        return {'x': x, 'w_qkv': w_qkv, 'w_out': w_out, 'sorf_signs': sorf_signs, 'sorf_scales': sorf_scales}
    _L0_attn_in = _L0_attn_setup()

    def _L0_ffn_setup():
        import jax, jax.numpy as jnp
        import numpy as np
        DIM = 128

        def _reference_tuple_inner(x, W_r, W_k, W_v, mu_r, mu_k):
            B, T, C = x.shape
            x_prev = jnp.concatenate([jnp.zeros((B, 1, C), x.dtype), x[:, :-1, :]], axis=1)
            xr = mu_r * x + (1.0 - mu_r) * x_prev
            xk = mu_k * x + (1.0 - mu_k) * x_prev
            r = jax.nn.sigmoid(jnp.einsum('btc,dc->btd', xr, W_r))
            k = jnp.einsum('btc,dc->btd', xk, W_k)
            k_act = jnp.square(jax.nn.relu(k))
            out = r * jnp.einsum('btc,dc->btd', k_act, W_v)
            new_state = x[:, -1, :]
            return (out, new_state)
        key = jax.random.key(seed)
        ks = jax.random.split(key, 6)
        B, T, C = (8, 256, DIM)
        x = jax.random.normal(ks[0], (B, T, C), dtype=jnp.float32)
        s = 1.0 / np.sqrt(C)
        W_r = jax.random.uniform(ks[1], (C, C), jnp.float32, -s, s)
        W_k = jax.random.uniform(ks[2], (C, C), jnp.float32, -s, s)
        W_v = jax.random.uniform(ks[3], (C, C), jnp.float32, -s, s)
        mu_r = jax.random.uniform(ks[4], (C,), jnp.float32)
        mu_k = jax.random.uniform(ks[5], (C,), jnp.float32)
        return {'x': x, 'W_r': W_r, 'W_k': W_k, 'W_v': W_v, 'mu_r': mu_r, 'mu_k': mu_k}
    _L0_ffn_in = _L0_ffn_setup()

    def _L1_attn_setup():
        import jax, jax.numpy as jnp
        import numpy as np
        key = jax.random.key(seed)
        k_u, k_wl, k_b, k_c = jax.random.split(key, 4)
        B_, T, D, N = (4, 512, 128, 32)
        u = jax.random.normal(k_u, (B_, T, D), dtype=jnp.float32)
        Wl = jax.random.normal(k_wl, (N, D), dtype=jnp.float32) * 0.02
        bl = jnp.full((N,), 2.0, dtype=jnp.float32)
        xav_b = 0.5 * np.sqrt(6.0 / (D + N))
        Wb = jax.random.uniform(k_b, (N, D), dtype=jnp.float32, minval=-xav_b, maxval=xav_b)
        xav_c = 0.5 * np.sqrt(6.0 / (N + D))
        Wc = jax.random.uniform(k_c, (D, N), dtype=jnp.float32, minval=-xav_c, maxval=xav_c)
        Dp = jnp.zeros((D,), dtype=jnp.float32)
        return {'u': u, 'Wl': Wl, 'bl': bl, 'Wb': Wb, 'Wc': Wc, 'Dp': Dp}
    _L1_attn_in = _L1_attn_setup()

    def _L1_ffn_setup():
        import jax, jax.numpy as jnp
        import numpy as np
        B, S, D = (1, 256, 128)
        E, K, F = (8, 2, 176)
        NS = 2
        SCALE = 2.5

        def _swiglu_mlp(x, wg, wu, wd):
            return jax.nn.silu(x @ wg) * (x @ wu) @ wd
        key = jax.random.key(seed)
        ks = jax.random.split(key, 8)
        s = 0.02
        return {'hidden_states': jax.random.normal(ks[0], (B, S, D), jnp.float32), 'gate_w': jax.random.normal(ks[1], (E, D), jnp.float32) * s, 'w_gate': jax.random.normal(ks[2], (E, D, F), jnp.float32) * s, 'w_up': jax.random.normal(ks[3], (E, D, F), jnp.float32) * s, 'w_down': jax.random.normal(ks[4], (E, F, D), jnp.float32) * s, 'sw_gate': jax.random.normal(ks[5], (D, F * NS), jnp.float32) * s, 'sw_up': jax.random.normal(ks[6], (D, F * NS), jnp.float32) * s, 'sw_down': jax.random.normal(ks[7], (F * NS, D), jnp.float32) * s}
    _L1_ffn_in = _L1_ffn_setup()
    _d = {'L0_attn_x': _L0_attn_in['x'], 'L0_attn_w_qkv': _L0_attn_in['w_qkv'], 'L0_attn_w_out': _L0_attn_in['w_out'], 'L0_attn_sorf_signs': _L0_attn_in['sorf_signs'], 'L0_attn_sorf_scales': _L0_attn_in['sorf_scales'], 'L0_ffn_W_r': _L0_ffn_in['W_r'], 'L0_ffn_W_k': _L0_ffn_in['W_k'], 'L0_ffn_W_v': _L0_ffn_in['W_v'], 'L0_ffn_mu_r': _L0_ffn_in['mu_r'], 'L0_ffn_mu_k': _L0_ffn_in['mu_k'], 'L1_attn_Wl': _L1_attn_in['Wl'], 'L1_attn_bl': _L1_attn_in['bl'], 'L1_attn_Wb': _L1_attn_in['Wb'], 'L1_attn_Wc': _L1_attn_in['Wc'], 'L1_attn_Dp': _L1_attn_in['Dp'], 'L1_ffn_gate_w': _L1_ffn_in['gate_w'], 'L1_ffn_w_gate': _L1_ffn_in['w_gate'], 'L1_ffn_w_up': _L1_ffn_in['w_up'], 'L1_ffn_w_down': _L1_ffn_in['w_down'], 'L1_ffn_sw_gate': _L1_ffn_in['sw_gate'], 'L1_ffn_sw_up': _L1_ffn_in['sw_up'], 'L1_ffn_sw_down': _L1_ffn_in['sw_down']}
    _x0 = _d['L0_attn_x']
    _d['L0_attn_x'] = jax.random.normal(jax.random.fold_in(jax.random.key(seed), 1), (8, 1024, 128), dtype=_x0.dtype)
    del _x0
    return _d

def reference(L0_attn_x, L0_attn_w_qkv, L0_attn_w_out, L0_attn_sorf_signs, L0_attn_sorf_scales, L0_ffn_W_r, L0_ffn_W_k, L0_ffn_W_v, L0_ffn_mu_r, L0_ffn_mu_k, L1_attn_Wl, L1_attn_bl, L1_attn_Wb, L1_attn_Wc, L1_attn_Dp, L1_ffn_gate_w, L1_ffn_w_gate, L1_ffn_w_up, L1_ffn_w_down, L1_ffn_sw_gate, L1_ffn_sw_up, L1_ffn_sw_down):

    def _L0_attn_ref(x, w_qkv, w_out, sorf_signs, sorf_scales):
        import math
        import jax, jax.numpy as jnp
        import numpy as np
        EPS = 1e-06
        NB_FEATURES = 32
        NUM_HEADS = 16

        def fwht(x):
            shape = x.shape
            P = shape[-1]
            h = 1
            while h < P:
                x = x.reshape(shape[:-1] + (-1, 2 * h))
                a, b = (x[..., :h], x[..., h:])
                x = jnp.concatenate([a + b, a - b], axis=-1).reshape(shape)
                h *= 2
            return x

        def apply_rope(q, k):
            C, H, L, D = q.shape
            dtype = q.dtype
            freqs = 10000.0 ** (-jnp.arange(0, D, 2, dtype=dtype) / D)
            pos = jnp.arange(L - 1, dtype=dtype)[:, None]
            ang = pos * freqs
            cos, sin = (jnp.cos(ang), jnp.sin(ang))

            def rot(t):
                ts = t[..., 1:, :]
                t1, t2 = (ts[..., 0::2], ts[..., 1::2])
                re = t1 * cos - t2 * sin
                im = t1 * sin + t2 * cos
                rs = jnp.stack([re, im], axis=-1).reshape(ts.shape)
                return jnp.concatenate([t[..., :1, :], rs], axis=-2)
            return (rot(q), rot(k))

        def sorf_phi(x, signs, scales, m):
            C, H, L, D = x.shape
            R, P = (signs.shape[1], signs.shape[-1])
            x_p = x if D == P else jnp.pad(x, ((0, 0), (0, 0), (0, 0), (0, P - D)))
            inv = 1.0 / math.sqrt(P)
            s1 = signs[None, :, :, 0, None, :]
            s2 = signs[None, :, :, 1, None, :]
            s3 = signs[None, :, :, 2, None, :]
            g = (scales * inv)[None, :, :, None, :]
            t = fwht(x_p[:, :, None, :, :] * s1) * inv
            t = fwht(t * s2) * inv
            t = fwht(t * s3) * inv
            block = t * g
            phi = block.transpose(0, 1, 3, 2, 4).reshape(C, H, L, R * P)[..., :m]
            x_norm_sq = jnp.sum(x * x, axis=-1, keepdims=True) / 2.0
            return jnp.exp(phi - x_norm_sq) / math.sqrt(m)
        C, L, E = x.shape
        H = NUM_HEADS
        D = E // H
        qkv = x @ w_qkv.T
        q, k, v = jnp.split(qkv, 3, axis=-1)
        to_heads = lambda t: t.reshape(C, L, H, D).transpose(0, 2, 1, 3)
        q, k, v = (to_heads(q), to_heads(k), to_heads(v))
        q, k = apply_rope(q, k)
        q_phi = sorf_phi(q, sorf_signs, sorf_scales, NB_FEATURES)
        k_phi = sorf_phi(k, sorf_signs, sorf_scales, NB_FEATURES)
        S = jnp.einsum('chlm,chld->chmd', k_phi, v)
        sum_k = jnp.sum(k_phi, axis=2)
        numer = jnp.einsum('chlm,chmd->chld', q_phi, S)
        denom = jnp.maximum(jnp.einsum('chlm,chm->chl', q_phi, sum_k), EPS)
        out_heads = numer / denom[..., None]
        out = out_heads.transpose(0, 2, 1, 3).reshape(C, L, E)
        return out @ w_out.T

    def _L0_ffn_ref(x, W_r, W_k, W_v, mu_r, mu_k):
        import jax, jax.numpy as jnp
        import numpy as np
        DIM = 128

        def _reference_tuple_inner(x, W_r, W_k, W_v, mu_r, mu_k):
            B, T, C = x.shape
            x_prev = jnp.concatenate([jnp.zeros((B, 1, C), x.dtype), x[:, :-1, :]], axis=1)
            xr = mu_r * x + (1.0 - mu_r) * x_prev
            xk = mu_k * x + (1.0 - mu_k) * x_prev
            r = jax.nn.sigmoid(jnp.einsum('btc,dc->btd', xr, W_r))
            k = jnp.einsum('btc,dc->btd', xk, W_k)
            k_act = jnp.square(jax.nn.relu(k))
            out = r * jnp.einsum('btc,dc->btd', k_act, W_v)
            new_state = x[:, -1, :]
            return (out, new_state)
        return _reference_tuple_inner(x, W_r, W_k, W_v, mu_r, mu_k)[0]

    def _L1_attn_ref(u, Wl, bl, Wb, Wc, Dp):
        import jax, jax.numpy as jnp
        import numpy as np
        lam = jax.nn.sigmoid(jnp.einsum('btd,nd->btn', u, Wl) + bl)
        Bu = jnp.einsum('btd,nd->btn', u, Wb)

        def step(h, inp):
            lam_t, bu_t = inp
            h = lam_t * h + bu_t
            return (h, h)
        h0 = jnp.zeros((u.shape[0], Wl.shape[0]), dtype=u.dtype)
        _, H = jax.lax.scan(step, h0, (jnp.swapaxes(lam, 0, 1), jnp.swapaxes(Bu, 0, 1)))
        H = jnp.swapaxes(H, 0, 1)
        y = jnp.einsum('btn,dn->btd', H, Wc) + u * Dp
        return y

    def _L1_ffn_ref(hidden_states, gate_w, w_gate, w_up, w_down, sw_gate, sw_up, sw_down):
        import jax, jax.numpy as jnp
        import numpy as np
        B, S, D = (1, 256, 128)
        E, K, F = (8, 2, 176)
        NS = 2
        SCALE = 2.5

        def _swiglu_mlp(x, wg, wu, wd):
            return jax.nn.silu(x @ wg) * (x @ wu) @ wd
        identity = hidden_states
        x = hidden_states.reshape(-1, hidden_states.shape[-1])
        T = x.shape[0]
        logits = x.astype(jnp.float32) @ gate_w.astype(jnp.float32).T
        scores = jax.nn.softmax(logits, axis=-1)
        topk_w, topk_i = jax.lax.top_k(scores, K)
        topk_w = topk_w / (topk_w.sum(-1, keepdims=True) + 1e-20) * SCALE
        combine = jnp.zeros((T, E), jnp.float32).at[jnp.arange(T)[:, None], topk_i].set(topk_w)
        g = jax.nn.silu(jnp.einsum('td,edf->etf', x, w_gate)) * jnp.einsum('td,edf->etf', x, w_up)
        expert_out = jnp.einsum('etf,efd->etd', g, w_down)
        y = jnp.einsum('te,etd->td', combine, expert_out).astype(x.dtype)
        y = y.reshape(identity.shape)
        return y + _swiglu_mlp(identity, sw_gate, sw_up, sw_down)
    x = L0_attn_x
    x = x + _layernorm(_L0_attn_ref(_layernorm(x, axis=-1), L0_attn_w_qkv, L0_attn_w_out, L0_attn_sorf_signs, L0_attn_sorf_scales), axis=-1)
    x = x + _layernorm(_L0_ffn_ref(_layernorm(x, axis=-1), L0_ffn_W_r, L0_ffn_W_k, L0_ffn_W_v, L0_ffn_mu_r, L0_ffn_mu_k), axis=-1)
    x = x + _layernorm(_L1_attn_ref(_layernorm(x, axis=-1), L1_attn_Wl, L1_attn_bl, L1_attn_Wb, L1_attn_Wc, L1_attn_Dp), axis=-1)
    x = x + _layernorm(_L1_ffn_ref(_layernorm(x, axis=-1), L1_ffn_gate_w, L1_ffn_w_gate, L1_ffn_w_up, L1_ffn_w_down, L1_ffn_sw_gate, L1_ffn_sw_up, L1_ffn_sw_down), axis=-1)
    return x

_drawn_inputs = setup_inputs


def setup_inputs(seed=0):
    import zlib

    import numpy as np

    out = dict(_drawn_inputs(seed))
    spreads = {'L1_attn_bl': (2.0, 0.2), 'L1_attn_Dp': (0.0, 0.1)}
    factors = {}
    for name, (base, spread) in spreads.items():
        noise = np.random.default_rng([zlib.crc32(name.encode()), seed]).standard_normal(out[name].shape)
        drawn = base * np.exp(spread * noise) if base else spread * noise
        out[name] = jnp.asarray(drawn.astype(out[name].dtype))
    for name, factor in factors.items():
        out[name] = (out[name] * factor).astype(out[name].dtype)
    return out
```

```python
from contextlib import ExitStack

import numpy as np

import concourse.bass as bass
from concourse import mybir

F32 = mybir.dt.float32
F32R = mybir.dt.float32r
ALU = mybir.AluOpType
ACT = mybir.ActivationFunctionType

P = 128
B, L, D = 8, 1024, 128
TB = 512
TPB = TB // P
NB = B * L // TB
BPS = L // TB
H, DH = 16, 8
M = 32
PP = 64
HH = H // 2
GH = P // M
NG = H // GH
VW = DH + 1
NS = 32
E, F = 8, 176
SF = 352
EQ = P // E
JE = F // EQ
HF = E * F + SF
NJ = -(-HF // P)
LAST = HF - (NJ - 1) * P
LN_EPS = 1e-5
DEN_EPS = 1e-6
TOP_EPS = 1e-20
ROUTE_SCALE = 2.5

C_COS, C_SIN = 0, L
C_ID = 2 * L
C_HAD = C_ID + P
C_M8 = C_HAD + PP
C_M4 = C_M8 + HH
C_N = C_M4 + GH


def rows(j):
    return P if j < NJ - 1 else LAST


def build(nc, x, wqkv, wout, consts, s1c, s23, scl, wr, wk, wv, mu, wlb, bl, wc, dp, gate, wg, wu, wd, out):
    ctx = ExitStack()
    with ctx:
        def sb(name, shape, dt=F32):
            return ctx.enter_context(nc.sbuf_tensor(name, shape, dt))

        def sem(name):
            return ctx.enter_context(nc.semaphore(name))

        banks = [ctx.enter_context(nc.psum_tensor(f"bank{i}", [P, TB], F32)) for i in range(8)]

        xres = sb("xres", [P, NB * TB])
        cst = sb("cst", [P, C_N])
        ident = cst[:, C_ID:C_ID + P]
        had = cst[0:PP, C_HAD:C_HAD + PP]
        wout_sb = sb("wout_sb", [P, D])
        s1_sb = sb("s1_sb", [PP, 2])
        s23_sb = sb("s23_sb", [PP, 2, H])
        scl_sb = sb("scl_sb", [PP, 2, M])
        wr_sb, wk_sb, wv_sb = sb("wr_sb", [P, D]), sb("wk_sb", [P, D]), sb("wv_sb", [P, D])
        mu_sb = sb("mu_sb", [P, 2])
        wlb_sb = sb("wlb_sb", [P, 2 * NS])
        bl_sb = sb("bl_sb", [NS, 1])
        wc_sb = sb("wc_sb", [NS, D])
        dp_sb = sb("dp_sb", [P, 1])
        dpd_sb = sb("dpd_sb", [P, P])
        gate_sb = sb("gate_sb", [P, E])
        blh_sb = sb("blh_sb", [NS, 1])
        wstage = sb("wstage", [P, HF])
        gate_hi, gate_lo = sb("gate_hi", [P, E], F32R), sb("gate_lo", [P, E], F32R)
        wg_hi, wg_lo = sb("wg_hi", [P, HF], F32R), sb("wg_lo", [P, HF], F32R)
        wu_hi, wu_lo = sb("wu_hi", [P, HF], F32R), sb("wu_lo", [P, HF], F32R)
        wd_sb = sb("wd_sb", [P, NJ, D])
        feat = sb("feat", [P, 2, HH, M])
        sorf_a = sb("sorf_a", [PP, H, DH])
        sorf_b = sb("sorf_b", [PP, H, DH])
        sorf_c = sb("sorf_c", [PP, 2, M])
        sorf_d = sb("sorf_d", [PP, 2, M])
        mhalf = sb("mhalf", [P, 8])

        bn = sb("bn", [P, 2, TPB, 6])
        mv = sb("mv", [P, 2, TPB, 5])
        rs = sb("rs", [P, 2, 3, TPB])
        ybn = sb("ybn", [P, 2, TPB, 6])
        ymv = sb("ymv", [P, 2, TPB, 5])
        yrs = sb("yrs", [P, 2, 3, TPB])
        nm = sb("nm", [P, 2, TPB])
        ynm = sb("ynm", [P, 2, TPB])
        xn = sb("xn", [P, 2, TPB, D])
        xt = sb("xt", [P, 2, TB])
        tmp = sb("tmp", [P, 2, TB])

        s_cst, s_wA, s_wB, s_wC, s_w1, s_w2, s_w3 = (sem(n) for n in
            ("s_cst", "s_wA", "s_wB", "s_wC", "s_w1", "s_w2", "s_w3"))
        s_x = [sem(f"s_x{i}") for i in range(2)]
        s_prep = sem("s_prep")
        s_sorf_v, s_sorf_p = sem("s_sorf_v"), sem("s_sorf_p")
        s_dpd = sem("s_dpd")
        s_wsplit = sem("s_wsplit")
        s_out = sem("s_out")

        class Phase:
            def __init__(self, n):
                self.bn = sem(n + "_bn")
                self.mv = sem(n + "_mv")
                self.rs = sem(n + "_rs")
                self.xn = sem(n + "_xn")
                self.tr = sem(n + "_tr")
                self.xt = sem(n + "_xt")
                self.y = sem(n + "_y")
                self.ybn = sem(n + "_ybn")
                self.ymv = sem(n + "_ymv")
                self.yrs = sem(n + "_yrs")
                self.tmp = sem(n + "_tmp")
                self.xa = sem(n + "_xa")

        A, Bp, C, R, X = Phase("a"), Phase("b"), Phase("c"), Phase("r"), Phase("x")

        class Norm:
            def __init__(self, n):
                self.st = sb(n + "_st", [P, 2, TPB, 6])
                self.m = sb(n + "_m", [P, 2, TPB, 5])
                self.r = sb(n + "_r", [P, 2, 3, TPB])
                self.n = sb(n + "_n", [P, 2, TPB])

        def after(eng, s, n):
            if not isinstance(n, int) or n > 0:
                eng.wait_ge(s, n)

        def blk(t, b):
            return t[:, bass.ds(b * TB, TB)]

        def tile(t, b, i):
            return t[:, bass.ds(b * TB + i * P, P)]

        def aggregate(dve, stats, m, par, seen, done, b):
            dve.wait_ge(seen, 4 * b + 1)
            s = stats[:, par, :, :]
            dve.tensor_tensor(m[:, par, :, 2], s[:, :, 1], s[:, :, 4], ALU.subtract).then_inc(seen, 1)
            dve.tensor_tensor(m[:, par, :, 3], s[:, :, 2], s[:, :, 5], ALU.add)
            dve.tensor_tensor(m[:, par, :, 0], s[:, :, 1], s[:, :, 4], ALU.add)
            dve.wait_ge(seen, 4 * b + 2)
            dve.scalar_tensor_tensor(out=m[:, par, :, 4], in0=m[:, par, :, 2], scalar=D / 4.0,
                                     in1=m[:, par, :, 2], op0=ALU.mult, op1=ALU.mult).then_inc(seen, 2)
            dve.wait_ge(seen, 4 * b + 4)
            dve.tensor_tensor(m[:, par, :, 1], m[:, par, :, 3], m[:, par, :, 4], ALU.add).then_inc(done, 1)

        def ln_stats(dve, ph, b, par):
            for i in range(TPB):
                ins = dve.bn_stats(bn[:, par, i, :], tile(xres, b, i))
            ins.then_inc(ph.bn, 1)
            aggregate(dve, bn, mv, par, ph.bn, ph.mv, b)

        def root(pool, ready, done, m, r, n, b, par, eps=LN_EPS):
            pool.wait_ge(ready, b + 1)
            pool.tensor_tensor(n[:, par, :], m[:, par, :, 0], mhalf[:, 0:TPB], ALU.mult).then_inc(done, 1)
            pool.tensor_scalar(r[:, par, 0, :], m[:, par, :, 1], 1.0 / D, eps, ALU.mult, ALU.add).then_inc(done, 1)
            pool.wait_ge(done, 4 * b + 2)
            pool.tensor_tensor(r[:, par, 1, :], r[:, par, 0, :], mhalf[:, 0:TPB], ALU.pow).then_inc(done, 1)
            pool.wait_ge(done, 4 * b + 3)
            pool.tensor_tensor(r[:, par, 2, :], n[:, par, :], r[:, par, 1, :], ALU.mult).then_inc(done, 1)

        def ln_norm(dve, ph, b, par, has_prev):
            dve.wait_ge(ph.rs, 4 * b + 4)
            if has_prev:
                dve.wait_ge(ph.tr, b - 1)
            for i in range(TPB):
                ins = dve.tensor_scalar(xn[:, par, i, :], tile(xres, b, i), rs[:, par, 1, i:i + 1],
                                        rs[:, par, 2, i:i + 1], ALU.mult, ALU.add)
            ins.then_inc(ph.xn, 1)

        def transposes(pe, ph, b, par):
            pe.wait_ge(ph.xn, b + 1)
            for i in range(TPB):
                ins = pe.transpose(banks[0][:, i * P:(i + 1) * P], xn[:, par, i, :], ident)
            ins.then_inc(ph.tr, 1)

        def y_stats(dve, ph, b, par, y):
            dve.wait_ge(ph.y, b + 1)
            for i in range(TPB):
                ins = dve.bn_stats(ybn[:, par, i, :], y[:, i * P:(i + 1) * P])
            ins.then_inc(ph.ybn, 1)
            aggregate(dve, ybn, ymv, par, ph.ybn, ph.ymv, b)

        def y_apply(act, ph, b, par, y, has_prev):
            act.wait_ge(ph.yrs, 4 * b + 4)
            if has_prev:
                act.wait_ge(ph.xa, b - 1)
            for i in range(TPB):
                ins = act.activation(tmp[:, par, i * P:(i + 1) * P], y[:, i * P:(i + 1) * P], ACT.Identity,
                                     scale=yrs[:, par, 1, i:i + 1], bias=yrs[:, par, 2, i:i + 1])
            ins.then_inc(ph.tmp, 1)

        def residual(pool, ph, b, par):
            pool.wait_ge(ph.tmp, b + 1)
            pool.tensor_tensor(blk(xres, b), blk(xres, b), tmp[:, par, :], ALU.add).then_inc(ph.xa, 1)

        def sweep(eng, pair, n=NB):
            pair(0, True, False)
            with eng.Fori(1, n // 2 - 1) as s:
                pair(s * 2, False, False)
            pair(n - 2, False, True)

        def sublayer_done(eng, ph):
            eng.wait_ge(ph.xa, NB)

        early = ExitStack()

        def tmp_sb(name, shape, dt=F32):
            return early.enter_context(nc.sbuf_tensor(name, shape, dt))

        wqkv_sb = tmp_sb("wqkv_sb", [P, 5 * D])

        cat_q = tmp_sb("cat_q", [P, 2, 2, TB])
        cat_k = tmp_sb("cat_k", [P, 2, TB])
        rot = tmp_sb("rot", [P, 2, TB])
        vals = tmp_sb("vals", [P, 2, TPB, H, VW])
        kphi = tmp_sb("kphi", [P, 2, H * M])
        qphi = tmp_sb("qphi", [P, 2, TB])
        sbd = tmp_sb("sbd", [P, NG, GH, VW])
        den = tmp_sb("den", [P, TPB, H])
        rden = tmp_sb("rden", [P, TPB, H])
        o_sb = tmp_sb("o_sb", [P, 2, TPB, H, DH])
        ot_sb = tmp_sb("ot_sb", [P, TB])
        a_q, a_qs = sem("a_q"), sem("a_qs")
        a_rot = sem("a_rot")
        a_catr = sem("a_catr")
        a_cats = sem("a_cats")
        a_vp, a_v = sem("a_vp"), sem("a_v")
        a_ones = sem("a_ones")
        a_fk, a_ek = sem("a_fk"), sem("a_ek")
        a_s = sem("a_s")
        a_sbd = sem("a_sbd")
        a_fq, a_eq = sem("a_fq"), sem("a_eq")
        a_o = sem("a_o")
        a_den = sem("a_den")
        a_on = sem("a_on")
        a_ot, a_ots = sem("a_ot"), sem("a_ots")
        O01, O23 = banks[6], banks[3]
        S0, O0 = 0, NG * GH * VW
        OW = H * VW

        def a_front_pe(pe, b, par, first):
            if not first:
                pe.wait_ge(a_v, b)
                pe.wait_ge(a_ots, b - 2)
            transposes(pe, A, b, par)
            pe.wait_ge(A.xt, b + 1)
            for n in range(2):
                if n or not first:
                    pe.wait_ge(a_rot, 4 * b + 2 * n)
                pe.matmul(banks[1][:, :], wqkv_sb[:, 2 * n * D:(2 * n + 1) * D], xt[:, par, :],
                          start=True, stop=True).then_inc(a_q, 1)
                pe.matmul(banks[2][:, :], wqkv_sb[:, (2 * n + 1) * D:(2 * n + 2) * D], xt[:, par, :],
                          start=True, stop=True).then_inc(a_qs, 1)
                if n == 0:
                    for i in range(TPB):
                        ins = pe.matmul(banks[0][:, i * P:(i + 1) * P], xt[:, par, i * P:(i + 1) * P],
                                        wqkv_sb[:, 4 * D:5 * D], start=True, stop=True)
                    ins.then_inc(a_vp, 1)

        def a_keys_pe(pe, b, par, seq, first_block, has_prev):
            pe.wait_ge(a_cats, 2 * b + 2)
            pe.wait_ge(a_v, b + 1)
            if first_block and has_prev:
                pe.wait_ge(a_den, 3 * b)
                pe.wait_ge(a_on, b)

            def features(i):
                if has_prev or not first_block or i >= 2:
                    pe.wait_ge(a_ek, TPB * b + i - 1)
                if i < 2 and has_prev and first_block:
                    pe.wait_ge(a_eq, NG * b)
                for h in range(2):
                    ins = pe.matmul(banks[4 + i % 2][:, h * HH * M:(h + 1) * HH * M],
                                    cat_k[:, h, i * P:(i + 1) * P], feat[:, h, :, :], start=True, stop=True)
                ins.then_inc(a_fk, 1)

            def state(i):
                pe.wait_ge(a_ek, TPB * b + i + 1)
                for g in range(NG):
                    ins = pe.matmul(banks[3][:, S0 + g * GH * VW:S0 + (g + 1) * GH * VW],
                                    kphi[:, i % 2, g * P:(g + 1) * P], vals[:, par, i, g * GH:(g + 1) * GH, :],
                                    start=(first_block and i == 0 and g == 0), stop=True, skip_group_check=True)
                ins.then_inc(a_s, 1)

            features(0)
            for i in range(1, TPB):
                features(i)
                state(i - 1)
            state(TPB - 1)

        def a_query_pe(pe, b, par, seq, has_prev):
            def features(g):
                if g < 2 and par == 0:
                    pe.wait_ge(a_ek, TPB * (b + 2))
                elif has_prev or par or g >= 2:
                    pe.wait_ge(a_eq, NG * b + g - 1)
                pe.matmul(banks[4 + g % 2][:, :], feat[:, g // 2, (g % 2) * GH:(g % 2 + 1) * GH, :],
                          cat_q[:, par, g // 2, :], start=True, stop=True).then_inc(a_fq, 1)

            def outputs(g):
                pe.wait_ge(a_eq, NG * b + g + 1)
                if g == 0:
                    pe.wait_ge(a_sbd, seq + 1)
                    if par or has_prev:
                        pe.wait_ge(a_on, b)
                for i in range(TPB):
                    bank, c = (O01, i * OW) if i < 2 else (O23, O0 + (i - 2) * OW)
                    ins = pe.matmul(bank[:, c + g * GH * VW:c + (g + 1) * GH * VW],
                                    qphi[:, g % 2, i * P:(i + 1) * P], sbd[:, g, :, :], start=True, stop=True)
                ins.then_inc(a_o, 1)

            pe.wait_ge(a_cats, 2 * b + 2)
            features(0)
            for g in range(1, NG):
                features(g)
                outputs(g - 1)
            outputs(NG - 1)

        def a_back_pe(pe, b, par, end=False):
            pe.wait_ge(a_v, NB if end else b + 3)
            if par or not isinstance(b, int) or b:
                pe.wait_ge(a_ots, b)
            pe.wait_ge(a_on, b + 1)
            for i in range(TPB):
                ins = pe.transpose(banks[0][:, i * P:(i + 1) * P],
                                   o_sb[:, par, i, :, :].rearrange("p h d -> p (h d)"), ident)
            ins.then_inc(a_ot, 1)

        def a_proj_pe(pe, b, par, has_prev):
            pe.wait_ge(a_ots, b + 1)
            if has_prev:
                pe.wait_ge(A.tmp, b)
            for i in range(TPB):
                ins = pe.matmul(banks[7][:, i * P:(i + 1) * P], ot_sb[:, i * P:(i + 1) * P], wout_sb[:, :],
                                start=True, stop=True)
            ins.then_inc(A.y, 1)

        def a_cat_dve(dve, b, par, pos, has_prev):
            for n in range(2):
                dve.wait_ge(a_q, 2 * b + n + 1)
                if n or has_prev:
                    dve.wait_ge(a_catr, 2 * b + n)
                dve.tensor_tensor(rot[:, 0, :], banks[1][:, :], cst[:, C_COS + pos:C_COS + pos + TB],
                                  ALU.mult).then_inc(a_rot, 1)
                dve.wait_ge(a_qs, 2 * b + n + 1)
                dve.tensor_tensor(rot[:, 1, :], banks[2][:, :], cst[:, C_SIN + pos:C_SIN + pos + TB],
                                  ALU.mult).then_inc(a_rot, 1)
                dve.wait_ge(a_rot, 4 * b + 2 * n + 2)
                if n == 0 and has_prev:
                    dve.wait_ge(a_fq, NG * (b - 1))
                if n == 1 and (has_prev or par):
                    dve.wait_ge(a_fk, TPB * b)
                for h in range(2):
                    dst = cat_k[0:PP, h, :] if n else cat_q[0:PP, par, h, :]
                    ins = dve.tensor_tensor(dst, rot[h * PP:(h + 1) * PP, 0, :], rot[h * PP:(h + 1) * PP, 1, :],
                                            ALU.add)
                ins.then_inc(a_catr, 1)

        def a_state_dve(dve, seq):
            dve.wait_ge(a_s, (seq + 1) * BPS * TPB)
            dve.tensor_tensor(sbd[:, :, :, :],
                              banks[3][:, S0:S0 + OW].rearrange("p (g h v) -> p g h v", g=NG, h=GH),
                              cst[:, C_M4:C_M4 + GH].unsqueeze(1).unsqueeze(3).broadcast_to([P, NG, GH, VW]),
                              ALU.mult).then_inc(a_sbd, 1)

        def a_divide_dve(dve, b, par, has_prev):
            dve.wait_ge(a_o, NG * (b + 1))
            if par or has_prev:
                dve.wait_ge(a_on, b)
            for n, (bank, c) in enumerate(((O01, 0), (O23, O0))):
                v = bank[:, c:c + 2 * OW].rearrange("p (t h v) -> p t h v", t=2, h=H)
                dve.tensor_scalar(den[:, 2 * n:2 * n + 2, :], v[:, :, :, DH], DEN_EPS, None,
                                  ALU.max).then_inc(a_den, 1)
            dve.wait_ge(a_den, 3 * b + 2)
            dve.reciprocal(rden[:, :, :], den[:, :, :]).then_inc(a_den, 1)
            dve.wait_ge(a_den, 3 * b + 3)
            if has_prev:
                dve.wait_ge(a_ot, b - 1)
            for n, (bank, c) in enumerate(((O01, 0), (O23, O0))):
                v = bank[:, c:c + 2 * OW].rearrange("p (t h v) -> p t h v", t=2, h=H)
                ins = dve.tensor_tensor(o_sb[:, par, 2 * n:2 * n + 2, :, :], v[:, :, :, 0:DH],
                                        rden[:, 2 * n:2 * n + 2, :].unsqueeze(3).broadcast_to([P, 2, H, DH]),
                                        ALU.mult)
            ins.then_inc(a_on, 1)

        def a_front_act(act, b, par, has_prev):
            act.wait_ge(A.tr, b + 1)
            if has_prev:
                act.wait_ge(a_qs, 2 * (b - 1))
            act.activation(xt[:, par, :], banks[0][:, :], ACT.Copy).then_inc(A.xt, 1)
            act.wait_ge(a_vp, b + 1)
            if has_prev:
                act.wait_ge(a_s, TPB * (b - 1))
            act.activation(vals[:, par, :, :, 0:DH].rearrange("p t h v -> p (t h) v"),
                           banks[0][:, :].rearrange("p (t h v) -> p (t h) v", t=TPB, h=H),
                           ACT.Copy).then_inc(a_v, 1)
            act.wait_ge(a_catr, 2 * b + 1)
            for h in range(2):
                ins = act.activation(cat_q[PP:P, par, h, :], cat_q[0:PP, par, h, :], ACT.Square)
            ins.then_inc(a_cats, 1)

        def a_squares_k_act(act, b):
            act.wait_ge(a_catr, 2 * b + 2)
            for h in range(2):
                ins = act.activation(cat_k[PP:P, h, :], cat_k[0:PP, h, :], ACT.Square)
            ins.then_inc(a_cats, 1)

        def a_keys_act(act, b, par, has_prev):
            for i in range(TPB):
                act.wait_ge(a_fk, TPB * b + i + 1)
                if has_prev or par or i >= 2:
                    act.wait_ge(a_s, TPB * b + i - 1)
                act.activation(kphi[:, i % 2, :], banks[4 + i % 2][:, :], ACT.Exp).then_inc(a_ek, 1)

        def a_query_act(act, b, par, has_prev):
            for g in range(NG):
                act.wait_ge(a_fq, NG * b + g + 1)
                if has_prev or par or g >= 2:
                    act.wait_ge(a_o, NG * b + g - 1)
                act.activation(qphi[:, g % 2, :], banks[4 + g % 2][:, :], ACT.Exp).then_inc(a_eq, 1)

        def a_back_act(act, b, has_prev):
            act.wait_ge(a_ot, b + 1)
            if has_prev:
                act.wait_ge(A.y, b)
            act.activation(ot_sb[:, :], banks[0][:, :], ACT.Copy).then_inc(a_ots, 1)

        early.close()

        LR, LC, LB = 1, 2, 3
        nb, nyb, ncx, nyc, nr, nx = (Norm(n) for n in ("nb", "nyb", "nc", "nyc", "nr", "nx"))

        def stats(dve, n, b, par, src, seen, done):
            for i in range(TPB):
                ins = dve.bn_stats(n.st[:, par, i, :], src(i))
            ins.then_inc(seen, 1)
            aggregate(dve, n.st, n.m, par, seen, done, b)

        def normalise(dve, ph, n, b, par, dst):
            dve.wait_ge(ph.rs, 4 * b + 4)
            after(dve, ph.tr, b)
            for i in range(TPB):
                ins = dve.tensor_scalar(dst[:, i, :], tile(xres, b, i), n.r[:, par, 1, i:i + 1],
                                        n.r[:, par, 2, i:i + 1], ALU.mult, ALU.add)
            ins.then_inc(ph.xn, 1)

        def transpose(pe, ph, b, src):
            pe.wait_ge(ph.xn, b + 1)
            for i in range(TPB):
                ins = pe.transpose(banks[0][:, i * P:(i + 1) * P], src[:, i, :], ident)
            ins.then_inc(ph.tr, 1)

        def apply(act, ph, n, b, par, y, dst):
            act.wait_ge(ph.yrs, 4 * b + 4)
            after(act, ph.xa, b)
            for i in range(TPB):
                ins = act.activation(dst[:, i * P:(i + 1) * P], y[:, i * P:(i + 1) * P], ACT.Identity,
                                     scale=n.r[:, par, 1, i:i + 1], bias=n.r[:, par, 2, i:i + 1])
            ins.then_inc(ph.tmp, 1)

        p_seen, d_seen = sem("p_seen"), sem("d_seen")

        def add_residual(pool, ph, b, src):
            pool.wait_ge(ph.tmp, b + 1)
            pool.nop().then_inc(p_seen, 1)
            pool.tensor_tensor(blk(xres, b), blk(xres, b), src[:, :], ALU.add).then_inc(ph.xa, 1)

        xnb = sb("xnb", [P, TPB, D])
        xs = sb("xs", [P, 2, TB + 1])
        dx = sb("dx", [P, TB])
        xr, xk = sb("xr", [P, TB]), sb("xk", [P, TB])
        krelu = sb("krelu", [P, TB])
        kact = sb("kact", [P, TB])
        rgate = sb("rgate", [P, TB])
        yb = sb("yb", [P, TB])
        tmpb = sb("tmpb", [P, TB])
        b_x0 = sem("b_x0")
        b_zero = sem("b_zero")
        b_dx, b_xr, b_xk = sem("b_dx"), sem("b_xr"), sem("b_xk")
        b_k, b_r, b_v = sem("b_k"), sem("b_r"), sem("b_v")
        b_kr, b_ka, b_rg = sem("b_kr"), sem("b_ka"), sem("b_rg")

        def b_stats_dve(dve, b, par):
            stats(dve, nb, b, par, lambda i: tile(xres, b, i), Bp.bn, Bp.mv)

        def b_shift_act(act, b, par):
            act.wait_ge(Bp.tr, b + 1)
            after(act, b_xk, b - 1)
            act.activation(xs[:, par, 1:TB + 1], banks[0][:, :], ACT.Copy).then_inc(Bp.xt, 1)
            if par:
                act.wait_ge(Bp.xt, b)
                act.activation(xs[:, 1, 0:1], xs[:, 0, TB:TB + 1], ACT.Copy).then_inc(b_x0, 2)

        def b_mix_dve(dve, b, par):
            dve.wait_ge(Bp.xt, b + 1)
            if par:
                dve.wait_ge(b_x0, b + 1)
            after(dve, b_xk, b)
            dve.tensor_tensor(dx[:, :], xs[:, par, 1:TB + 1], xs[:, par, 0:TB], ALU.subtract).then_inc(b_dx, 1)
            dve.wait_ge(b_dx, b + 1)
            after(dve, b_r, b)
            after(dve, b_k, b)
            dve.scalar_tensor_tensor(out=xr[:, :], in0=dx[:, :], scalar=mu_sb[:, 0:1],
                                     in1=xs[:, par, 0:TB], op0=ALU.mult, op1=ALU.add).then_inc(b_xr, 1)
            dve.scalar_tensor_tensor(out=xk[:, :], in0=dx[:, :], scalar=mu_sb[:, 1:2],
                                     in1=xs[:, par, 0:TB], op0=ALU.mult, op1=ALU.add).then_inc(b_xk, 1)

        def b_in_pe(pe, b):
            pe.wait_ge(b_xr, b + 1)
            after(pe, Bp.y, b)
            for i in range(TPB):
                ins = pe.matmul(banks[7][:, i * P:(i + 1) * P], xr[:, i * P:(i + 1) * P], wr_sb[:, :],
                                start=True, stop=True)
            ins.then_inc(b_r, 1)
            pe.wait_ge(b_xk, b + 1)
            after(pe, c_yc, b - LB + LC)
            pe.matmul(banks[5][:, :], wk_sb[:, :], xk[:, :], start=True, stop=True).then_inc(b_k, 1)

        def b_value_pe(pe, b):
            pe.wait_ge(b_ka, b + 1)
            pe.wait_ge(b_rg, b + 1)
            for i in range(TPB):
                ins = pe.matmul(banks[7][:, i * P:(i + 1) * P], kact[:, i * P:(i + 1) * P], wv_sb[:, :],
                                start=True, stop=True)
            ins.then_inc(b_v, 1)

        def b_mid_act(act, b):
            act.wait_ge(b_r, b + 1)
            after(act, Bp.y, b)
            act.activation(rgate[:, :], banks[7][:, :], ACT.Tanh, scale=0.5).then_inc(b_rg, 1)
            act.wait_ge(b_k, b + 1)
            after(act, b_ka, b)
            act.activation(krelu[:, :], banks[5][:, :], ACT.Relu).then_inc(b_kr, 1)
            act.wait_ge(b_kr, b + 1)
            after(act, b_v, b)
            act.activation(kact[:, :], krelu[:, :], ACT.Square).then_inc(b_ka, 1)

        def b_gate_dve(dve, b, par):
            dve.wait_ge(b_rg, b + 1)
            dve.wait_ge(b_v, b + 1)
            after(dve, Bp.tmp, b)
            dve.scalar_tensor_tensor(out=yb[:, :], in0=rgate[:, :], scalar=1.0, in1=banks[7][:, :],
                                     op0=ALU.add, op1=ALU.mult).then_inc(Bp.y, 1)
            dve.wait_ge(Bp.y, b + 1)
            stats(dve, nyb, b, par, lambda i: yb[:, i * P:(i + 1) * P], Bp.ybn, Bp.ymv)

        xnc = sb("xnc", [P, TPB, D])
        ut = sb("ut", [P, TB])
        lam, bu, hs = sb("lam", [NS, TB]), sb("bu", [NS, TB]), sb("hs", [NS, 2, TB])
        yc = sb("yc", [P, TB])
        tmpc = sb("tmpc", [P, TB])
        c_lb, c_lam, c_bu, c_h = sem("c_lb"), sem("c_lam"), sem("c_bu"), sem("c_h")
        c_th = sem("c_th")
        c_yc = sem("c_yc")

        def c_stats_dve(dve, b, par):
            dve.wait_ge(Bp.xa, b + 1)
            dve.nop().then_inc(d_seen, 1)
            stats(dve, ncx, b, par, lambda i: tile(xres, b, i), C.bn, C.mv)

        def c_front_act(act, b):
            act.wait_ge(C.tr, b + 1)
            after(act, C.y, b)
            act.activation(ut[:, :], banks[0][:, :], ACT.Copy).then_inc(C.xt, 1)

        def c_in_pe(pe, b):
            pe.wait_ge(C.xt, b + 1)
            after(pe, b_kr, b - LC + LB + 1) if not isinstance(b, int) or b - LC + LB < NB else None
            pe.matmul(banks[5][0:2 * NS, :], wlb_sb[:, :], ut[:, :], start=True, stop=True).then_inc(c_lb, 1)

        def c_gates_act(act, b):
            act.wait_ge(c_lb, b + 1)
            after(act, c_lam, b)
            after(act, c_h, b)
            act.activation(bu[:, :], banks[5][NS:2 * NS, :], ACT.Copy).then_inc(c_bu, 1)
            act.activation(lam[:, :], banks[5][0:NS, :], ACT.Tanh, bias=blh_sb[:, 0:1], scale=0.5).then_inc(c_th, 1)

        def c_scan_dve(dve, b, par):
            dve.wait_ge(c_th, b + 1)
            dve.tensor_scalar(lam[:, :], lam[:, :], 0.5, 0.5, ALU.mult, ALU.add).then_inc(c_lam, 1)
            dve.wait_ge(c_lam, b + 1)
            dve.wait_ge(c_bu, b + 1)
            after(dve, C.y, b - 1)
            if par:
                dve.wait_ge(c_h, b)
            dve.tensor_tensor_scan(hs[:, par, :], lam[:, :], bu[:, :],
                                   hs[:, 0, TB - 1:TB] if par else 0.0, ALU.mult, ALU.add).then_inc(c_h, 1)

        def c_out_pe(pe, b, par):
            pe.wait_ge(c_h, b + 1)
            for i in range(TPB):
                y = banks[5][:, i * P:(i + 1) * P]
                pe.matmul(y, ut[:, i * P:(i + 1) * P], dpd_sb[:, :], start=True, stop=False)
                ins = pe.matmul(y, hs[:, par, i * P:(i + 1) * P], wc_sb[:, :], start=False, stop=True)
            ins.then_inc(C.y, 1)

        def c_y_act(act, b):
            act.wait_ge(C.y, b + 1)
            after(act, C.tmp, b)
            act.activation(yc[:, :], banks[5][:, :], ACT.Copy).then_inc(c_yc, 1)

        def c_ystats_dve(dve, b, par):
            dve.wait_ge(c_yc, b + 1)
            stats(dve, nyc, b, par, lambda i: yc[:, i * P:(i + 1) * P], C.ybn, C.ymv)

        xnr = sb("xnr", [P, TPB, D])
        xh, xl = sb("xh", [P, 2, TB], F32R), sb("xl", [P, 2, TB], F32R)
        ew = sb("ew", [P, TPB, E])
        mk = sb("mk", [P, TPB, E])
        top8 = sb("top8", [P, TPB, 8])
        low = sb("low", [P, 8, TPB])
        cexp = sb("cexp", [P, TPB, E, EQ])
        cw = sb("cw", [P, 2, TB])
        r_xh, r_xl, r_lg = sem("r_xh"), sem("r_xl"), sem("r_lg")
        r_sub, r_exp = sem("r_sub"), sem("r_exp")
        r_step = sem("r_step")
        x_cexp, x_ct, x_cw = sem("x_cexp"), sem("x_ct"), sem("x_cw")

        def r_stats_dve(dve, b, par):
            dve.wait_ge(C.xa, b + 1)
            dve.nop().then_inc(d_seen, 1)
            stats(dve, nr, b, par, lambda i: tile(xres, b, i), R.bn, R.mv)

        def r_hi_act(act, b, par):
            act.wait_ge(R.tr, b + 1)
            after(act, x_u, NJ * (b - 1))
            act.activation(xh[:, par, :], banks[0][:, :], ACT.Copy).then_inc(r_xh, 1)

        def r_lo_dve(dve, b, par):
            dve.wait_ge(r_xh, b + 1)
            after(dve, x_u, NJ * (b - 1))
            dve.tensor_tensor(xl[:, par, :], banks[0][:, :], xh[:, par, :].bitcast(F32),
                              ALU.subtract).then_inc(r_xl, 1)

        def r_logits_pe(pe, b, par):
            pe.wait_ge(r_xl, b + 1)
            for i in range(TPB):
                c = slice(i * P, (i + 1) * P)
                y = banks[0][:, i * E:(i + 1) * E]
                pe.matmul(y, xl[:, par, c], gate_hi[:, :], start=True, stop=False)
                pe.matmul(y, xh[:, par, c], gate_lo[:, :], start=False, stop=False)
                ins = pe.matmul(y, xh[:, par, c], gate_hi[:, :], start=False, stop=True)
            ins.then_inc(r_lg, 1)

        def wide(v):
            return v.unsqueeze(2).broadcast_to([P, TPB, E])

        def r_scores_dve(dve, b):
            dve.wait_ge(r_lg, b + 1)
            lg = banks[0][:, 0:TPB * E].rearrange("p (t e) -> p t e", t=TPB)
            dve.tensor_reduce(low[:, 0, :], lg, mybir.AxisListType.X, ALU.max).then_inc(r_sub, 1)
            dve.wait_ge(r_sub, 2 * b + 1)
            dve.tensor_tensor(ew[:, :, :], lg, wide(low[:, 0, :]), ALU.subtract).then_inc(r_sub, 1)

        def r_exp_act(act, b):
            act.wait_ge(r_sub, 2 * b + 2)
            act.activation(ew[:, :, :], ew[:, :, :], ACT.Exp).then_inc(r_exp, 1)

        def r_top_dve(dve, b):
            dve.wait_ge(r_exp, b + 1)
            dve.tensor_reduce(low[:, 1, :], ew[:, :, :], mybir.AxisListType.X, ALU.add).then_inc(r_step, 1)
            for t in range(TPB):
                ins = dve.max(top8[:, t, :], ew[:, t, :])
            ins.then_inc(r_step, 1)
            dve.wait_ge(r_step, 10 * b + 2)
            dve.tensor_tensor(low[:, 3, :], top8[:, :, 0], top8[:, :, 1], ALU.add).then_inc(r_step, 1)
            dve.reciprocal(low[:, 2, :], low[:, 1, :]).then_inc(r_step, 1)
            dve.wait_ge(r_step, 10 * b + 3)
            dve.tensor_scalar(top8[:, :, 2:8], top8[:, :, 2:8], 0.0, -1.0, ALU.mult, ALU.add).then_inc(r_step, 1)
            dve.wait_ge(r_step, 10 * b + 5)
            dve.tensor_tensor(low[:, 4, :], low[:, 3, :], low[:, 2, :], ALU.mult)
            for t in range(TPB):
                ins = dve.match_replace(mk[:, t, :], top8[:, t, :], ew[:, t, :], -2.0)
            ins.then_inc(r_step, 1)
            dve.wait_ge(r_step, 10 * b + 6)
            dve.tensor_scalar(low[:, 5, :], low[:, 4, :], TOP_EPS, None, ALU.add).then_inc(r_step, 1)
            dve.scalar_tensor_tensor(out=mk[:, :, :], in0=mk[:, :, :], scalar=-2.0, in1=ew[:, :, :],
                                     op0=ALU.is_equal, op1=ALU.mult).then_inc(r_step, 1)
            dve.wait_ge(r_step, 10 * b + 7)
            dve.reciprocal(low[:, 6, :], low[:, 5, :]).then_inc(r_step, 1)
            dve.wait_ge(r_step, 10 * b + 9)
            dve.scalar_tensor_tensor(out=low[:, 7, :], in0=low[:, 6, :], scalar=ROUTE_SCALE, in1=low[:, 2, :],
                                     op0=ALU.mult, op1=ALU.mult).then_inc(r_step, 1)
            dve.wait_ge(r_step, 10 * b + 10)
            after(dve, x_ct, b)
            for t in range(TPB):
                ins = dve.tensor_scalar(cexp[:, t, :, :], mk[:, t, :].unsqueeze(2).broadcast_to([P, E, EQ]),
                                        low[:, 7, t:t + 1], None, ALU.mult)
            ins.then_inc(x_cexp, 1)

        def r_weights_pe(pe, b):
            pe.wait_ge(x_cexp, b + 1)
            for i in range(TPB):
                ins = pe.transpose(banks[0][:, i * P:(i + 1) * P],
                                   cexp[:, i, :, :].rearrange("p e q -> p (e q)"), ident)
            ins.then_inc(x_ct, 1)

        def r_weights_act(act, b, par):
            act.wait_ge(x_ct, b + 1)
            after(act, x_gc, JE * (b - 1))
            act.activation(cw[:, par, :], banks[0][:, :], ACT.Copy).then_inc(x_cw, 1)

        sil = sb("sil", [P, 2, TB])
        gu = sb("gu", [P, 2, TB])
        gc = sb("gc", [P, 3, TB])
        gs = sb("gs", [P, NJ - JE, TB])
        yx = sb("yx", [P, TB])
        tmpx = sb("tmpx", [P, TB])
        x_g, x_u, x_sil, x_gu = sem("x_g"), sem("x_u"), sem("x_sil"), sem("x_gu")
        x_gc = sem("x_gc")
        x_d = sem("x_d")
        x_y = sem("x_yc")

        def x_hidden_pe(pe, b, par, j):
            m, c = rows(j), slice(j * P, j * P + rows(j))
            n = NJ * b + j
            if j == 0:
                pe.wait_ge(r_xl, b + 1)
            for hi, lo, bank, used, done in ((wg_hi, wg_lo, banks[1 + j % 2], x_sil, x_g),
                                             (wu_hi, wu_lo, banks[3 + j % 2], x_gu, x_u)):
                after(pe, used, n - 1)
                pe.matmul(bank[0:m, :], lo[:, c], xh[:, par, :], start=True, stop=False)
                pe.matmul(bank[0:m, :], hi[:, c], xl[:, par, :], start=False, stop=False)
                pe.matmul(bank[0:m, :], hi[:, c], xh[:, par, :], start=False, stop=True).then_inc(done, 1)

        def x_down_pe(pe, b, j):
            if j < JE:
                pe.wait_ge(x_gc, JE * b + j + 1)
            else:
                pe.wait_ge(x_gu, NJ * b + j + 1)
            if j == 0:
                after(pe, x_y, b)
            m = rows(j)
            src = gc[0:m, j % 3, :] if j < JE else gs[0:m, j - JE, :]
            for i in range(TPB):
                ins = pe.matmul(banks[6][:, i * P:(i + 1) * P], src[:, i * P:(i + 1) * P], wd_sb[0:m, j, :],
                                start=(j == 0 and i == 0), stop=True, skip_group_check=True)
            ins.then_inc(x_d, 1)

        def x_chunk_act(act, b, j):
            m = rows(j)
            act.wait_ge(x_g, NJ * b + j + 1)
            after(act, x_gu, NJ * b + j - 1)
            act.activation(sil[0:m, j % 2, :], banks[1 + j % 2][0:m, :], ACT.Silu).then_inc(x_sil, 1)

        def x_chunk_dve(dve, b, j):
            m = rows(j)
            dve.wait_ge(x_u, NJ * b + j + 1)
            dve.wait_ge(x_sil, NJ * b + j + 1)
            if j < JE:
                after(dve, x_gc, JE * b + j - 1 if j >= 2 else JE * b)
                dst = gu[0:m, j % 2, :]
            else:
                after(dve, x_d, NJ * (b - 1) + j + 1)
                dst = gs[0:m, j - JE, :]
            dve.tensor_tensor(dst, banks[3 + j % 2][0:m, :], sil[0:m, j % 2, :], ALU.mult).then_inc(x_gu, 1)

        def x_chunk_pool(pool, b, par, j):
            if j == 0:
                pool.wait_ge(x_cw, b + 1)
            pool.wait_ge(x_gu, NJ * b + j + 1)
            after(pool, x_d, NJ * b + j - 2 if j >= 3 else NJ * (b - 1) + JE)
            pool.tensor_tensor(gc[:, j % 3, :], gu[:, j % 2, :], cw[:, par, :], ALU.mult).then_inc(x_gc, 1)

        def x_y_act(act, b):
            act.wait_ge(x_d, NJ * (b + 1))
            after(act, X.tmp, b)
            act.activation(yx[:, :], banks[6][:, :], ACT.Copy).then_inc(x_y, 1)

        def x_ystats_dve(dve, b, par):
            dve.wait_ge(x_y, b + 1)
            stats(dve, nx, b, par, lambda i: yx[:, i * P:(i + 1) * P], X.ybn, X.ymv)

        def together(eng, chunk, pieces):
            def iteration(b, par):
                loop = not isinstance(b, int)
                for j in range(NJ + 1):
                    if loop or 0 <= b < NB:
                        chunk(b, par, j)
                    for slot, lag, step in pieces:
                        if slot == j and (loop or 0 <= b + lag < NB):
                            step(b + lag, (par + lag) % 2)

            for b in range(-LB, 2):
                iteration(b, b % 2)
            with eng.Fori(1, (NB - LB - 1) // 2) as s:
                iteration(s * 2, 0)
                iteration(s * 2 + 1, 1)
            for b in range((NB - LB - 1) // 2 * 2, NB + 1):
                iteration(b, b % 2)

        block = ctx.enter_context(nc.Block())

        @block.sync
        def _(sp):
            for dst, src in ((cst, consts), (wqkv_sb, wqkv)):
                sp.dma_start(dst[:, :], src).then_inc(s_cst, 16)
            for b in range(2):
                sp.dma_start(xres[:, b * TB:(b + 1) * TB].rearrange("p (t d) -> p t d", t=TPB),
                             x[b].rearrange("(t p) d -> p t d", p=P)).then_inc(s_x[0], 16)
            sp.dma_start(s1_sb[:, :], s1c).then_inc(s_wA, 16)
            sp.dma_start(s23_sb[:, :, :], s23).then_inc(s_wA, 16)
            sp.dma_start(scl_sb[:, :, :], scl).then_inc(s_wA, 16)
            sp.dma_start(wout_sb[:, :], wout).then_inc(s_wA, 16)
            sp.dma_start(xres[:, 2 * TB:NB * TB].rearrange("p (c t d) -> p (c t) d", c=NB - 2, t=TPB),
                         x[2:NB].rearrange("c (t p) d -> p (c t) d", p=P)).then_inc(s_x[1], 16)
            for dst, src in ((wr_sb, wr), (wk_sb, wk), (wv_sb, wv), (mu_sb, mu)):
                sp.dma_start(dst[:, :], src).then_inc(s_wB, 16)
            for dst, src in ((wlb_sb, wlb), (bl_sb, bl), (wc_sb, wc), (dp_sb, dp), (gate_sb, gate)):
                sp.dma_start(dst[:, :], src).then_inc(s_wC, 16)
            sp.dma_start(wstage[:, :], wg).then_inc(s_w1, 16)
            sp.dma_start(wd_sb[:, 0:NJ - 1, :], wd[0:(NJ - 1) * P, :].rearrange("(j p) d -> p j d", p=P)).then_inc(s_w3, 16)
            sp.dma_start(wd_sb[0:LAST, NJ - 1, :], wd[(NJ - 1) * P:HF, :]).then_inc(s_w3, 16)
            sp.wait_ge(s_wsplit, 2)
            sp.dma_start(wstage[:, :], wu).then_inc(s_w2, 16)
            with sp.Fori(0, NB) as b:
                sp.wait_ge(X.xa, b + 1)
                sp.dma_start(out[bass.ds(b, 1), :, :].rearrange("c (t p) d -> p (c t) d", p=P),
                             blk(xres, b).rearrange("p (t d) -> p t d", t=TPB)).then_inc(s_out, 16)
            sp.wait_ge(s_out, 16 * NB)

        @block.gpsimd
        def _(pool):
            pool.memset(mhalf[:, :], -0.5).then_inc(s_prep, 1)
            pool.memset(vals[:, :, :, :, DH:VW], 1.0).then_inc(a_ones, 1)
            pool.wait_ge(s_prep, 1)

            for b in range(2):
                root(pool, A.mv, A.rs, mv, rs, nm, b, b % 2)

            def pair_a(b0, first, last):
                for c in range(2):
                    if not last:
                        root(pool, A.mv, A.rs, mv, rs, nm, b0 + c + 2, c)
                    if c or not first:
                        root(pool, A.ymv, A.yrs, ymv, yrs, ynm, b0 + c - 1, 1 - c)
                        residual(pool, A, b0 + c - 1, 1 - c)
            sweep(pool, pair_a)
            root(pool, A.ymv, A.yrs, ymv, yrs, ynm, NB - 1, 1)
            residual(pool, A, NB - 1, 1)
            sublayer_done(pool, A)
            pool.memset(xs[:, 0, 0:1], 0.0).then_inc(b_zero, 1)

            def chunk(b, par, j):
                if j < JE:
                    x_chunk_pool(pool, b, par, j)

            together(pool, chunk, [
                (0, LB, lambda b, p: root(pool, Bp.mv, Bp.rs, nb.m, nb.r, nb.n, b, p)),
                (2, LC, lambda b, p: root(pool, C.mv, C.rs, ncx.m, ncx.r, ncx.n, b, p)),
                (2, -1, lambda b, p: root(pool, X.ymv, X.yrs, nx.m, nx.r, nx.n, b, p)),
                (4, LR, lambda b, p: root(pool, R.mv, R.rs, nr.m, nr.r, nr.n, b, p)),
                (5, -1, lambda b, p: add_residual(pool, X, b, tmpx)),
                (10, LB, lambda b, p: root(pool, Bp.ymv, Bp.yrs, nyb.m, nyb.r, nyb.n, b, p, 4 * LN_EPS)),
                (12, LB, lambda b, p: add_residual(pool, Bp, b, tmpb)),
                (14, LC, lambda b, p: root(pool, C.ymv, C.yrs, nyc.m, nyc.r, nyc.n, b, p)),
                (14, LC, lambda b, p: add_residual(pool, C, b, tmpc)),
            ])

        @block.scalar
        def _(act):
            a_front_act(act, 0, 0, False)
            a_squares_k_act(act, 0)

            def pair_a(b0, first, last):
                b1, b2 = b0 + 1, b0 + 2
                a_front_act(act, b1, 1, not first)
                if not first:
                    a_back_act(act, b0 - 1, True)
                a_keys_act(act, b0, 0, not first)
                a_squares_k_act(act, b1)
                a_keys_act(act, b1, 1, not first)
                if not first:
                    y_apply(act, A, b0 - 1, 1, banks[7], True)
                a_query_act(act, b0, 0, not first)
                if not last:
                    a_front_act(act, b2, 0, True)
                    a_squares_k_act(act, b2)
                a_back_act(act, b0, not first)
                a_query_act(act, b1, 1, not first)
                y_apply(act, A, b0, 0, banks[7], not first)
            act.wait_ge(a_ones, 1)
            sweep(act, pair_a)
            a_back_act(act, NB - 1, True)
            y_apply(act, A, NB - 1, 1, banks[7], True)
            sublayer_done(act, A)

            act.wait_ge(s_dpd, 2)

            def chunk(b, par, j):
                if j == 0:
                    r_weights_act(act, b, par)
                if j < NJ:
                    x_chunk_act(act, b, j)

            together(act, chunk, [
                (0, -1, lambda b, p: x_y_act(act, b)),
                (4, LB, lambda b, p: b_shift_act(act, b, p)),
                (4, -1, lambda b, p: apply(act, X, nx, b, p, yx, tmpx)),
                (5, LC, lambda b, p: c_front_act(act, b)),
                (6, LB, lambda b, p: b_mid_act(act, b)),
                (7, LR, lambda b, p: r_hi_act(act, b, p)),
                (9, LC, lambda b, p: c_gates_act(act, b)),
                (11, LR, lambda b, p: r_exp_act(act, b)),
                (11, LB, lambda b, p: apply(act, Bp, nyb, b, p, yb, tmpb)),
                (12, LC, lambda b, p: c_y_act(act, b)),
                (14, LC, lambda b, p: apply(act, C, nyc, b, p, yc, tmpc)),
            ])

        @block.tensor
        def _(pe):
            pe.wait_ge(s_cst, 32)
            for n in range(2):
                pe.wait_ge(s_sorf_v, n + 1)
                if n == 0:
                    pe.matmul(banks[1][0:PP, 0:P], had, sorf_a[:, :, :], start=True, stop=True).then_inc(s_sorf_p, 1)
                else:
                    for h in range(2):
                        ins = pe.matmul(banks[2][0:PP, h * M:(h + 1) * M],
                                        sorf_b[:, h * HH:(h + 1) * HH, :].rearrange("p h d -> p (h d)"),
                                        had[:, 0:M], start=True, stop=True)
                    ins.then_inc(s_sorf_p, 1)
            pe.wait_ge(s_sorf_v, 6)
            a_front_pe(pe, 0, 0, True)

            def pair_a(b0, first, last):
                b1, b2 = b0 + 1, b0 + 2
                if first:
                    pe.wait_ge(a_v, 1)
                    transposes_a1(pe)
                else:
                    a_front_pe(pe, b1, 1, False)
                    a_back_pe(pe, b0 - 1, 1)
                a_keys_pe(pe, b0, 0, None, True, not first)
                if not first:
                    a_proj_pe(pe, b0 - 1, 1, True)
                a_keys_pe(pe, b1, 1, None, False, not first)
                seq = (b0 // 2) if first or last else pair_a.seq
                a_query_pe(pe, b0, 0, seq, not first)
                if not last:
                    a_front_pe(pe, b2, 0, False)
                a_back_pe(pe, b0, 0, last)
                a_query_pe(pe, b1, 1, seq, not first)
                a_proj_pe(pe, b0, 0, not first)

            def transposes_a1(pe):
                transposes(pe, A, 1, 1)
                pe.wait_ge(A.xt, 2)
                a_front_rest(pe, 1, 1)

            def a_front_rest(pe, b, par):
                for n in range(2):
                    pe.wait_ge(a_rot, 4 * b + 2 * n)
                    pe.matmul(banks[1][:, :], wqkv_sb[:, 2 * n * D:(2 * n + 1) * D], xt[:, par, :],
                              start=True, stop=True).then_inc(a_q, 1)
                    pe.matmul(banks[2][:, :], wqkv_sb[:, (2 * n + 1) * D:(2 * n + 2) * D], xt[:, par, :],
                              start=True, stop=True).then_inc(a_qs, 1)
                    if n == 0:
                        for i in range(TPB):
                            ins = pe.matmul(banks[0][:, i * P:(i + 1) * P], xt[:, par, i * P:(i + 1) * P],
                                            wqkv_sb[:, 4 * D:5 * D], start=True, stop=True)
                        ins.then_inc(a_vp, 1)

            pe.wait_ge(s_wA, 4 * 16)
            pair_a(0, True, False)
            with pe.Fori(1, B - 1) as s:
                pair_a.seq = s
                pair_a(s * 2, False, False)
            pair_a(NB - 2, False, True)
            a_back_pe(pe, NB - 1, 1, True)
            a_proj_pe(pe, NB - 1, 1, True)
            sublayer_done(pe, A)

            pe.wait_ge(s_wB, 4 * 16)
            pe.wait_ge(s_wC, 5 * 16)
            pe.wait_ge(s_w3, 2 * 16)
            pe.wait_ge(s_dpd, 2)
            pe.wait_ge(s_wsplit, 6)
            LAG = 2

            def chunk(b, par, j):
                if j < NJ:
                    x_hidden_pe(pe, b, par, j)
                if j >= LAG:
                    x_down_pe(pe, b, j - LAG)
                if j == NJ:
                    for i in range(NJ + 1 - LAG, NJ):
                        x_down_pe(pe, b, i)

            def turn_b(b, p):
                if not isinstance(b, int) or b > LB - LR:
                    pe.wait_ge(x_cw, b - LB + LR)
                transpose(pe, Bp, b, xnb)

            def turn_c(b, p):
                after(pe, Bp.xt, b + LB - LC + 1) if not isinstance(b, int) or b + LB - LC < NB else pe.wait_ge(Bp.xt, NB)
                transpose(pe, C, b, xnc)

            def turn_r(b, p):
                after(pe, C.xt, b + LC - LR + 1) if not isinstance(b, int) or b + LC - LR < NB else pe.wait_ge(C.xt, NB)
                after(pe, x_cw, b)
                transpose(pe, R, b, xnr)

            together(pe, chunk, [
                (3, LB, turn_b),
                (4, LC, turn_c),
                (6, LR, turn_r),
                (6, LB, lambda b, p: b_in_pe(pe, b)),
                (8, LC, lambda b, p: c_in_pe(pe, b)),
                (8, LB, lambda b, p: b_value_pe(pe, b)),
                (9, LR, lambda b, p: r_logits_pe(pe, b, p)),
                (11, LC, lambda b, p: c_out_pe(pe, b, p)),
                (14, LR, lambda b, p: r_weights_pe(pe, b)),
            ])

        @block.vector
        def _(dve):
            dve.wait_ge(s_wA, 4 * 16)
            dve.wait_ge(s_cst, 32)
            dve.tensor_tensor(sorf_a[:, :, :], had[:, 0:DH].unsqueeze(1).broadcast_to([PP, H, DH]),
                              s23_sb[:, 0, :].unsqueeze(2).broadcast_to([PP, H, DH]), ALU.mult).then_inc(s_sorf_v, 1)
            dve.wait_ge(s_sorf_p, 1)
            dve.tensor_tensor(sorf_b[:, :, :], banks[1][0:PP, 0:P].rearrange("p (h d) -> p h d", h=H),
                              s23_sb[:, 1, :].unsqueeze(2).broadcast_to([PP, H, DH]), ALU.mult).then_inc(s_sorf_v, 1)
            dve.wait_ge(s_sorf_p, 2)
            for h in range(2):
                ins = dve.tensor_scalar(sorf_c[:, h, :], banks[2][0:PP, h * M:(h + 1) * M], s1_sb[:, h:h + 1],
                                        1.0 / PP ** 2, ALU.mult, ALU.mult)
            ins.then_inc(s_sorf_v, 1)
            dve.wait_ge(s_sorf_v, 3)
            dve.tensor_tensor(sorf_d[:, :, :], sorf_c[:, :, :], scl_sb[:, :, :], ALU.mult).then_inc(s_sorf_v, 1)
            dve.wait_ge(s_sorf_v, 4)
            m8 = cst[:, C_M8:C_M8 + HH]
            for h in range(2):
                ins = dve.tensor_tensor(feat[0:PP, h, :, :], sorf_d[:, h, :].unsqueeze(1).broadcast_to([PP, HH, M]),
                                        m8[0:PP].unsqueeze(2).broadcast_to([PP, HH, M]), ALU.mult)
            ins.then_inc(s_sorf_v, 1)
            for h in range(2):
                ins = dve.tensor_copy(feat[PP:P, h, :, :], m8[PP:P].unsqueeze(2).broadcast_to([PP, HH, M]))
            ins.then_inc(s_sorf_v, 1)

            dve.wait_ge(s_x[0], 32)
            for b in range(2):
                ln_stats(dve, A, b, b)
                ln_norm(dve, A, b, b, False)
            a_cat_dve(dve, 0, 0, 0, False)
            dve.wait_ge(s_x[1], 16)

            def pair_a(b0, first, last):
                b1, b2 = b0 + 1, b0 + 2
                a_cat_dve(dve, b1, 1, TB, not first)
                if not last:
                    ln_stats(dve, A, b2, 0)
                if not first:
                    a_tail(b0 - 1, 1)
                if not last:
                    ln_norm(dve, A, b2, 0, True)
                a_state_dve(dve, (b0 // 2) if first or last else pair_a.seq)
                a_divide_dve(dve, b0, 0, not first)
                if not last:
                    ln_stats(dve, A, b2 + 1, 1)
                    a_cat_dve(dve, b2, 0, 0, True)
                a_tail(b0, 0)
                if not last:
                    ln_norm(dve, A, b2 + 1, 1, True)
                a_divide_dve(dve, b1, 1, not first)

            def a_tail(b, par):
                y_stats(dve, A, b, par, banks[7])

            pair_a(0, True, False)
            with dve.Fori(1, B - 1) as s:
                pair_a.seq = s
                pair_a(s * 2, False, False)
            pair_a(NB - 2, False, True)
            a_tail(NB - 1, 1)

            def split_w(hi, lo, src, k):
                dve.tensor_copy(hi[:, :], src[:, :]).then_inc(s_wsplit, 1)
                dve.wait_ge(s_wsplit, k + 1)
                dve.tensor_tensor(lo[:, :], src[:, :], hi[:, :].bitcast(F32), ALU.subtract).then_inc(s_wsplit, 1)
            dve.wait_ge(s_w1, 16)
            split_w(wg_hi, wg_lo, wstage, 0)
            dve.wait_ge(s_wC, 5 * 16)
            split_w(gate_hi, gate_lo, gate_sb, 2)
            dve.tensor_scalar(dpd_sb[:, :], ident, dp_sb[:, 0:1], None, ALU.mult).then_inc(s_dpd, 1)
            dve.tensor_scalar(blh_sb[:, :], bl_sb[:, :], 0.5, None, ALU.mult).then_inc(s_dpd, 1)
            dve.wait_ge(s_w2, 16)
            split_w(wu_hi, wu_lo, wstage, 4)
            sublayer_done(dve, A)
            dve.wait_ge(s_wB, 4 * 16)
            dve.wait_ge(b_zero, 1)

            def chunk(b, par, j):
                if j < NJ:
                    x_chunk_dve(dve, b, j)

            together(dve, chunk, [
                (0, LB, lambda b, p: b_stats_dve(dve, b, p)),
                (1, -1, lambda b, p: x_ystats_dve(dve, b, p)),
                (1, LC, lambda b, p: c_stats_dve(dve, b, p)),
                (2, LB, lambda b, p: normalise(dve, Bp, nb, b, p, xnb)),
                (3, LC, lambda b, p: normalise(dve, C, ncx, b, p, xnc)),
                (3, LR, lambda b, p: r_stats_dve(dve, b, p)),
                (5, LB, lambda b, p: b_mix_dve(dve, b, p)),
                (5, LR, lambda b, p: normalise(dve, R, nr, b, p, xnr)),
                (8, LR, lambda b, p: r_lo_dve(dve, b, p)),
                (9, LB, lambda b, p: b_gate_dve(dve, b, p)),
                (10, LC, lambda b, p: c_scan_dve(dve, b, p)),
                (10, LR, lambda b, p: r_scores_dve(dve, b)),
                (12, LR, lambda b, p: r_top_dve(dve, b)),
                (13, LC, lambda b, p: c_ystats_dve(dve, b, p)),
            ])


def constants():
    c = np.zeros((P, C_N), np.float32)
    freqs = np.float32(10000.0) ** (-np.arange(0, DH, 2, dtype=np.float32) / np.float32(DH))
    ang = np.arange(L - 1, dtype=np.float32)[:, None] * freqs.astype(np.float32)
    ang = np.concatenate([np.zeros((1, DH // 2), np.float32), ang]).astype(np.float64)
    ch = np.arange(P)
    pair = (ch % DH) // 2
    c[:, C_COS:C_COS + L] = np.cos(ang)[:, pair].T
    c[:, C_SIN:C_SIN + L] = np.sin(ang)[:, pair].T * np.where(ch % 2 == 0, -1.0, 1.0)[:, None]
    c[:, C_ID:C_ID + P] = np.eye(P)
    had = np.ones((1, 1))
    while had.shape[0] < PP:
        had = np.block([[had, had], [had, -had]])
    c[0:PP, C_HAD:C_HAD + PP] = had
    own = (np.arange(PP)[:, None] // DH) == np.arange(HH)[None, :]
    c[0:PP, C_M8:C_M8 + HH] = own
    c[PP:P, C_M8:C_M8 + HH] = -0.5 * own
    c[:, C_M4:C_M4 + GH] = ((ch[:, None] // M) == np.arange(GH)[None, :]) / float(M)
    return c


def kernel(L0_attn_x, L0_attn_w_qkv, L0_attn_w_out, L0_attn_sorf_signs, L0_attn_sorf_scales, L0_ffn_W_r, L0_ffn_W_k,
           L0_ffn_W_v, L0_ffn_mu_r, L0_ffn_mu_k, L1_attn_Wl, L1_attn_bl, L1_attn_Wb, L1_attn_Wc, L1_attn_Dp,
           L1_ffn_gate_w, L1_ffn_w_gate, L1_ffn_w_up, L1_ffn_w_down, L1_ffn_sw_gate, L1_ffn_sw_up, L1_ffn_sw_down):
    import concourse.bacc as bacc
    from concourse.bass_utils import run_bass_kernel_spmd

    swap = np.arange(D).reshape(-1, 2)[:, ::-1].reshape(-1)
    q, k, v = (np.asarray(L0_attn_w_qkv)[i * D:(i + 1) * D] for i in range(3))
    signs = np.asarray(L0_attn_sorf_signs)[:, 0]
    scales = np.asarray(L0_attn_sorf_scales)[:, 0, 0:M]

    def experts(w, shared):
        w = np.asarray(w).reshape(E, D, JE, EQ).transpose(1, 2, 0, 3).reshape(D, E * F)
        return np.concatenate([w, np.asarray(shared)], axis=1)

    arrays = {
        "x": np.asarray(L0_attn_x).reshape(NB, TB, D),
        "wqkv": np.concatenate([q, q[swap], k, k[swap], v]).T,
        "wout": np.asarray(L0_attn_w_out).T,
        "consts": constants(),
        "s1c": signs[:, 0, 0:DH].reshape(2, PP).T,
        "s23": signs[:, 1:3].transpose(2, 1, 0),
        "scl": np.broadcast_to(scales.reshape(2, HH, 1, M), (2, HH, DH, M)).transpose(1, 2, 0, 3).reshape(PP, 2, M),
        "wr": np.asarray(L0_ffn_W_r).T, "wk": np.asarray(L0_ffn_W_k).T, "wv": np.asarray(L0_ffn_W_v).T,
        "mu": np.stack([np.asarray(L0_ffn_mu_r), np.asarray(L0_ffn_mu_k)], axis=1),
        "wlb": np.concatenate([np.asarray(L1_attn_Wl), np.asarray(L1_attn_Wb)]).T,
        "bl": np.asarray(L1_attn_bl).reshape(NS, 1),
        "wc": np.asarray(L1_attn_Wc).T,
        "dp": np.asarray(L1_attn_Dp).reshape(D, 1),
        "gate": np.asarray(L1_ffn_gate_w).T,
        "wg": experts(L1_ffn_w_gate, L1_ffn_sw_gate),
        "wu": experts(L1_ffn_w_up, L1_ffn_sw_up),
        "wd": np.concatenate([np.asarray(L1_ffn_w_down).reshape(E, JE, EQ, D).transpose(1, 0, 2, 3).reshape(E * F, D),
                              np.asarray(L1_ffn_sw_down)]),
    }
    nc = bacc.Bacc("TRN2", target_bir_lowering=False, num_devices=1)
    arrays = {n: np.ascontiguousarray(a) for n, a in arrays.items()}
    args = [nc.dram_tensor(n, a.shape, F32, kind="ExternalInput").ap() for n, a in arrays.items()]
    args.append(nc.dram_tensor("out", (NB, TB, D), F32, kind="ExternalOutput").ap())
    build(nc, *args)
    r = run_bass_kernel_spmd(nc, [arrays], core_ids=[0])
    return r.results[0]["out"].reshape(B, L, D)
```

```python
from contextlib import ExitStack

import numpy as np

import concourse.bass as bass
from concourse import mybir

F32 = mybir.dt.float32
F32R = mybir.dt.float32r
ALU = mybir.AluOpType
ACT = mybir.ActivationFunctionType

P = 128
B, L, D = 8, 1024, 128
TB = 512
TPB = TB // P
NB = B * L // TB
BPS = L // TB
H, DH = 16, 8
M = 32
PP = 64
HH = H // 2
GH = P // M
NG = H // GH
VW = DH + 1
NS = 32
E, F = 8, 176
SF = 352
EQ = P // E
JE = F // EQ
HF = E * F + SF
NJ = -(-HF // P)
LAST = HF - (NJ - 1) * P
LN_EPS = 1e-5
DEN_EPS = 1e-6
TOP_EPS = 1e-20
ROUTE_SCALE = 2.5

C_COS, C_SIN = 0, L
C_ID = 2 * L
C_HAD = C_ID + P
C_M8 = C_HAD + PP
C_M4 = C_M8 + HH
C_N = C_M4 + GH


def rows(j):
    return P if j < NJ - 1 else LAST


def build(nc, x, wqkv, wout, consts, s1c, s23, scl, wr, wk, wv, mu, wlb, bl, wc, dp, gate, wg, wu, wd, out):
    ctx = ExitStack()
    with ctx:
        def sb(name, shape, dt=F32):
            return ctx.enter_context(nc.sbuf_tensor(name, shape, dt))

        def sem(name):
            return ctx.enter_context(nc.semaphore(name))

        banks = [ctx.enter_context(nc.psum_tensor(f"bank{i}", [P, TB], F32)) for i in range(8)]

        xres = sb("xres", [P, NB * TB])
        cst = sb("cst", [P, C_N])
        ident = cst[:, C_ID:C_ID + P]
        had = cst[0:PP, C_HAD:C_HAD + PP]
        wout_sb = sb("wout_sb", [P, D])
        s1_sb = sb("s1_sb", [PP, 2])
        s23_sb = sb("s23_sb", [PP, 2, H])
        scl_sb = sb("scl_sb", [PP, 2, M])
        wr_sb, wk_sb, wv_sb = sb("wr_sb", [P, D]), sb("wk_sb", [P, D]), sb("wv_sb", [P, D])
        mu_sb = sb("mu_sb", [P, 2])
        wlb_sb = sb("wlb_sb", [P, 2 * NS])
        bl_sb = sb("bl_sb", [NS, 1])
        wc_sb = sb("wc_sb", [NS, D])
        dp_sb = sb("dp_sb", [P, 1])
        dpd_sb = sb("dpd_sb", [P, P])
        gate_sb = sb("gate_sb", [P, E])
        blh_sb = sb("blh_sb", [NS, 1])
        wstage = sb("wstage", [P, HF])
        gate_hi, gate_lo = sb("gate_hi", [P, E], F32R), sb("gate_lo", [P, E], F32R)
        wg_hi, wg_lo = sb("wg_hi", [P, HF], F32R), sb("wg_lo", [P, HF], F32R)
        wu_hi, wu_lo = sb("wu_hi", [P, HF], F32R), sb("wu_lo", [P, HF], F32R)
        wd_sb = sb("wd_sb", [P, NJ, D])
        feat = sb("feat", [P, 2, HH, M])
        sorf_a = sb("sorf_a", [PP, H, DH])
        sorf_b = sb("sorf_b", [PP, H, DH])
        sorf_c = sb("sorf_c", [PP, 2, M])
        sorf_d = sb("sorf_d", [PP, 2, M])
        mhalf = sb("mhalf", [P, 8])

        s_cst, s_wA, s_wB, s_wC, s_w1, s_w2, s_w3 = (sem(n) for n in
            ("s_cst", "s_wA", "s_wB", "s_wC", "s_w1", "s_w2", "s_w3"))
        s_x = [sem(f"s_x{i}") for i in range(2)]
        s_prep = sem("s_prep")
        s_sorf_v, s_sorf_p = sem("s_sorf_v"), sem("s_sorf_p")
        s_dpd = sem("s_dpd")
        s_wsplit = sem("s_wsplit")
        s_out = sem("s_out")

        class Phase:
            def __init__(self, n):
                self.bn = sem(n + "_bn")
                self.mv = sem(n + "_mv")
                self.rs = sem(n + "_rs")
                self.xn = sem(n + "_xn")
                self.tr = sem(n + "_tr")
                self.xt = sem(n + "_xt")
                self.y = sem(n + "_y")
                self.ybn = sem(n + "_ybn")
                self.ymv = sem(n + "_ymv")
                self.yrs = sem(n + "_yrs")
                self.tmp = sem(n + "_tmp")
                self.xa = sem(n + "_xa")

        A, Bp, C, R, X = Phase("a"), Phase("b"), Phase("c"), Phase("r"), Phase("x")

        class Norm:
            def __init__(self, n):
                self.st = sb(n + "_st", [P, 2, TPB, 6])
                self.m = sb(n + "_m", [P, 2, TPB, 5])
                self.r = sb(n + "_r", [P, 2, 3, TPB])
                self.n = sb(n + "_n", [P, 2, TPB])

        def after(eng, s, n):
            if not isinstance(n, int) or n > 0:
                eng.wait_ge(s, n)

        def blocks(n):
            return min(max(n, 0), NB) if isinstance(n, int) else n

        def blk(t, b):
            return t[:, bass.ds(b * TB, TB)]

        def tile(t, b, i):
            return t[:, bass.ds(b * TB + i * P, P)]

        def aggregate(dve, stats, m, par, seen, done, b):
            dve.wait_ge(seen, 4 * b + 1)
            s = stats[:, par, :, :]
            dve.tensor_tensor(m[:, par, :, 2], s[:, :, 1], s[:, :, 4], ALU.subtract).then_inc(seen, 1)
            dve.tensor_tensor(m[:, par, :, 3], s[:, :, 2], s[:, :, 5], ALU.add)
            dve.tensor_tensor(m[:, par, :, 0], s[:, :, 1], s[:, :, 4], ALU.add)
            dve.wait_ge(seen, 4 * b + 2)
            dve.scalar_tensor_tensor(out=m[:, par, :, 4], in0=m[:, par, :, 2], scalar=D / 4.0,
                                     in1=m[:, par, :, 2], op0=ALU.mult, op1=ALU.mult).then_inc(seen, 2)
            dve.wait_ge(seen, 4 * b + 4)
            dve.tensor_tensor(m[:, par, :, 1], m[:, par, :, 3], m[:, par, :, 4], ALU.add).then_inc(done, 1)

        def root(pool, ready, done, m, r, n, b, par, eps=LN_EPS):
            pool.wait_ge(ready, b + 1)
            pool.tensor_tensor(n[:, par, :], m[:, par, :, 0], mhalf[:, 0:TPB], ALU.mult).then_inc(done, 1)
            pool.tensor_scalar(r[:, par, 0, :], m[:, par, :, 1], 1.0 / D, eps, ALU.mult, ALU.add).then_inc(done, 1)
            pool.wait_ge(done, 4 * b + 2)
            pool.tensor_tensor(r[:, par, 1, :], r[:, par, 0, :], mhalf[:, 0:TPB], ALU.pow).then_inc(done, 1)
            pool.wait_ge(done, 4 * b + 3)
            pool.tensor_tensor(r[:, par, 2, :], n[:, par, :], r[:, par, 1, :], ALU.mult).then_inc(done, 1)

        LR, LC, LB, LQ, LK, LF = 1, 2, 3, 4, 5, 6
        na, nya, nb, nyb, ncx, nyc, nr, nx = (Norm(n) for n in ("na", "nya", "nb", "nyb", "nc", "nyc", "nr", "nx"))

        def stats(dve, n, b, par, src, seen, done, ready=None):
            if ready is not None:
                dve.wait_ge(ready, b + 1)
            for i in range(TPB):
                ins = dve.bn_stats(n.st[:, par, i, :], src(i))
            ins.then_inc(seen, 1)
            aggregate(dve, n.st, n.m, par, seen, done, b)

        def normalise(dve, ph, n, b, par, dst):
            dve.wait_ge(ph.rs, 4 * b + 4)
            after(dve, ph.tr, b)
            for i in range(TPB):
                ins = dve.tensor_scalar(dst[:, i, :], tile(xres, b, i), n.r[:, par, 1, i:i + 1],
                                        n.r[:, par, 2, i:i + 1], ALU.mult, ALU.add)
            ins.then_inc(ph.xn, 1)

        def transpose(pe, ph, b, src):
            pe.wait_ge(ph.xn, b + 1)
            for i in range(TPB):
                ins = pe.transpose(banks[0][:, i * P:(i + 1) * P], src[:, i, :], ident)
            ins.then_inc(ph.tr, 1)

        def apply(act, ph, n, b, par, y, dst):
            act.wait_ge(ph.yrs, 4 * b + 4)
            after(act, ph.xa, b)
            for i in range(TPB):
                ins = act.activation(dst[:, i * P:(i + 1) * P], y[:, i * P:(i + 1) * P], ACT.Identity,
                                     scale=n.r[:, par, 1, i:i + 1], bias=n.r[:, par, 2, i:i + 1])
            ins.then_inc(ph.tmp, 1)

        p_seen, d_seen = sem("p_seen"), sem("d_seen")

        def add_residual(pool, ph, b, src):
            pool.wait_ge(ph.tmp, b + 1)
            pool.nop().then_inc(p_seen, 1)
            pool.tensor_tensor(blk(xres, b), blk(xres, b), src[:, :], ALU.add).then_inc(ph.xa, 1)

        wqkv_sb = sb("wqkv_sb", [P, 5 * D])
        xna = sb("xna", [P, TPB, D])
        xta = sb("xta", [P, TB])
        cat_q = sb("cat_q", [P, 2, 2, TB])
        cat_k = sb("cat_k", [P, 2, TB])
        rot = sb("rot", [P, 2, TB])
        vals = sb("vals", [P, TPB, H, VW])
        kphi = sb("kphi", [P, 2, H * M])
        qphi = sb("qphi", [P, 2, TB])
        s_even = sb("s_even", [P, H * VW])
        s_all = sb("s_all", [P, H * VW])
        sbd = sb("sbd", [P, NG, GH, VW])
        den = sb("den", [P, 2, TPB, HH])
        rden = sb("rden", [P, 2, TPB, HH])
        o_sb = sb("o_sb", [P, TPB, H, DH])
        ot_sb = sb("ot_sb", [P, TB])
        ya = sb("ya", [P, TB])
        tmpa = sb("tmpa", [P, TB])
        a_q, a_qs = sem("a_q"), sem("a_qs")
        a_rot = sem("a_rot")
        a_catr = sem("a_catr")
        a_cats = sem("a_cats")
        a_vp, a_v = sem("a_vp"), sem("a_v")
        a_ones = sem("a_ones")
        a_fk, a_ek = sem("a_fk"), sem("a_ek")
        a_s = sem("a_s")
        a_sum = sem("a_sum")
        a_state = sem("a_state")
        a_fq, a_eq = sem("a_fq"), sem("a_eq")
        a_o = sem("a_o")
        a_den = sem("a_den")
        a_on = sem("a_on")
        a_ot, a_ots = sem("a_ot"), sem("a_ots")
        a_yc = sem("a_yc")
        OW = HH * VW

        def a_front_pe(pe, b):
            after(pe, a_ots, blocks(b - LF + LQ + 1))
            if isinstance(b, int):
                after(pe, a_v, b)
            transpose(pe, A, b, xna)

        def a_products_pe(pe, b, n):
            if n == 0:
                pe.wait_ge(A.xt, b + 1)
                after(pe, b_kr, blocks(b - LF + LB + 1))
                after(pe, c_th, blocks(b - LF + LC + 1))
                if isinstance(b, int):
                    after(pe, a_rot, 4 * b)
            else:
                pe.wait_ge(a_rot, 4 * b + 2)
            pe.matmul(banks[5][:, :], wqkv_sb[:, 2 * n * D:(2 * n + 1) * D], xta[:, :],
                      start=True, stop=True).then_inc(a_q, 1)
            pe.matmul(banks[6][:, :], wqkv_sb[:, (2 * n + 1) * D:(2 * n + 2) * D], xta[:, :],
                      start=True, stop=True).then_inc(a_qs, 1)

        def a_values_pe(pe, b):
            after(pe, r_xl, blocks(b - LF + LR + 1))
            for i in range(TPB):
                ins = pe.matmul(banks[0][:, i * P:(i + 1) * P], xta[:, i * P:(i + 1) * P],
                                wqkv_sb[:, 4 * D:5 * D], start=True, stop=True)
            ins.then_inc(a_vp, 1)

        def a_banks_pe(pe, i):
            after(pe, b_kr, blocks(i + LB))
            after(pe, c_yc, blocks(i + LC))
            after(pe, Bp.y, blocks(i + LB))
            if isinstance(i, int):
                after(pe, a_yc, blocks(i + LQ))

        def a_keys_pe(pe, b, steps):
            for i in steps:
                if i == 0:
                    a_banks_pe(pe, b - LK)
                    pe.wait_ge(a_cats, 2 * b + 2)
                if i < TPB:
                    if i >= 2:
                        pe.wait_ge(a_ek, TPB * b + i - 1)
                    for h in range(2):
                        ins = pe.matmul(banks[5 + i % 2][:, h * HH * M:(h + 1) * HH * M],
                                        cat_k[:, h, i * P:(i + 1) * P], feat[:, h, :, :], start=True, stop=True)
                    ins.then_inc(a_fk, 1)
                if i >= 2:
                    a_state_pe(pe, b, i - 2)
            if TPB in steps:
                a_state_pe(pe, b, TPB - 1)

        def a_state_pe(pe, b, i):
            if i == 0:
                pe.wait_ge(a_v, b + 1)
            pe.wait_ge(a_ek, TPB * b + i + 1)
            for g in range(NG):
                ins = pe.matmul(banks[7][:, g * GH * VW:(g + 1) * GH * VW],
                                kphi[:, i % 2, g * P:(g + 1) * P], vals[:, i, g * GH:(g + 1) * GH, :],
                                start=(i == 0 and g == 0), stop=True, skip_group_check=True)
            ins.then_inc(a_s, 1)

        def a_query_pe(pe, b, par, steps):
            def features(g):
                if g < 2:
                    after(pe, a_ek, TPB * blocks(b - LQ + LK + 1))
                else:
                    pe.wait_ge(a_eq, NG * b + g - 1)
                pe.matmul(banks[5 + g % 2][:, :], feat[:, g // 2, (g % 2) * GH:(g % 2 + 1) * GH, :],
                          cat_q[:, par, g // 2, :], start=True, stop=True).then_inc(a_fq, 1)

            def outputs(g):
                pe.wait_ge(a_eq, NG * b + g + 1)
                if g == 0:
                    pe.wait_ge(a_state, blocks(b + 2))
                elif g == 2:
                    after(pe, x_cw, blocks(b - LQ + 1))
                    if isinstance(b, int):
                        after(pe, a_v, blocks(b - LQ + LF))
                        after(pe, Bp.xt, blocks(b - LQ + LB + 1))
                        after(pe, C.xt, blocks(b - LQ + LC + 1))
                bank = banks[7] if g < 2 else banks[0]
                for i in range(TPB):
                    c = i * OW + g % 2 * GH * VW
                    ins = pe.matmul(bank[:, c:c + GH * VW], qphi[:, g % 2, i * P:(i + 1) * P], sbd[:, g, :, :],
                                    start=True, stop=True)
                ins.then_inc(a_o, 1)

            for g in steps:
                if g == 0 and isinstance(b, int) and b - LQ + LK >= NB:
                    a_banks_pe(pe, b - LQ)
                if g < NG:
                    features(g)
                if g >= 1:
                    outputs(g - 1)

        def a_back_pe(pe, b):
            pe.wait_ge(a_on, 2 * b + 2)
            for i in range(TPB):
                ins = pe.transpose(banks[0][:, i * P:(i + 1) * P],
                                   o_sb[:, i, :, :].rearrange("p h d -> p (h d)"), ident)
            ins.then_inc(a_ot, 1)

        def a_out_pe(pe, b):
            pe.wait_ge(a_ots, b + 1)
            for i in range(TPB):
                ins = pe.matmul(banks[7][:, i * P:(i + 1) * P], ot_sb[:, i * P:(i + 1) * P], wout_sb[:, :],
                                start=True, stop=True)
            ins.then_inc(A.y, 1)

        def a_cat_dve(dve, b, par, n):
            pos = par * TB
            dve.wait_ge(a_q, 2 * b + n + 1)
            after(dve, a_catr, 2 * b + n)
            dve.tensor_tensor(rot[:, 0, :], banks[5][:, :], cst[:, C_COS + pos:C_COS + pos + TB],
                              ALU.mult).then_inc(a_rot, 1)
            dve.wait_ge(a_qs, 2 * b + n + 1)
            dve.tensor_tensor(rot[:, 1, :], banks[6][:, :], cst[:, C_SIN + pos:C_SIN + pos + TB],
                              ALU.mult).then_inc(a_rot, 1)
            dve.wait_ge(a_rot, 4 * b + 2 * n + 2)
            if n == 0:
                after(dve, a_fq, NG * (b - 1))
            else:
                after(dve, a_fk, TPB * b)
            for h in range(2):
                dst = cat_k[0:PP, h, :] if n else cat_q[0:PP, par, h, :]
                ins = dve.tensor_tensor(dst, rot[h * PP:(h + 1) * PP, 0, :], rot[h * PP:(h + 1) * PP, 1, :],
                                        ALU.add)
            ins.then_inc(a_catr, 1)

        def a_state_dve(dve, b, par):
            dve.wait_ge(a_s, TPB * (b + 1))
            if par == 0:
                dve.tensor_copy(s_even[:, :], banks[7][:, 0:H * VW]).then_inc(a_state, 1)
                return
            dve.wait_ge(a_state, b)
            dve.tensor_tensor(s_all[:, :], banks[7][:, 0:H * VW], s_even[:, :], ALU.add).then_inc(a_sum, 2)
            dve.wait_ge(a_sum, b + 1)
            after(dve, a_o, NG * (b - 1))
            dve.tensor_tensor(sbd[:, :, :, :], s_all[:, :].rearrange("p (g h v) -> p g h v", g=NG, h=GH),
                              cst[:, C_M4:C_M4 + GH].unsqueeze(1).unsqueeze(3).broadcast_to([P, NG, GH, VW]),
                              ALU.mult).then_inc(a_state, 1)

        def a_divide_dve(dve, b, n):
            v = banks[0 if n else 7][:, 0:TPB * OW].rearrange("p (t h v) -> p t h v", t=TPB, h=HH)
            dve.wait_ge(a_o, NG * b + 2 * n + 2)
            dve.tensor_scalar(den[:, n, :, :], v[:, :, :, DH], DEN_EPS, None, ALU.max).then_inc(a_den, 1)
            dve.wait_ge(a_den, 4 * b + 2 * n + 1)
            dve.reciprocal(rden[:, n, :, :], den[:, n, :, :]).then_inc(a_den, 1)
            dve.wait_ge(a_den, 4 * b + 2 * n + 2)
            after(dve, a_ot, b)
            dve.tensor_tensor(o_sb[:, :, n * HH:(n + 1) * HH, :], v[:, :, :, 0:DH],
                              rden[:, n, :, :].unsqueeze(3).broadcast_to([P, TPB, HH, DH]),
                              ALU.mult).then_inc(a_on, 1)

        def a_xt_act(act, b):
            act.wait_ge(A.tr, b + 1)
            after(act, a_vp, b)
            act.activation(xta[:, :], banks[0][:, :], ACT.Copy).then_inc(A.xt, 1)

        def a_squares_q_act(act, b, par):
            act.wait_ge(a_catr, 2 * b + 1)
            for h in range(2):
                ins = act.activation(cat_q[PP:P, par, h, :], cat_q[0:PP, par, h, :], ACT.Square)
            ins.then_inc(a_cats, 1)

        def a_squares_k_act(act, b):
            act.wait_ge(a_catr, 2 * b + 2)
            for h in range(2):
                ins = act.activation(cat_k[PP:P, h, :], cat_k[0:PP, h, :], ACT.Square)
            ins.then_inc(a_cats, 1)

        def a_values_act(act, b):
            act.wait_ge(a_vp, b + 1)
            after(act, a_s, TPB * b)
            act.activation(vals[:, :, :, 0:DH].rearrange("p t h v -> p (t h) v"),
                           banks[0][:, :].rearrange("p (t h v) -> p (t h) v", t=TPB, h=H),
                           ACT.Copy).then_inc(a_v, 1)

        def a_keys_act(act, b):
            for i in range(TPB):
                act.wait_ge(a_fk, TPB * b + i + 1)
                after(act, a_s, TPB * b + i - 1)
                act.activation(kphi[:, i % 2, :], banks[5 + i % 2][:, :], ACT.Exp).then_inc(a_ek, 1)

        def a_query_act(act, b, groups):
            for g in groups:
                act.wait_ge(a_fq, NG * b + g + 1)
                after(act, a_o, NG * b + g - 1)
                act.activation(qphi[:, g % 2, :], banks[5 + g % 2][:, :], ACT.Exp).then_inc(a_eq, 1)

        def a_back_act(act, b):
            act.wait_ge(a_ot, b + 1)
            after(act, A.y, b)
            act.activation(ot_sb[:, :], banks[0][:, :], ACT.Copy).then_inc(a_ots, 1)

        def a_y_act(act, b):
            act.wait_ge(A.y, b + 1)
            after(act, A.tmp, b)
            act.activation(ya[:, :], banks[7][:, :], ACT.Copy).then_inc(a_yc, 1)

        def b_front_pe(pe, b):
            after(pe, r_sub, 2 * blocks(b - LB + LR))
            if isinstance(b, int):
                after(pe, a_v, blocks(b - LB + LF))
            transpose(pe, Bp, b, xnb)

        def c_front_pe(pe, b):
            after(pe, Bp.xt, blocks(b - LC + LB + 1))
            if isinstance(b, int):
                after(pe, r_sub, 2 * blocks(b - LC + LR))
            transpose(pe, C, b, xnc)

        def r_front_pe(pe, b):
            after(pe, A.xt, blocks(b - LR + LF + 1))
            if isinstance(b, int):
                after(pe, a_ots, blocks(b - LR + LQ + 1))
                after(pe, x_cw, blocks(b - LR + 1))
                after(pe, Bp.xt, blocks(b - LR + LB + 1))
                after(pe, C.xt, blocks(b - LR + LC + 1))
            transpose(pe, R, b, xnr)

        xnb = sb("xnb", [P, TPB, D])
        xs = sb("xs", [P, 2, TB + 1])
        dx = sb("dx", [P, TB])
        xr, xk = sb("xr", [P, TB]), sb("xk", [P, TB])
        kact = sb("kact", [P, TB])
        rgate = sb("rgate", [P, TB])
        yb = sb("yb", [P, TB])
        tmpb = sb("tmpb", [P, TB])
        b_x0 = sem("b_x0")
        b_zero = sem("b_zero")
        b_dx, b_xr, b_xk = sem("b_dx"), sem("b_xr"), sem("b_xk")
        b_k, b_r, b_v = sem("b_k"), sem("b_r"), sem("b_v")
        b_kr, b_ka, b_rg = sem("b_kr"), sem("b_ka"), sem("b_rg")

        def b_stats_dve(dve, b, par):
            dve.wait_ge(A.xa, b + 1)
            dve.nop().then_inc(d_seen, 1)
            stats(dve, nb, b, par, lambda i: tile(xres, b, i), Bp.bn, Bp.mv)

        def b_shift_act(act, b, par):
            act.wait_ge(Bp.tr, b + 1)
            after(act, b_xk, b - 1)
            act.activation(xs[:, par, 1:TB + 1], banks[0][:, :], ACT.Copy).then_inc(Bp.xt, 1)
            if par:
                act.wait_ge(Bp.xt, b)
                act.activation(xs[:, 1, 0:1], xs[:, 0, TB:TB + 1], ACT.Copy).then_inc(b_x0, 2)

        def b_mix_dve(dve, b, par):
            dve.wait_ge(Bp.xt, b + 1)
            if par:
                dve.wait_ge(b_x0, b + 1)
            after(dve, b_xk, b)
            dve.tensor_tensor(dx[:, :], xs[:, par, 1:TB + 1], xs[:, par, 0:TB], ALU.subtract).then_inc(b_dx, 1)
            dve.wait_ge(b_dx, b + 1)
            after(dve, b_r, b)
            after(dve, b_k, b)
            dve.scalar_tensor_tensor(out=xr[:, :], in0=dx[:, :], scalar=mu_sb[:, 0:1],
                                     in1=xs[:, par, 0:TB], op0=ALU.mult, op1=ALU.add).then_inc(b_xr, 1)
            dve.scalar_tensor_tensor(out=xk[:, :], in0=dx[:, :], scalar=mu_sb[:, 1:2],
                                     in1=xs[:, par, 0:TB], op0=ALU.mult, op1=ALU.add).then_inc(b_xk, 1)

        def b_in_pe(pe, b):
            pe.wait_ge(b_xr, b + 1)
            after(pe, a_yc, blocks(b - LB + LQ + 1))
            for i in range(TPB):
                ins = pe.matmul(banks[7][:, i * P:(i + 1) * P], xr[:, i * P:(i + 1) * P], wr_sb[:, :],
                                start=True, stop=True)
            ins.then_inc(b_r, 1)

        def b_key_pe(pe, b):
            pe.wait_ge(b_xk, b + 1)
            pe.matmul(banks[5][:, :], wk_sb[:, :], xk[:, :], start=True, stop=True).then_inc(b_k, 1)

        def b_value_pe(pe, b):
            pe.wait_ge(b_ka, b + 1)
            pe.wait_ge(b_rg, b + 1)
            for i in range(TPB):
                ins = pe.matmul(banks[7][:, i * P:(i + 1) * P], kact[:, i * P:(i + 1) * P], wv_sb[:, :],
                                start=True, stop=True)
            ins.then_inc(b_v, 1)

        def b_gate_act(act, b):
            act.wait_ge(b_r, b + 1)
            after(act, Bp.y, b)
            act.activation(rgate[:, :], banks[7][:, :], ACT.Tanh, scale=0.5).then_inc(b_rg, 1)

        def b_key_act(act, b):
            act.wait_ge(b_k, b + 1)
            after(act, b_v, b)
            act.activation(kact[:, :], banks[5][:, :], ACT.Relu).then_inc(b_kr, 1)
            act.wait_ge(b_kr, b + 1)
            act.activation(kact[:, :], kact[:, :], ACT.Square).then_inc(b_ka, 1)

        def b_gate_dve(dve, b, par):
            dve.wait_ge(b_rg, b + 1)
            dve.wait_ge(b_v, b + 1)
            after(dve, Bp.tmp, b)
            dve.scalar_tensor_tensor(out=yb[:, :], in0=rgate[:, :], scalar=1.0, in1=banks[7][:, :],
                                     op0=ALU.add, op1=ALU.mult).then_inc(Bp.y, 1)
            dve.wait_ge(Bp.y, b + 1)
            stats(dve, nyb, b, par, lambda i: yb[:, i * P:(i + 1) * P], Bp.ybn, Bp.ymv)

        xnc = sb("xnc", [P, TPB, D])
        ut = sb("ut", [P, TB])
        lam, bu, hs = sb("lam", [NS, TB]), sb("bu", [NS, TB]), sb("hs", [NS, 2, TB])
        yc = sb("yc", [P, TB])
        tmpc = sb("tmpc", [P, TB])
        c_lb, c_lam, c_bu, c_h = sem("c_lb"), sem("c_lam"), sem("c_bu"), sem("c_h")
        c_th = sem("c_th")
        c_yc = sem("c_yc")

        def c_stats_dve(dve, b, par):
            dve.wait_ge(Bp.xa, b + 1)
            dve.nop().then_inc(d_seen, 1)
            stats(dve, ncx, b, par, lambda i: tile(xres, b, i), C.bn, C.mv)

        def c_front_act(act, b):
            act.wait_ge(C.tr, b + 1)
            after(act, C.y, b)
            act.activation(ut[:, :], banks[0][:, :], ACT.Copy).then_inc(C.xt, 1)

        def c_in_pe(pe, b):
            pe.wait_ge(C.xt, b + 1)
            pe.matmul(banks[6][0:2 * NS, :], wlb_sb[:, :], ut[:, :], start=True, stop=True).then_inc(c_lb, 1)

        def c_gates_act(act, b):
            act.wait_ge(c_lb, b + 1)
            after(act, c_lam, b)
            after(act, c_h, b)
            act.activation(bu[:, :], banks[6][NS:2 * NS, :], ACT.Copy).then_inc(c_bu, 1)
            act.activation(lam[:, :], banks[6][0:NS, :], ACT.Tanh, bias=blh_sb[:, 0:1], scale=0.5).then_inc(c_th, 1)

        def c_scan_dve(dve, b, par):
            dve.wait_ge(c_th, b + 1)
            dve.tensor_scalar(lam[:, :], lam[:, :], 0.5, 0.5, ALU.mult, ALU.add).then_inc(c_lam, 1)
            dve.wait_ge(c_lam, b + 1)
            dve.wait_ge(c_bu, b + 1)
            after(dve, C.y, b - 1)
            if par:
                dve.wait_ge(c_h, b)
            dve.tensor_tensor_scan(hs[:, par, :], lam[:, :], bu[:, :],
                                   hs[:, 0, TB - 1:TB] if par else 0.0, ALU.mult, ALU.add).then_inc(c_h, 1)

        def c_out_pe(pe, b, par):
            pe.wait_ge(c_h, b + 1)
            after(pe, a_rot, 4 * blocks(b - LC + LF + 1))
            for i in range(TPB):
                y = banks[6][:, i * P:(i + 1) * P]
                pe.matmul(y, ut[:, i * P:(i + 1) * P], dpd_sb[:, :], start=True, stop=False)
                ins = pe.matmul(y, hs[:, par, i * P:(i + 1) * P], wc_sb[:, :], start=False, stop=True)
            ins.then_inc(C.y, 1)

        def c_y_act(act, b):
            act.wait_ge(C.y, b + 1)
            after(act, C.tmp, b)
            act.activation(yc[:, :], banks[6][:, :], ACT.Copy).then_inc(c_yc, 1)

        def c_ystats_dve(dve, b, par):
            dve.wait_ge(c_yc, b + 1)
            stats(dve, nyc, b, par, lambda i: yc[:, i * P:(i + 1) * P], C.ybn, C.ymv)

        xnr = sb("xnr", [P, TPB, D])
        xh, xl = sb("xh", [P, 2, TB], F32R), sb("xl", [P, 2, TB], F32R)
        ew = sb("ew", [P, TPB, E])
        mk = sb("mk", [P, TPB, E])
        top8 = sb("top8", [P, TPB, 8])
        low = sb("low", [P, 8, TPB])
        cexp = sb("cexp", [P, TPB, E, EQ])
        cw = sb("cw", [P, 2, TB])
        r_xh, r_xl, r_lg = sem("r_xh"), sem("r_xl"), sem("r_lg")
        r_sub, r_exp = sem("r_sub"), sem("r_exp")
        r_step = sem("r_step")
        x_cexp, x_ct, x_cw = sem("x_cexp"), sem("x_ct"), sem("x_cw")

        def r_stats_dve(dve, b, par):
            dve.wait_ge(C.xa, b + 1)
            dve.nop().then_inc(d_seen, 1)
            stats(dve, nr, b, par, lambda i: tile(xres, b, i), R.bn, R.mv)

        def r_hi_act(act, b, par):
            act.wait_ge(R.tr, b + 1)
            after(act, x_u, NJ * (b - 1))
            act.activation(xh[:, par, :], banks[0][:, :], ACT.Copy).then_inc(r_xh, 1)

        def r_lo_dve(dve, b, par):
            dve.wait_ge(r_xh, b + 1)
            after(dve, x_u, NJ * (b - 1))
            dve.tensor_tensor(xl[:, par, :], banks[0][:, :], xh[:, par, :].bitcast(F32),
                              ALU.subtract).then_inc(r_xl, 1)

        def r_logits_pe(pe, b, par):
            pe.wait_ge(r_xl, b + 1)
            if isinstance(b, int) and b == 0:
                pe.wait_ge(s_wsplit, 6)
            after(pe, a_v, blocks(b - LR + LF + 1))
            for i in range(TPB):
                c = slice(i * P, (i + 1) * P)
                y = banks[0][:, i * E:(i + 1) * E]
                pe.matmul(y, xl[:, par, c], gate_hi[:, :], start=True, stop=False)
                pe.matmul(y, xh[:, par, c], gate_lo[:, :], start=False, stop=False)
                ins = pe.matmul(y, xh[:, par, c], gate_hi[:, :], start=False, stop=True)
            ins.then_inc(r_lg, 1)

        def wide(v):
            return v.unsqueeze(2).broadcast_to([P, TPB, E])

        def r_scores_dve(dve, b):
            dve.wait_ge(r_lg, b + 1)
            lg = banks[0][:, 0:TPB * E].rearrange("p (t e) -> p t e", t=TPB)
            dve.tensor_reduce(low[:, 0, :], lg, mybir.AxisListType.X, ALU.max).then_inc(r_sub, 1)
            dve.wait_ge(r_sub, 2 * b + 1)
            dve.tensor_tensor(ew[:, :, :], lg, wide(low[:, 0, :]), ALU.subtract).then_inc(r_sub, 1)

        def r_exp_act(act, b):
            act.wait_ge(r_sub, 2 * b + 2)
            act.activation(ew[:, :, :], ew[:, :, :], ACT.Exp).then_inc(r_exp, 1)

        def r_top_dve(dve, b):
            dve.wait_ge(r_exp, b + 1)
            dve.tensor_reduce(low[:, 1, :], ew[:, :, :], mybir.AxisListType.X, ALU.add).then_inc(r_step, 1)
            for t in range(TPB):
                ins = dve.max(top8[:, t, :], ew[:, t, :])
            ins.then_inc(r_step, 1)
            dve.wait_ge(r_step, 10 * b + 2)
            dve.tensor_tensor(low[:, 3, :], top8[:, :, 0], top8[:, :, 1], ALU.add).then_inc(r_step, 1)
            dve.reciprocal(low[:, 2, :], low[:, 1, :]).then_inc(r_step, 1)
            dve.wait_ge(r_step, 10 * b + 3)
            dve.tensor_scalar(top8[:, :, 2:8], top8[:, :, 2:8], 0.0, -1.0, ALU.mult, ALU.add).then_inc(r_step, 1)
            dve.wait_ge(r_step, 10 * b + 5)
            dve.tensor_tensor(low[:, 4, :], low[:, 3, :], low[:, 2, :], ALU.mult)
            for t in range(TPB):
                ins = dve.match_replace(mk[:, t, :], top8[:, t, :], ew[:, t, :], -2.0)
            ins.then_inc(r_step, 1)
            dve.wait_ge(r_step, 10 * b + 6)
            dve.tensor_scalar(low[:, 5, :], low[:, 4, :], TOP_EPS, None, ALU.add).then_inc(r_step, 1)
            dve.scalar_tensor_tensor(out=mk[:, :, :], in0=mk[:, :, :], scalar=-2.0, in1=ew[:, :, :],
                                     op0=ALU.is_equal, op1=ALU.mult).then_inc(r_step, 1)
            dve.wait_ge(r_step, 10 * b + 7)
            dve.reciprocal(low[:, 6, :], low[:, 5, :]).then_inc(r_step, 1)
            dve.wait_ge(r_step, 10 * b + 9)
            dve.scalar_tensor_tensor(out=low[:, 7, :], in0=low[:, 6, :], scalar=ROUTE_SCALE, in1=low[:, 2, :],
                                     op0=ALU.mult, op1=ALU.mult).then_inc(r_step, 1)
            dve.wait_ge(r_step, 10 * b + 10)
            after(dve, x_ct, b)
            for t in range(TPB):
                ins = dve.tensor_scalar(cexp[:, t, :, :], mk[:, t, :].unsqueeze(2).broadcast_to([P, E, EQ]),
                                        low[:, 7, t:t + 1], None, ALU.mult)
            ins.then_inc(x_cexp, 1)

        def r_weights_pe(pe, b):
            pe.wait_ge(x_cexp, b + 1)
            after(pe, C.xt, blocks(b + LC + 1))
            for i in range(TPB):
                ins = pe.transpose(banks[0][:, i * P:(i + 1) * P],
                                   cexp[:, i, :, :].rearrange("p e q -> p (e q)"), ident)
            ins.then_inc(x_ct, 1)

        def r_weights_act(act, b, par):
            act.wait_ge(x_ct, b + 1)
            after(act, x_gc, JE * (b - 1))
            act.activation(cw[:, par, :], banks[0][:, :], ACT.Copy).then_inc(x_cw, 1)

        ORDER = list(range(JE, NJ)) + list(range(JE))
        LAG = 2
        sil = sb("sil", [P, 2, TB])
        gu = sb("gu", [P, 2, TB])
        gc = sb("gc", [P, 3, TB])
        yx = sb("yx", [P, TB])
        tmpx = sb("tmpx", [P, TB])
        x_g, x_u, x_sil, x_gu = sem("x_g"), sem("x_u"), sem("x_sil"), sem("x_gu")
        x_gc = sem("x_gc")
        x_d = sem("x_d")
        x_y = sem("x_yc")

        def gate_bank(k):
            return banks[1 + 2 * k % 3]

        def up_bank(k):
            return banks[1 + (2 * k + 1) % 3]

        def x_hidden_pe(pe, b, par, k):
            j = ORDER[k]
            m, c = rows(j), slice(j * P, j * P + rows(j))
            n = NJ * b + k
            if k == 0:
                pe.wait_ge(r_xl, b + 1)
                if isinstance(b, int) and b == 0:
                    pe.wait_ge(s_wsplit, 6)
            after(pe, x_gu, n - 1 if k else n)
            if k == 1:
                after(pe, x_sil, n - 1)
            pe.matmul(gate_bank(k)[0:m, :], wg_lo[:, c], xh[:, par, :], start=True, stop=False)
            pe.matmul(gate_bank(k)[0:m, :], wg_hi[:, c], xl[:, par, :], start=False, stop=False)
            pe.matmul(gate_bank(k)[0:m, :], wg_hi[:, c], xh[:, par, :], start=False, stop=True).then_inc(x_g, 1)
            if k:
                pe.wait_ge(x_sil, n)
            pe.matmul(up_bank(k)[0:m, :], wu_lo[:, c], xh[:, par, :], start=True, stop=False)
            pe.matmul(up_bank(k)[0:m, :], wu_hi[:, c], xl[:, par, :], start=False, stop=False)
            pe.matmul(up_bank(k)[0:m, :], wu_hi[:, c], xh[:, par, :], start=False, stop=True).then_inc(x_u, 1)

        def x_down_pe(pe, b, k):
            j = ORDER[k]
            if j < JE:
                pe.wait_ge(x_gc, JE * b + j + 1)
            else:
                pe.wait_ge(x_gu, NJ * b + k + 1)
            if k == 0:
                after(pe, x_y, b)
            m = rows(j)
            src = gc[0:m, k % 3, :]
            for i in range(TPB):
                ins = pe.matmul(banks[4][:, i * P:(i + 1) * P], src[:, i * P:(i + 1) * P], wd_sb[0:m, j, :],
                                start=(k == 0 and i == 0), stop=True, skip_group_check=True)
            ins.then_inc(x_d, 1)

        def x_chunk_act(act, b, k):
            m = rows(ORDER[k])
            act.wait_ge(x_g, NJ * b + k + 1)
            after(act, x_gu, NJ * b + k - 1)
            act.activation(sil[0:m, k % 2, :], gate_bank(k)[0:m, :], ACT.Silu).then_inc(x_sil, 1)

        def x_chunk_dve(dve, b, k):
            j = ORDER[k]
            m = rows(j)
            dve.wait_ge(x_u, NJ * b + k + 1)
            dve.wait_ge(x_sil, NJ * b + k + 1)
            if j < JE:
                after(dve, x_gc, JE * b + j - 1 if j >= 2 else JE * b)
                dst = gu[0:m, j % 2, :]
            else:
                after(dve, x_d, NJ * b)
                dst = gc[0:m, k, :]
            dve.tensor_tensor(dst, up_bank(k)[0:m, :], sil[0:m, k % 2, :], ALU.mult).then_inc(x_gu, 1)

        def x_chunk_pool(pool, b, par, k):
            j = ORDER[k]
            if j >= JE:
                return
            if j == 0:
                pool.wait_ge(x_cw, b + 1)
            pool.wait_ge(x_gu, NJ * b + k + 1)
            after(pool, x_d, NJ * b + k - 2)
            pool.tensor_tensor(gc[:, k % 3, :], gu[:, j % 2, :], cw[:, par, :], ALU.mult).then_inc(x_gc, 1)

        def x_y_act(act, b):
            act.wait_ge(x_d, NJ * (b + 1))
            after(act, X.tmp, b)
            act.activation(yx[:, :], banks[4][:, :], ACT.Copy).then_inc(x_y, 1)

        def x_ystats_dve(dve, b, par):
            dve.wait_ge(x_y, b + 1)
            stats(dve, nx, b, par, lambda i: yx[:, i * P:(i + 1) * P], X.ybn, X.ymv)

        def together(eng, chunk, pieces):
            def iteration(i, par):
                loop = not isinstance(i, int)
                for k in range(-1, NJ):
                    if k >= 0 and (loop or 0 <= i < NB):
                        chunk(i, par, k)
                    for slot, lag, step in pieces:
                        if slot == k and (loop or 0 <= i + lag < NB):
                            step(i + lag, (par + lag) % 2)

            start, stop = 2, (NB - LF) // 2 * 2
            for i in range(-LF, start):
                iteration(i, i % 2)
            with eng.Fori(start // 2, stop // 2) as s:
                iteration(s * 2, 0)
                iteration(s * 2 + 1, 1)
            for i in range(stop, NB + 1):
                iteration(i, i % 2)

        block = ctx.enter_context(nc.Block())

        @block.sync
        def _(sp):
            for dst, src in ((cst, consts), (wqkv_sb, wqkv)):
                sp.dma_start(dst[:, :], src).then_inc(s_cst, 16)
            for b in range(2):
                sp.dma_start(xres[:, b * TB:(b + 1) * TB].rearrange("p (t d) -> p t d", t=TPB),
                             x[b].rearrange("(t p) d -> p t d", p=P)).then_inc(s_x[0], 16)
            sp.dma_start(s1_sb[:, :], s1c).then_inc(s_wA, 16)
            sp.dma_start(s23_sb[:, :, :], s23).then_inc(s_wA, 16)
            sp.dma_start(scl_sb[:, :, :], scl).then_inc(s_wA, 16)
            sp.dma_start(wout_sb[:, :], wout).then_inc(s_wA, 16)
            sp.dma_start(xres[:, 2 * TB:NB * TB].rearrange("p (c t d) -> p (c t) d", c=NB - 2, t=TPB),
                         x[2:NB].rearrange("c (t p) d -> p (c t) d", p=P)).then_inc(s_x[1], 16)
            for dst, src in ((wr_sb, wr), (wk_sb, wk), (wv_sb, wv), (mu_sb, mu)):
                sp.dma_start(dst[:, :], src).then_inc(s_wB, 16)
            for dst, src in ((wlb_sb, wlb), (bl_sb, bl), (wc_sb, wc), (dp_sb, dp), (gate_sb, gate)):
                sp.dma_start(dst[:, :], src).then_inc(s_wC, 16)
            sp.dma_start(wstage[:, :], wg).then_inc(s_w1, 16)
            sp.dma_start(wd_sb[:, 0:NJ - 1, :], wd[0:(NJ - 1) * P, :].rearrange("(j p) d -> p j d", p=P)).then_inc(s_w3, 16)
            sp.dma_start(wd_sb[0:LAST, NJ - 1, :], wd[(NJ - 1) * P:HF, :]).then_inc(s_w3, 16)
            sp.wait_ge(s_wsplit, 2)
            sp.dma_start(wstage[:, :], wu).then_inc(s_w2, 16)
            with sp.Fori(0, NB) as b:
                sp.wait_ge(X.xa, b + 1)
                sp.dma_start(out[bass.ds(b, 1), :, :].rearrange("c (t p) d -> p (c t) d", p=P),
                             blk(xres, b).rearrange("p (t d) -> p t d", t=TPB)).then_inc(s_out, 16)
            sp.wait_ge(s_out, 16 * NB)

        @block.gpsimd
        def _(pool):
            pool.memset(mhalf[:, :], -0.5).then_inc(s_prep, 1)
            pool.memset(vals[:, :, :, DH:VW], 1.0).then_inc(a_ones, 1)
            pool.wait_ge(s_prep, 1)

            pool.memset(xs[:, 0, 0:1], 0.0).then_inc(b_zero, 1)

            together(pool, lambda b, par, k: x_chunk_pool(pool, b, par, k), [
                (-1, LB, lambda b, p: root(pool, Bp.mv, Bp.rs, nb.m, nb.r, nb.n, b, p)),
                (-1, LC, lambda b, p: root(pool, C.mv, C.rs, ncx.m, ncx.r, ncx.n, b, p)),
                (-1, LF, lambda b, p: root(pool, A.mv, A.rs, na.m, na.r, na.n, b, p)),
                (-1, LR, lambda b, p: root(pool, R.mv, R.rs, nr.m, nr.r, nr.n, b, p)),
                (2, -1, lambda b, p: root(pool, X.ymv, X.yrs, nx.m, nx.r, nx.n, b, p)),
                (3, LQ, lambda b, p: root(pool, A.ymv, A.yrs, nya.m, nya.r, nya.n, b, p)),
                (4, -1, lambda b, p: add_residual(pool, X, b, tmpx)),
                (5, LQ, lambda b, p: add_residual(pool, A, b, tmpa)),
                (7, LB, lambda b, p: root(pool, Bp.ymv, Bp.yrs, nyb.m, nyb.r, nyb.n, b, p, 4 * LN_EPS)),
                (8, LC, lambda b, p: root(pool, C.ymv, C.yrs, nyc.m, nyc.r, nyc.n, b, p)),
                (9, LB, lambda b, p: add_residual(pool, Bp, b, tmpb)),
                (10, LC, lambda b, p: add_residual(pool, C, b, tmpc)),
            ])

        @block.scalar
        def _(act):
            act.wait_ge(s_dpd, 2)
            act.wait_ge(a_ones, 1)

            together(act, lambda b, par, k: x_chunk_act(act, b, k), [
                (-1, 0, lambda b, p: r_exp_act(act, b)),
                (-1, LK, lambda b, p: a_keys_act(act, b)),
                (-1, LB, lambda b, p: b_shift_act(act, b, p)),
                (-1, LQ, lambda b, p: a_query_act(act, b, range(0, 1))),
                (-1, LC, lambda b, p: c_front_act(act, b)),
                (-1, LQ, lambda b, p: a_query_act(act, b, range(1, 3))),
                (-1, 0, lambda b, p: r_weights_act(act, b, p)),
                (-1, LQ, lambda b, p: a_query_act(act, b, range(3, NG))),
                (0, -1, lambda b, p: x_y_act(act, b)),
                (0, LB, lambda b, p: b_key_act(act, b)),
                (0, LC, lambda b, p: c_gates_act(act, b)),
                (1, LQ, lambda b, p: a_back_act(act, b)),
                (2, LF, lambda b, p: a_xt_act(act, b)),
                (3, LQ, lambda b, p: a_y_act(act, b)),
                (3, -1, lambda b, p: apply(act, X, nx, b, p, yx, tmpx)),
                (4, LF, lambda b, p: a_squares_q_act(act, b, p)),
                (5, LR, lambda b, p: r_hi_act(act, b, p)),
                (5, LB, lambda b, p: b_gate_act(act, b)),
                (5, LQ, lambda b, p: apply(act, A, nya, b, p, ya, tmpa)),
                (6, LF, lambda b, p: a_squares_k_act(act, b)),
                (7, LC, lambda b, p: c_y_act(act, b)),
                (8, LF, lambda b, p: a_values_act(act, b)),
                (8, LB, lambda b, p: apply(act, Bp, nyb, b, p, yb, tmpb)),
                (9, LC, lambda b, p: apply(act, C, nyc, b, p, yc, tmpc)),
            ])

        @block.tensor
        def _(pe):
            pe.wait_ge(s_cst, 32)
            for n in range(2):
                pe.wait_ge(s_sorf_v, n + 1)
                if n == 0:
                    pe.matmul(banks[1][0:PP, 0:P], had, sorf_a[:, :, :], start=True, stop=True).then_inc(s_sorf_p, 1)
                else:
                    for h in range(2):
                        ins = pe.matmul(banks[2][0:PP, h * M:(h + 1) * M],
                                        sorf_b[:, h * HH:(h + 1) * HH, :].rearrange("p h d -> p (h d)"),
                                        had[:, 0:M], start=True, stop=True)
                    ins.then_inc(s_sorf_p, 1)
            pe.wait_ge(s_sorf_v, 6)
            pe.wait_ge(s_wA, 4 * 16)
            pe.wait_ge(s_wB, 4 * 16)
            pe.wait_ge(s_wC, 5 * 16)

            def chunk(b, par, k):
                if isinstance(b, int) and b == 0 and k == 0:
                    pe.wait_ge(s_w3, 2 * 16)
                x_hidden_pe(pe, b, par, k)
                if k >= LAG:
                    x_down_pe(pe, b, k - LAG)

            def tail(b):
                for k in range(NJ - LAG, NJ):
                    x_down_pe(pe, b, k)

            together(pe, chunk, [
                (-1, LK, lambda b, p: a_keys_pe(pe, b, range(0, 2))),
                (-1, -1, lambda b, p: tail(b)),
                (-1, LK, lambda b, p: a_keys_pe(pe, b, range(2, TPB))),
                (-1, LB, lambda b, p: b_front_pe(pe, b)),
                (-1, LK, lambda b, p: a_keys_pe(pe, b, range(TPB, TPB + 1))),
                (-1, LQ, lambda b, p: a_query_pe(pe, b, p, range(0, 1))),
                (-1, LC, lambda b, p: c_front_pe(pe, b)),
                (-1, LQ, lambda b, p: a_query_pe(pe, b, p, range(1, 3))),
                (-1, 0, lambda b, p: r_weights_pe(pe, b)),
                (-1, LQ, lambda b, p: a_query_pe(pe, b, p, range(3, NG + 1))),
                (0, LB, lambda b, p: b_key_pe(pe, b)),
                (0, LC, lambda b, p: c_in_pe(pe, b)),
                (1, LQ, lambda b, p: a_back_pe(pe, b)),
                (2, LF, lambda b, p: a_front_pe(pe, b)),
                (2, LQ, lambda b, p: a_out_pe(pe, b)),
                (3, LF, lambda b, p: a_products_pe(pe, b, 0)),
                (4, LR, lambda b, p: r_front_pe(pe, b)),
                (4, LB, lambda b, p: b_in_pe(pe, b)),
                (5, LF, lambda b, p: a_products_pe(pe, b, 1)),
                (6, LB, lambda b, p: b_value_pe(pe, b)),
                (7, LF, lambda b, p: a_values_pe(pe, b)),
                (7, LC, lambda b, p: c_out_pe(pe, b, p)),
                (8, LR, lambda b, p: r_logits_pe(pe, b, p)),
            ])

        @block.vector
        def _(dve):
            dve.wait_ge(s_wA, 4 * 16)
            dve.wait_ge(s_wB, 4 * 16)
            dve.wait_ge(s_cst, 32)
            dve.tensor_tensor(sorf_a[:, :, :], had[:, 0:DH].unsqueeze(1).broadcast_to([PP, H, DH]),
                              s23_sb[:, 0, :].unsqueeze(2).broadcast_to([PP, H, DH]), ALU.mult).then_inc(s_sorf_v, 1)
            dve.wait_ge(s_sorf_p, 1)
            dve.tensor_tensor(sorf_b[:, :, :], banks[1][0:PP, 0:P].rearrange("p (h d) -> p h d", h=H),
                              s23_sb[:, 1, :].unsqueeze(2).broadcast_to([PP, H, DH]), ALU.mult).then_inc(s_sorf_v, 1)
            dve.wait_ge(s_sorf_p, 2)
            for h in range(2):
                ins = dve.tensor_scalar(sorf_c[:, h, :], banks[2][0:PP, h * M:(h + 1) * M], s1_sb[:, h:h + 1],
                                        1.0 / PP ** 2, ALU.mult, ALU.mult)
            ins.then_inc(s_sorf_v, 1)
            dve.wait_ge(s_sorf_v, 3)
            dve.tensor_tensor(sorf_d[:, :, :], sorf_c[:, :, :], scl_sb[:, :, :], ALU.mult).then_inc(s_sorf_v, 1)
            dve.wait_ge(s_sorf_v, 4)
            m8 = cst[:, C_M8:C_M8 + HH]
            for h in range(2):
                ins = dve.tensor_tensor(feat[0:PP, h, :, :], sorf_d[:, h, :].unsqueeze(1).broadcast_to([PP, HH, M]),
                                        m8[0:PP].unsqueeze(2).broadcast_to([PP, HH, M]), ALU.mult)
            ins.then_inc(s_sorf_v, 1)
            for h in range(2):
                ins = dve.tensor_copy(feat[PP:P, h, :, :], m8[PP:P].unsqueeze(2).broadcast_to([PP, HH, M]))
            ins.then_inc(s_sorf_v, 1)

            dve.wait_ge(s_wC, 5 * 16)
            dve.tensor_scalar(dpd_sb[:, :], ident, dp_sb[:, 0:1], None, ALU.mult).then_inc(s_dpd, 1)
            dve.tensor_scalar(blh_sb[:, :], bl_sb[:, :], 0.5, None, ALU.mult).then_inc(s_dpd, 1)

            def split_w(hi, lo, src, k):
                dve.tensor_copy(hi[:, :], src[:, :]).then_inc(s_wsplit, 1)
                dve.wait_ge(s_wsplit, k + 1)
                dve.tensor_tensor(lo[:, :], src[:, :], hi[:, :].bitcast(F32), ALU.subtract).then_inc(s_wsplit, 1)

            def split_router(b):
                if isinstance(b, int) and b == 0:
                    split_w(gate_hi, gate_lo, gate_sb, 4)

            def split_gate(b):
                if isinstance(b, int) and b == 0:
                    dve.wait_ge(s_w1, 16)
                    split_w(wg_hi, wg_lo, wstage, 0)

            def split_up(b):
                if isinstance(b, int) and b == 0:
                    dve.wait_ge(s_w2, 16)
                    split_w(wu_hi, wu_lo, wstage, 2)

            def a_stats(b, par):
                if isinstance(b, int) and b in (0, 2):
                    dve.wait_ge(s_x[b // 2], 32 if b == 0 else 16)
                stats(dve, na, b, par, lambda i: tile(xres, b, i), A.bn, A.mv)

            together(dve, lambda b, par, k: x_chunk_dve(dve, b, k), [
                (-1, LB, lambda b, p: b_stats_dve(dve, b, p)),
                (-1, LC, lambda b, p: c_stats_dve(dve, b, p)),
                (-1, LF, lambda b, p: a_stats(b, p)),
                (-1, LB, lambda b, p: normalise(dve, Bp, nb, b, p, xnb)),
                (-1, LC, lambda b, p: normalise(dve, C, ncx, b, p, xnc)),
                (-1, 0, lambda b, p: r_top_dve(dve, b)),
                (-1, LR, lambda b, p: r_stats_dve(dve, b, p)),
                (-1, LK, lambda b, p: a_state_dve(dve, b, p)),
                (-1, LB, lambda b, p: b_mix_dve(dve, b, p)),
                (-1, LQ, lambda b, p: a_divide_dve(dve, b, 0)),
                (-1, LF, lambda b, p: normalise(dve, A, na, b, p, xna)),
                (-1, LR, lambda b, p: normalise(dve, R, nr, b, p, xnr)),
                (-1, LQ, lambda b, p: a_divide_dve(dve, b, 1)),
                (-1, LR, lambda b, p: split_router(b)),
                (-1, LQ, lambda b, p: split_gate(b)),
                (-1, LB, lambda b, p: split_up(b)),
                (1, LC, lambda b, p: c_scan_dve(dve, b, p)),
                (1, -1, lambda b, p: x_ystats_dve(dve, b, p)),
                (3, LQ, lambda b, p: stats(dve, nya, b, p, lambda i: ya[:, i * P:(i + 1) * P],
                                           A.ybn, A.ymv, a_yc)),
                (3, LF, lambda b, p: a_cat_dve(dve, b, p, 0)),
                (5, LR, lambda b, p: r_lo_dve(dve, b, p)),
                (5, LF, lambda b, p: a_cat_dve(dve, b, p, 1)),
                (7, LB, lambda b, p: b_gate_dve(dve, b, p)),
                (8, LC, lambda b, p: c_ystats_dve(dve, b, p)),
                (9, LR, lambda b, p: r_scores_dve(dve, b)),
            ])


def constants():
    c = np.zeros((P, C_N), np.float32)
    freqs = np.float32(10000.0) ** (-np.arange(0, DH, 2, dtype=np.float32) / np.float32(DH))
    ang = np.arange(L - 1, dtype=np.float32)[:, None] * freqs.astype(np.float32)
    ang = np.concatenate([np.zeros((1, DH // 2), np.float32), ang]).astype(np.float64)
    ch = np.arange(P)
    pair = (ch % DH) // 2
    c[:, C_COS:C_COS + L] = np.cos(ang)[:, pair].T
    c[:, C_SIN:C_SIN + L] = np.sin(ang)[:, pair].T * np.where(ch % 2 == 0, -1.0, 1.0)[:, None]
    c[:, C_ID:C_ID + P] = np.eye(P)
    had = np.ones((1, 1))
    while had.shape[0] < PP:
        had = np.block([[had, had], [had, -had]])
    c[0:PP, C_HAD:C_HAD + PP] = had
    own = (np.arange(PP)[:, None] // DH) == np.arange(HH)[None, :]
    c[0:PP, C_M8:C_M8 + HH] = own
    c[PP:P, C_M8:C_M8 + HH] = -0.5 * own
    c[:, C_M4:C_M4 + GH] = ((ch[:, None] // M) == np.arange(GH)[None, :]) / float(M)
    return c


def kernel(L0_attn_x, L0_attn_w_qkv, L0_attn_w_out, L0_attn_sorf_signs, L0_attn_sorf_scales, L0_ffn_W_r, L0_ffn_W_k,
           L0_ffn_W_v, L0_ffn_mu_r, L0_ffn_mu_k, L1_attn_Wl, L1_attn_bl, L1_attn_Wb, L1_attn_Wc, L1_attn_Dp,
           L1_ffn_gate_w, L1_ffn_w_gate, L1_ffn_w_up, L1_ffn_w_down, L1_ffn_sw_gate, L1_ffn_sw_up, L1_ffn_sw_down):
    import concourse.bacc as bacc
    from concourse.bass_utils import run_bass_kernel_spmd

    swap = np.arange(D).reshape(-1, 2)[:, ::-1].reshape(-1)
    q, k, v = (np.asarray(L0_attn_w_qkv)[i * D:(i + 1) * D] for i in range(3))
    signs = np.asarray(L0_attn_sorf_signs)[:, 0]
    scales = np.asarray(L0_attn_sorf_scales)[:, 0, 0:M]

    def experts(w, shared):
        w = np.asarray(w).reshape(E, D, JE, EQ).transpose(1, 2, 0, 3).reshape(D, E * F)
        return np.concatenate([w, np.asarray(shared)], axis=1)

    arrays = {
        "x": np.asarray(L0_attn_x).reshape(NB, TB, D),
        "wqkv": np.concatenate([q, q[swap], k, k[swap], v]).T,
        "wout": np.asarray(L0_attn_w_out).T,
        "consts": constants(),
        "s1c": signs[:, 0, 0:DH].reshape(2, PP).T,
        "s23": signs[:, 1:3].transpose(2, 1, 0),
        "scl": np.broadcast_to(scales.reshape(2, HH, 1, M), (2, HH, DH, M)).transpose(1, 2, 0, 3).reshape(PP, 2, M),
        "wr": np.asarray(L0_ffn_W_r).T, "wk": np.asarray(L0_ffn_W_k).T, "wv": np.asarray(L0_ffn_W_v).T,
        "mu": np.stack([np.asarray(L0_ffn_mu_r), np.asarray(L0_ffn_mu_k)], axis=1),
        "wlb": np.concatenate([np.asarray(L1_attn_Wl), np.asarray(L1_attn_Wb)]).T,
        "bl": np.asarray(L1_attn_bl).reshape(NS, 1),
        "wc": np.asarray(L1_attn_Wc).T,
        "dp": np.asarray(L1_attn_Dp).reshape(D, 1),
        "gate": np.asarray(L1_ffn_gate_w).T,
        "wg": experts(L1_ffn_w_gate, L1_ffn_sw_gate),
        "wu": experts(L1_ffn_w_up, L1_ffn_sw_up),
        "wd": np.concatenate([np.asarray(L1_ffn_w_down).reshape(E, JE, EQ, D).transpose(1, 0, 2, 3).reshape(E * F, D),
                              np.asarray(L1_ffn_sw_down)]),
    }
    nc = bacc.Bacc("TRN2", target_bir_lowering=False, num_devices=1)
    arrays = {n: np.ascontiguousarray(a) for n, a in arrays.items()}
    args = [nc.dram_tensor(n, a.shape, F32, kind="ExternalInput").ap() for n, a in arrays.items()]
    args.append(nc.dram_tensor("out", (NB, TB, D), F32, kind="ExternalOutput").ap())
    build(nc, *args)
    r = run_bass_kernel_spmd(nc, [arrays], core_ids=[0])
    return r.results[0]["out"].reshape(B, L, D)
```

```python
from contextlib import ExitStack

import numpy as np

import concourse.bass as bass
from concourse import mybir

F32 = mybir.dt.float32
F32R = mybir.dt.float32r
ALU = mybir.AluOpType
ACT = mybir.ActivationFunctionType

P = 128
B, L, D = 8, 1024, 128
TB = 512
TPB = TB // P
NB = B * L // TB
BPS = L // TB
H, DH = 16, 8
M = 32
PP = 64
HH = H // 2
GH = P // M
NG = H // GH
VW = DH + 1
NS = 32
E, F = 8, 176
SF = 352
EQ = P // E
JE = F // EQ
HF = E * F + SF
NJ = -(-HF // P)
LAST = HF - (NJ - 1) * P
LN_EPS = 1e-5
DEN_EPS = 1e-6
TOP_EPS = 1e-20
ROUTE_SCALE = 2.5

C_ID = 0
C_HAD = C_ID + P
C_M8 = C_HAD + PP
C_M4 = C_M8 + HH
C_COS = C_M4 + GH
C_SIN = C_COS + L
C_N = C_SIN + L


def rows(j):
    return P if j < NJ - 1 else LAST


def build(nc, x, wqkv, wout, consts, s1c, s23, scl, wr, wk, wv, mu, wlb, bl, wc, dp, gate, wg, wu, wd, out):
    ctx = ExitStack()
    with ctx:
        def sb(name, shape, dt=F32):
            return ctx.enter_context(nc.sbuf_tensor(name, shape, dt))

        def sem(name):
            return ctx.enter_context(nc.semaphore(name))

        banks = [ctx.enter_context(nc.psum_tensor(f"bank{i}", [P, TB], F32)) for i in range(8)]

        xres = sb("xres", [P, NB * TB])
        cst = sb("cst", [P, C_N])
        ident = cst[:, C_ID:C_ID + P]
        had = cst[0:PP, C_HAD:C_HAD + PP]
        wout_sb = sb("wout_sb", [P, D])
        s1_sb = sb("s1_sb", [PP, 2])
        s23_sb = sb("s23_sb", [PP, 2, H])
        scl_sb = sb("scl_sb", [PP, 2, M])
        wr_sb, wk_sb, wv_sb = sb("wr_sb", [P, D]), sb("wk_sb", [P, D]), sb("wv_sb", [P, D])
        mu_sb = sb("mu_sb", [P, 2])
        wlb_sb = sb("wlb_sb", [P, 2 * NS])
        bl_sb = sb("bl_sb", [NS, 1])
        wc_sb = sb("wc_sb", [NS, D])
        dp_sb = sb("dp_sb", [P, D])
        gate_sb = sb("gate_sb", [P, E])
        blh_sb = sb("blh_sb", [NS, 1])
        wstage = sb("wstage", [P, HF])
        gate_hi, gate_lo = sb("gate_hi", [P, E], F32R), sb("gate_lo", [P, E], F32R)
        wg_hi, wg_lo = sb("wg_hi", [P, HF], F32R), sb("wg_lo", [P, HF], F32R)
        wu_hi, wu_lo = sb("wu_hi", [P, HF], F32R), sb("wu_lo", [P, HF], F32R)
        wd_sb = sb("wd_sb", [P, NJ, D])
        feat = sb("feat", [P, 2, HH, M])
        sorf_a = sb("sorf_a", [PP, H, DH])
        sorf_b = sb("sorf_b", [PP, H, DH])
        sorf_c = sb("sorf_c", [PP, 2, M])
        sorf_d = sb("sorf_d", [PP, 2, M])
        mhalf = sb("mhalf", [P, 8])
        warm = sb("warm", [P, 1])

        l_consts, l_rope = sem("l_consts"), sem("l_rope")
        l_x = [sem(f"l_x{i}") for i in range(3)]
        l_attn, l_mix, l_rec = sem("l_attn"), sem("l_mix"), sem("l_rec")
        l_gate, l_up, l_down = sem("l_gate"), sem("l_up"), sem("l_down")
        s_prep = sem("s_prep")
        s_sorf_v, s_sorf_p = sem("s_sorf_v"), sem("s_sorf_p")
        s_blh = sem("s_blh")
        s_wsplit = sem("s_wsplit")
        s_out = sem("s_out")

        class Phase:
            def __init__(self, n):
                self.bn = sem(n + "_bn")
                self.mv = sem(n + "_mv")
                self.rs = sem(n + "_rs")
                self.xn = sem(n + "_xn")
                self.tr = sem(n + "_tr")
                self.xt = sem(n + "_xt")
                self.y = sem(n + "_y")
                self.ybn = sem(n + "_ybn")
                self.ymv = sem(n + "_ymv")
                self.yrs = sem(n + "_yrs")
                self.tmp = sem(n + "_tmp")
                self.xa = sem(n + "_xa")

        A, Bp, C, R, X = Phase("a"), Phase("b"), Phase("c"), Phase("r"), Phase("x")

        class Norm:
            def __init__(self, n):
                self.st = sb(n + "_st", [P, 2, TPB, 6])
                self.m = sb(n + "_m", [P, 2, TPB, 5])
                self.r = sb(n + "_r", [P, 2, 3, TPB])
                self.n = sb(n + "_n", [P, 2, TPB])

        def after(eng, s, n):
            if not isinstance(n, int) or n > 0:
                eng.wait_ge(s, n)

        def blocks(n):
            return min(max(n, 0), NB) if isinstance(n, int) else n

        def blk(t, b):
            return t[:, bass.ds(b * TB, TB)]

        def tile(t, b, i):
            return t[:, bass.ds(b * TB + i * P, P)]

        def aggregate(dve, stats, m, par, seen, done, b):
            dve.wait_ge(seen, 4 * b + 1)
            s = stats[:, par, :, :]
            dve.tensor_tensor(m[:, par, :, 2], s[:, :, 1], s[:, :, 4], ALU.subtract).then_inc(seen, 1)
            dve.tensor_tensor(m[:, par, :, 3], s[:, :, 2], s[:, :, 5], ALU.add)
            dve.tensor_tensor(m[:, par, :, 0], s[:, :, 1], s[:, :, 4], ALU.add)
            dve.wait_ge(seen, 4 * b + 2)
            dve.scalar_tensor_tensor(out=m[:, par, :, 4], in0=m[:, par, :, 2], scalar=D / 4.0,
                                     in1=m[:, par, :, 2], op0=ALU.mult, op1=ALU.mult).then_inc(seen, 2)
            dve.wait_ge(seen, 4 * b + 4)
            dve.tensor_tensor(m[:, par, :, 1], m[:, par, :, 3], m[:, par, :, 4], ALU.add).then_inc(done, 1)

        def root(pool, ready, done, m, r, n, b, par, eps=LN_EPS):
            pool.wait_ge(ready, b + 1)
            pool.tensor_tensor(n[:, par, :], m[:, par, :, 0], mhalf[:, 0:TPB], ALU.mult).then_inc(done, 1)
            pool.tensor_scalar(r[:, par, 0, :], m[:, par, :, 1], 1.0 / D, eps, ALU.mult, ALU.add).then_inc(done, 1)
            pool.wait_ge(done, 4 * b + 2)
            pool.tensor_tensor(r[:, par, 1, :], r[:, par, 0, :], mhalf[:, 0:TPB], ALU.pow).then_inc(done, 1)
            pool.wait_ge(done, 4 * b + 3)
            pool.tensor_tensor(r[:, par, 2, :], n[:, par, :], r[:, par, 1, :], ALU.mult).then_inc(done, 1)

        LR, LC, LB, LQ, LK, LF = 1, 2, 3, 4, 5, 6
        na, nya, nb, nyb, ncx, nyc, nr, nx = (Norm(n) for n in ("na", "nya", "nb", "nyb", "nc", "nyc", "nr", "nx"))

        def lags(i):
            return tuple(i + lag for lag in range(-1, LF + 1))

        def has(b):
            return not isinstance(b, int) or 0 <= b < NB

        def first(b):
            return isinstance(b, int) and b == 0

        def early(b, lag):
            return isinstance(b, int) and b <= lag

        def late(i):
            return isinstance(i, int) and i >= NB - LQ

        def stats(dve, n, b, par, src, seen, done, ready=None):
            if ready is not None:
                dve.wait_ge(ready, b + 1)
            for i in range(TPB):
                ins = dve.bn_stats(n.st[:, par, i, :], src(i))
            ins.then_inc(seen, 1)
            aggregate(dve, n.st, n.m, par, seen, done, b)

        def normalise(dve, ph, n, b, par, dst):
            dve.wait_ge(ph.rs, 4 * b + 4)
            after(dve, ph.tr, b)
            for i in range(TPB):
                ins = dve.tensor_scalar(dst[:, i, :], tile(xres, b, i), n.r[:, par, 1, i:i + 1],
                                        n.r[:, par, 2, i:i + 1], ALU.mult, ALU.add)
            ins.then_inc(ph.xn, 1)

        def transpose(pe, ph, b, src, bank=banks[0]):
            pe.wait_ge(ph.xn, b + 1)
            for i in range(TPB):
                ins = pe.transpose(bank[:, i * P:(i + 1) * P], src[:, i, :], ident)
            ins.then_inc(ph.tr, 1)

        def apply(act, ph, n, b, par, y, dst):
            act.wait_ge(ph.yrs, 4 * b + 4)
            after(act, ph.xa, b)
            for i in range(TPB):
                ins = act.activation(dst[:, i * P:(i + 1) * P], y[:, i * P:(i + 1) * P], ACT.Identity,
                                     scale=n.r[:, par, 1, i:i + 1], bias=n.r[:, par, 2, i:i + 1])
            ins.then_inc(ph.tmp, 1)

        p_seen, d_seen = sem("p_seen"), sem("d_seen")

        def add_residual(pool, ph, b, src):
            pool.wait_ge(ph.tmp, b + 1)
            pool.nop().then_inc(p_seen, 1)
            pool.tensor_tensor(blk(xres, b), blk(xres, b), src[:, :], ALU.add).then_inc(ph.xa, 1)

        wqkv_sb = sb("wqkv_sb", [P, 5 * D])
        xna = sb("xna", [P, TPB, D])
        xta = sb("xta", [P, TB])
        cat_q = sb("cat_q", [P, 2, 2, TB])
        cat_k = sb("cat_k", [P, 2, TB])
        rot = sb("rot", [P, 2, TB])
        vals = sb("vals", [P, TPB, H, VW])
        kphi = sb("kphi", [P, 2, H * M])
        qphi = sb("qphi", [P, 2, TB])
        s_even = sb("s_even", [P, H * VW])
        s_all = sb("s_all", [P, H * VW])
        sbd = sb("sbd", [P, NG, GH, VW])
        den = sb("den", [P, 2, TPB, HH])
        rden = sb("rden", [P, 2, TPB, HH])
        o_sb = sb("o_sb", [P, TPB, H, DH])
        ot_sb = sb("ot_sb", [P, TB])
        ya = sb("ya", [P, TB])
        tmpa = sb("tmpa", [P, TB])
        a_q, a_qs = sem("a_q"), sem("a_qs")
        a_rot = sem("a_rot")
        a_catr = sem("a_catr")
        a_cats = sem("a_cats")
        a_vp, a_v = sem("a_vp"), sem("a_v")
        a_ones = sem("a_ones")
        a_fk, a_ek = sem("a_fk"), sem("a_ek")
        a_s = sem("a_s")
        a_sum = sem("a_sum")
        a_state = sem("a_state")
        a_fq, a_eq = sem("a_fq"), sem("a_eq")
        a_o = sem("a_o")
        a_den = sem("a_den")
        a_on = sem("a_on")
        a_ot, a_ots = sem("a_ot"), sem("a_ots")
        a_yc = sem("a_yc")
        OW = HH * VW

        def a_banks(b):
            if early(b, LF - 1):
                return banks[4], banks[5:7], banks[1:3], banks[3]
            return banks[0], banks[5:7], banks[5:7], banks[0]

        def a_front_pe(pe, b):
            if not early(b, LF - 1):
                after(pe, a_ots, blocks(b - LF + LQ + 1))
            transpose(pe, A, b, xna, a_banks(b)[0])

        def a_products_pe(pe, b, n):
            m = 2 - 2 * n
            if n == 0:
                pe.wait_ge(A.xt, b + 1)
                after(pe, b_kr, blocks(b - LF + LB + 1))
                after(pe, c_th, blocks(b - LF + LC + 1))
                if isinstance(b, int):
                    after(pe, a_rot, 4 * b)
            elif not early(b, LF - 1):
                pe.wait_ge(a_rot, 4 * b + 2)
            elif b == 0:
                pe.wait_ge(s_sorf_v, 3)
            plain, swapped = a_banks(b)[1 + n]
            pe.matmul(plain[:, :], wqkv_sb[:, m * D:(m + 1) * D], xta[:, :],
                      start=True, stop=True).then_inc(a_q, 1)
            pe.matmul(swapped[:, :], wqkv_sb[:, (m + 1) * D:(m + 2) * D], xta[:, :],
                      start=True, stop=True).then_inc(a_qs, 1)

        def a_values_pe(pe, b):
            if early(b, LF - 1):
                after(pe, a_v, b)
            else:
                after(pe, r_xl, blocks(b - LF + LR + 1))
            bank = a_banks(b)[3]
            for i in range(TPB):
                ins = pe.matmul(bank[:, i * P:(i + 1) * P], xta[:, i * P:(i + 1) * P],
                                wqkv_sb[:, 4 * D:5 * D], start=True, stop=True)
            ins.then_inc(a_vp, 1)

        def a_rotated(i):
            return 4 * blocks(i + LF + 1) - (2 if early(i, -1) else 0)

        def a_bank_pe(pe, i, bank):
            if bank == 5:
                after(pe, a_rot, a_rotated(i - 1))
                if isinstance(i, int):
                    after(pe, b_kr, blocks(i + LB))
            elif bank == 6:
                after(pe, c_yc, blocks(i + LC))
            elif bank == 7:
                after(pe, Bp.y, blocks(i + LB))
                if isinstance(i, int):
                    after(pe, a_yc, blocks(i + LQ))

        def a_keys_pe(pe, b, steps):
            for i in steps:
                if i < 2:
                    a_bank_pe(pe, b - LK, 5 + i)
                if i == 0:
                    pe.wait_ge(a_cats, 2 * b + 1)
                if i < TPB:
                    if i >= 2:
                        pe.wait_ge(a_ek, TPB * b + i - 1)
                    for h in range(2):
                        ins = pe.matmul(banks[5 + i % 2][:, h * HH * M:(h + 1) * HH * M],
                                        cat_k[:, h, i * P:(i + 1) * P], feat[:, h, :, :], start=True, stop=True)
                    ins.then_inc(a_fk, 1)
                if i >= 2:
                    a_state_pe(pe, b, i - 2)
            if TPB in steps:
                a_state_pe(pe, b, TPB - 1)

        def a_state_pe(pe, b, i):
            if i == 0:
                a_bank_pe(pe, b - LK, 7)
                pe.wait_ge(a_v, b + 1)
            pe.wait_ge(a_ek, TPB * b + i + 1)
            for g in range(NG):
                ins = pe.matmul(banks[7][:, g * GH * VW:(g + 1) * GH * VW],
                                kphi[:, i % 2, g * P:(g + 1) * P], vals[:, i, g * GH:(g + 1) * GH, :],
                                start=(i == 0 and g == 0), stop=True, skip_group_check=True)
            ins.then_inc(a_s, 1)

        def a_query_pe(pe, b, par, steps):
            def features(g):
                if g == 0:
                    pe.wait_ge(a_cats, 2 * b + 2)
                if g < 2:
                    after(pe, a_ek, TPB * blocks(b - LQ + LK + 1))
                else:
                    pe.wait_ge(a_eq, NG * b + g - 1)
                pe.matmul(banks[5 + g % 2][:, :], feat[:, g // 2, (g % 2) * GH:(g % 2 + 1) * GH, :],
                          cat_q[:, par, g // 2, :], start=True, stop=True).then_inc(a_fq, 1)

            def outputs(g):
                pe.wait_ge(a_eq, NG * b + g + 1)
                if g == 0:
                    pe.wait_ge(a_state, blocks(b + 2))
                elif g == 2:
                    after(pe, x_cw, blocks(b - LQ + 1))
                    if isinstance(b, int):
                        after(pe, a_v, blocks(b - LQ + LF))
                        after(pe, Bp.xt, blocks(b - LQ + LB + 1))
                        after(pe, C.xt, blocks(b - LQ + LC + 1))
                bank = banks[7] if g < 2 else banks[0]
                for i in range(TPB):
                    c = i * OW + g % 2 * GH * VW
                    ins = pe.matmul(bank[:, c:c + GH * VW], qphi[:, g % 2, i * P:(i + 1) * P], sbd[:, g, :, :],
                                    start=True, stop=True)
                ins.then_inc(a_o, 1)

            for g in steps:
                if isinstance(b, int) and b - LQ + LK >= NB:
                    if g < 2:
                        a_bank_pe(pe, b - LQ, 5 + g)
                    if g == 1:
                        a_bank_pe(pe, b - LQ, 7)
                if g < NG:
                    features(g)
                if g >= 1:
                    outputs(g - 1)

        def a_back_pe(pe, b):
            pe.wait_ge(a_on, 2 * b + 2)
            for i in range(TPB):
                ins = pe.transpose(banks[0][:, i * P:(i + 1) * P],
                                   o_sb[:, i, :, :].rearrange("p h d -> p (h d)"), ident)
            ins.then_inc(a_ot, 1)

        def a_out_pe(pe, b):
            pe.wait_ge(a_ots, b + 1)
            if first(b):
                pe.wait_ge(l_attn, 4 * 16)
            for i in range(TPB):
                ins = pe.matmul(banks[7][:, i * P:(i + 1) * P], ot_sb[:, i * P:(i + 1) * P], wout_sb[:, :],
                                start=True, stop=True)
            ins.then_inc(A.y, 1)

        def a_cat_dve(dve, b, par, n):
            pos = par * TB
            if first(b) and n == 0:
                dve.wait_ge(l_rope, 16)
            dve.wait_ge(a_q, 2 * b + n + 1)
            after(dve, a_catr, 2 * b + n)
            plain, swapped = a_banks(b)[1 + n]
            dve.tensor_tensor(rot[:, 0, :], plain[:, :], cst[:, C_COS + pos:C_COS + pos + TB],
                              ALU.mult).then_inc(a_rot, 1)
            dve.wait_ge(a_qs, 2 * b + n + 1)
            dve.tensor_tensor(rot[:, 1, :], swapped[:, :], cst[:, C_SIN + pos:C_SIN + pos + TB],
                              ALU.mult).then_inc(a_rot, 1)
            dve.wait_ge(a_rot, 4 * b + 2 * n + 2)
            if n == 1:
                after(dve, a_fq, NG * (b - 1))
            else:
                after(dve, a_fk, TPB * b)
            for h in range(2):
                dst = cat_q[0:PP, par, h, :] if n else cat_k[0:PP, h, :]
                ins = dve.tensor_tensor(dst, rot[h * PP:(h + 1) * PP, 0, :], rot[h * PP:(h + 1) * PP, 1, :],
                                        ALU.add)
            ins.then_inc(a_catr, 1)

        def a_state_dve(dve, b, par):
            dve.wait_ge(a_s, TPB * (b + 1))
            if par == 0:
                dve.tensor_copy(s_even[:, :], banks[7][:, 0:H * VW]).then_inc(a_state, 1)
                return
            dve.wait_ge(a_state, b)
            dve.tensor_tensor(s_all[:, :], banks[7][:, 0:H * VW], s_even[:, :], ALU.add).then_inc(a_sum, 2)
            dve.wait_ge(a_sum, b + 1)
            after(dve, a_o, NG * (b - 1))
            dve.tensor_tensor(sbd[:, :, :, :], s_all[:, :].rearrange("p (g h v) -> p g h v", g=NG, h=GH),
                              cst[:, C_M4:C_M4 + GH].unsqueeze(1).unsqueeze(3).broadcast_to([P, NG, GH, VW]),
                              ALU.mult).then_inc(a_state, 1)

        def a_divide_dve(dve, b, n):
            v = banks[0 if n else 7][:, 0:TPB * OW].rearrange("p (t h v) -> p t h v", t=TPB, h=HH)
            dve.wait_ge(a_o, NG * b + 2 * n + 2)
            dve.tensor_scalar(den[:, n, :, :], v[:, :, :, DH], DEN_EPS, None, ALU.max).then_inc(a_den, 1)
            dve.wait_ge(a_den, 4 * b + 2 * n + 1)
            dve.reciprocal(rden[:, n, :, :], den[:, n, :, :]).then_inc(a_den, 1)
            dve.wait_ge(a_den, 4 * b + 2 * n + 2)
            after(dve, a_ot, b)
            dve.tensor_tensor(o_sb[:, :, n * HH:(n + 1) * HH, :], v[:, :, :, 0:DH],
                              rden[:, n, :, :].unsqueeze(3).broadcast_to([P, TPB, HH, DH]),
                              ALU.mult).then_inc(a_on, 1)

        def a_xt_act(act, b):
            act.wait_ge(A.tr, b + 1)
            after(act, a_vp, b)
            act.activation(xta[:, :], a_banks(b)[0][:, :], ACT.Copy).then_inc(A.xt, 1)

        def a_squares_q_act(act, b, par):
            act.wait_ge(a_catr, 2 * b + 2)
            for h in range(2):
                ins = act.activation(cat_q[PP:P, par, h, :], cat_q[0:PP, par, h, :], ACT.Square)
            ins.then_inc(a_cats, 1)

        def a_squares_k_act(act, b):
            act.wait_ge(a_catr, 2 * b + 1)
            for h in range(2):
                ins = act.activation(cat_k[PP:P, h, :], cat_k[0:PP, h, :], ACT.Square)
            ins.then_inc(a_cats, 1)

        def a_values_act(act, b):
            act.wait_ge(a_vp, b + 1)
            after(act, a_s, TPB * b)
            act.activation(vals[:, :, :, 0:DH].rearrange("p t h v -> p (t h) v"),
                           a_banks(b)[3][:, :].rearrange("p (t h v) -> p (t h) v", t=TPB, h=H),
                           ACT.Copy).then_inc(a_v, 1)

        def a_keys_act(act, b, tiles):
            for i in tiles:
                act.wait_ge(a_fk, TPB * b + i + 1)
                after(act, a_s, TPB * b + i - 1)
                act.activation(kphi[:, i % 2, :], banks[5 + i % 2][:, :], ACT.Exp).then_inc(a_ek, 1)

        def a_query_act(act, b, groups):
            for g in groups:
                act.wait_ge(a_fq, NG * b + g + 1)
                after(act, a_o, NG * b + g - 1)
                act.activation(qphi[:, g % 2, :], banks[5 + g % 2][:, :], ACT.Exp).then_inc(a_eq, 1)

        def a_back_act(act, b):
            act.wait_ge(a_ot, b + 1)
            after(act, A.y, b)
            act.activation(ot_sb[:, :], banks[0][:, :], ACT.Copy).then_inc(a_ots, 1)

        def a_y_act(act, b):
            act.wait_ge(A.y, b + 1)
            after(act, A.tmp, b)
            act.activation(ya[:, :], banks[7][:, :], ACT.Copy).then_inc(a_yc, 1)

        def b_front_pe(pe, b):
            after(pe, r_sub, 2 * blocks(b - LB + LR))
            if isinstance(b, int):
                after(pe, a_v, blocks(b - LB + LF))
                if b == 0:
                    pe.wait_ge(l_mix, 4 * 16)
            transpose(pe, Bp, b, xnb)

        def c_front_pe(pe, b):
            after(pe, Bp.xt, blocks(b - LC + LB + 1))
            if isinstance(b, int):
                after(pe, r_sub, 2 * blocks(b - LC + LR))
                if b == 0:
                    pe.wait_ge(l_rec, 5 * 16)
            transpose(pe, C, b, xnc)

        def r_front_pe(pe, b):
            after(pe, A.xt, blocks(b - LR + LF + 1))
            if isinstance(b, int):
                after(pe, a_ots, blocks(b - LR + LQ + 1))
                after(pe, x_cw, blocks(b - LR + 1))
                after(pe, Bp.xt, blocks(b - LR + LB + 1))
                after(pe, C.xt, blocks(b - LR + LC + 1))
            transpose(pe, R, b, xnr)

        xnb = sb("xnb", [P, TPB, D])
        xs = sb("xs", [P, 2, TB + 1])
        dx = sb("dx", [P, TB])
        xr, xk = sb("xr", [P, TB]), sb("xk", [P, TB])
        kact = sb("kact", [P, TB])
        rgate = sb("rgate", [P, TB])
        yb = sb("yb", [P, TB])
        tmpb = sb("tmpb", [P, TB])
        b_x0 = sem("b_x0")
        b_zero = sem("b_zero")
        b_dx, b_xr, b_xk = sem("b_dx"), sem("b_xr"), sem("b_xk")
        b_k, b_r, b_v = sem("b_k"), sem("b_r"), sem("b_v")
        b_kr, b_ka, b_rg = sem("b_kr"), sem("b_ka"), sem("b_rg")

        def b_stats_dve(dve, b, par):
            dve.wait_ge(A.xa, b + 1)
            dve.nop().then_inc(d_seen, 1)
            stats(dve, nb, b, par, lambda i: tile(xres, b, i), Bp.bn, Bp.mv)

        def b_shift_act(act, b, par):
            act.wait_ge(Bp.tr, b + 1)
            after(act, b_xk, b - 1)
            act.activation(xs[:, par, 1:TB + 1], banks[0][:, :], ACT.Copy).then_inc(Bp.xt, 1)
            if par:
                act.wait_ge(Bp.xt, b)
                act.activation(xs[:, 1, 0:1], xs[:, 0, TB:TB + 1], ACT.Copy).then_inc(b_x0, 2)

        def b_mix_dve(dve, b, par):
            dve.wait_ge(Bp.xt, b + 1)
            if par:
                dve.wait_ge(b_x0, b + 1)
            after(dve, b_xk, b)
            dve.tensor_tensor(dx[:, :], xs[:, par, 1:TB + 1], xs[:, par, 0:TB], ALU.subtract).then_inc(b_dx, 1)
            dve.wait_ge(b_dx, b + 1)
            after(dve, b_r, b)
            after(dve, b_k, b)
            dve.scalar_tensor_tensor(out=xr[:, :], in0=dx[:, :], scalar=mu_sb[:, 0:1],
                                     in1=xs[:, par, 0:TB], op0=ALU.mult, op1=ALU.add).then_inc(b_xr, 1)
            dve.scalar_tensor_tensor(out=xk[:, :], in0=dx[:, :], scalar=mu_sb[:, 1:2],
                                     in1=xs[:, par, 0:TB], op0=ALU.mult, op1=ALU.add).then_inc(b_xk, 1)

        def b_in_pe(pe, b):
            pe.wait_ge(b_xr, b + 1)
            after(pe, a_yc, blocks(b - LB + LQ + 1))
            for i in range(TPB):
                ins = pe.matmul(banks[7][:, i * P:(i + 1) * P], xr[:, i * P:(i + 1) * P], wr_sb[:, :],
                                start=True, stop=True)
            ins.then_inc(b_r, 1)

        def b_key_pe(pe, b):
            pe.wait_ge(b_xk, b + 1)
            pe.matmul(banks[5][:, :], wk_sb[:, :], xk[:, :], start=True, stop=True).then_inc(b_k, 1)

        def b_value_pe(pe, b):
            pe.wait_ge(b_ka, b + 1)
            pe.wait_ge(b_rg, b + 1)
            for i in range(TPB):
                ins = pe.matmul(banks[7][:, i * P:(i + 1) * P], kact[:, i * P:(i + 1) * P], wv_sb[:, :],
                                start=True, stop=True)
            ins.then_inc(b_v, 1)

        def b_gate_act(act, b):
            act.wait_ge(b_r, b + 1)
            after(act, Bp.y, b)
            act.activation(rgate[:, :], banks[7][:, :], ACT.Tanh, scale=0.5).then_inc(b_rg, 1)

        def b_key_act(act, b):
            act.wait_ge(b_k, b + 1)
            after(act, b_v, b)
            act.activation(kact[:, :], banks[5][:, :], ACT.Relu).then_inc(b_kr, 1)
            act.wait_ge(b_kr, b + 1)
            act.activation(kact[:, :], kact[:, :], ACT.Square).then_inc(b_ka, 1)

        def b_gate_dve(dve, b, par):
            dve.wait_ge(b_rg, b + 1)
            dve.wait_ge(b_v, b + 1)
            after(dve, Bp.tmp, b)
            dve.scalar_tensor_tensor(out=yb[:, :], in0=rgate[:, :], scalar=1.0, in1=banks[7][:, :],
                                     op0=ALU.add, op1=ALU.mult).then_inc(Bp.y, 1)
            dve.wait_ge(Bp.y, b + 1)
            stats(dve, nyb, b, par, lambda i: yb[:, i * P:(i + 1) * P], Bp.ybn, Bp.ymv)

        xnc = sb("xnc", [P, TPB, D])
        ut = sb("ut", [P, TB])
        lam, bu, hs = sb("lam", [NS, TB]), sb("bu", [NS, TB]), sb("hs", [NS, 2, TB])
        ud = sb("ud", [P, TPB, D])
        yc = sb("yc", [P, TB])
        tmpc = sb("tmpc", [P, TB])
        c_lb = sem("c_lb")
        c_bu = sem("c_bu")
        c_lam, c_h = sem("c_lam"), sem("c_h")
        c_th = sem("c_th")
        c_ud = sem("c_ud")
        c_yc = sem("c_yc")

        def c_stats_dve(dve, b, par):
            dve.wait_ge(Bp.xa, b + 1)
            dve.nop().then_inc(d_seen, 1)
            stats(dve, ncx, b, par, lambda i: tile(xres, b, i), C.bn, C.mv)

        def c_front_act(act, b):
            act.wait_ge(C.tr, b + 1)
            after(act, C.y, b)
            act.activation(ut[:, :], banks[0][:, :], ACT.Copy).then_inc(C.xt, 1)

        def c_in_pe(pe, b):
            pe.wait_ge(C.xt, b + 1)
            pe.matmul(banks[6][0:2 * NS, :], wlb_sb[:, :], ut[:, :], start=True, stop=True).then_inc(c_lb, 1)

        def c_gates_act(act, b):
            act.wait_ge(c_lb, b + 1)
            after(act, c_lam, b)
            after(act, c_h, b)
            act.activation(bu[:, :], banks[6][NS:2 * NS, :], ACT.Copy).then_inc(c_bu, 1)
            if first(b):
                act.wait_ge(s_blh, 1)
            act.activation(lam[:, :], banks[6][0:NS, :], ACT.Tanh, bias=blh_sb[:, 0:1], scale=0.5).then_inc(c_th, 1)

        def c_scan_dve(dve, b, par):
            dve.wait_ge(c_th, b + 1)
            dve.tensor_scalar(lam[:, :], lam[:, :], 0.5, 0.5, ALU.mult, ALU.add).then_inc(c_lam, 1)
            dve.wait_ge(c_lam, b + 1)
            dve.wait_ge(c_bu, b + 1)
            after(dve, C.y, b - 1)
            if par:
                dve.wait_ge(c_h, b)
            dve.tensor_tensor_scan(hs[:, par, :], lam[:, :], bu[:, :],
                                   hs[:, 0, TB - 1:TB] if par else 0.0, ALU.mult, ALU.add).then_inc(c_h, 1)

        def c_out_pe(pe, b, par):
            pe.wait_ge(c_h, b + 1)
            after(pe, a_rot, a_rotated(b - LC))
            for i in range(TPB):
                y = banks[6][:, i * P:(i + 1) * P]
                ins = pe.matmul(y, hs[:, par, i * P:(i + 1) * P], wc_sb[:, :], start=True, stop=True)
            ins.then_inc(C.y, 1)

        def c_skip_pool(pool, b):
            pool.wait_ge(C.xn, b + 1)
            if first(b):
                pool.wait_ge(l_rec, 5 * 16)
            after(pool, c_yc, b)
            pool.tensor_tensor(ud[:, :, :], xnc[:, :, :], dp_sb[:, :].unsqueeze(1).broadcast_to([P, TPB, D]),
                               ALU.mult).then_inc(c_ud, 1)

        def c_y_dve(dve, b):
            dve.wait_ge(c_ud, b + 1)
            dve.wait_ge(C.y, b + 1)
            after(dve, C.tmp, b)
            dve.tensor_tensor(yc[:, :], banks[6][:, :], ud[:, :, :].rearrange("p t d -> p (t d)"),
                              ALU.add).then_inc(c_yc, 1)

        def c_ystats_dve(dve, b, par):
            dve.wait_ge(c_yc, b + 1)
            stats(dve, nyc, b, par, lambda i: yc[:, i * P:(i + 1) * P], C.ybn, C.ymv)

        xnr = sb("xnr", [P, TPB, D])
        xh, xl = sb("xh", [P, 2, TB], F32R), sb("xl", [P, 2, TB], F32R)
        ew = sb("ew", [P, TPB, E])
        mk = sb("mk", [P, TPB, E])
        top8 = sb("top8", [P, TPB, 8])
        low = sb("low", [P, 8, TPB])
        cexp = sb("cexp", [P, TPB, E, EQ])
        cw = sb("cw", [P, 2, TB])
        r_xh, r_xl = sem("r_xh"), sem("r_xl")
        r_lg = sem("r_lg")
        r_sub, r_exp = sem("r_sub"), sem("r_exp")
        r_step = sem("r_step")
        x_cexp, x_ct, x_cw = sem("x_cexp"), sem("x_ct"), sem("x_cw")

        def r_stats_dve(dve, b, par):
            dve.wait_ge(C.xa, b + 1)
            dve.nop().then_inc(d_seen, 1)
            stats(dve, nr, b, par, lambda i: tile(xres, b, i), R.bn, R.mv)

        def r_hi_act(act, b, par):
            act.wait_ge(R.tr, b + 1)
            after(act, x_u, NJ * (b - 1))
            act.activation(xh[:, par, :], banks[0][:, :], ACT.Copy).then_inc(r_xh, 1)

        def r_lo_dve(dve, b, par):
            dve.wait_ge(r_xh, b + 1)
            after(dve, x_u, NJ * (b - 1))
            dve.tensor_tensor(xl[:, par, :], banks[0][:, :], xh[:, par, :].bitcast(F32),
                              ALU.subtract).then_inc(r_xl, 1)

        def r_logits_pe(pe, b, par):
            pe.wait_ge(r_xl, b + 1)
            if first(b):
                pe.wait_ge(s_wsplit, 6)
            if not early(b, 0):
                after(pe, a_v, blocks(b - LR + LF + 1))
            for i in range(TPB):
                c = slice(i * P, (i + 1) * P)
                y = banks[0][:, i * E:(i + 1) * E]
                pe.matmul(y, xl[:, par, c], gate_hi[:, :], start=True, stop=False)
                pe.matmul(y, xh[:, par, c], gate_lo[:, :], start=False, stop=False)
                ins = pe.matmul(y, xh[:, par, c], gate_hi[:, :], start=False, stop=True)
            ins.then_inc(r_lg, 1)

        def wide(v):
            return v.unsqueeze(2).broadcast_to([P, TPB, E])

        def r_scores_dve(dve, b):
            dve.wait_ge(r_lg, b + 1)
            lg = banks[0][:, 0:TPB * E].rearrange("p (t e) -> p t e", t=TPB)
            dve.tensor_reduce(low[:, 0, :], lg, mybir.AxisListType.X, ALU.max).then_inc(r_sub, 1)
            dve.wait_ge(r_sub, 2 * b + 1)
            dve.tensor_tensor(ew[:, :, :], lg, wide(low[:, 0, :]), ALU.subtract).then_inc(r_sub, 1)

        def r_exp_act(act, b):
            act.wait_ge(r_sub, 2 * b + 2)
            act.activation(ew[:, :, :], ew[:, :, :], ACT.Exp).then_inc(r_exp, 1)

        def r_top_dve(dve, b):
            dve.wait_ge(r_exp, b + 1)
            dve.tensor_reduce(low[:, 1, :], ew[:, :, :], mybir.AxisListType.X, ALU.add).then_inc(r_step, 1)
            for t in range(TPB):
                ins = dve.max(top8[:, t, :], ew[:, t, :])
            ins.then_inc(r_step, 1)
            dve.wait_ge(r_step, 10 * b + 2)
            dve.tensor_tensor(low[:, 3, :], top8[:, :, 0], top8[:, :, 1], ALU.add).then_inc(r_step, 1)
            dve.reciprocal(low[:, 2, :], low[:, 1, :]).then_inc(r_step, 1)
            dve.wait_ge(r_step, 10 * b + 3)
            dve.tensor_scalar(top8[:, :, 2:8], top8[:, :, 2:8], 0.0, -1.0, ALU.mult, ALU.add).then_inc(r_step, 1)
            dve.wait_ge(r_step, 10 * b + 5)
            dve.tensor_tensor(low[:, 4, :], low[:, 3, :], low[:, 2, :], ALU.mult)
            for t in range(TPB):
                ins = dve.match_replace(mk[:, t, :], top8[:, t, :], ew[:, t, :], -2.0)
            ins.then_inc(r_step, 1)
            dve.wait_ge(r_step, 10 * b + 6)
            dve.tensor_scalar(low[:, 5, :], low[:, 4, :], TOP_EPS, None, ALU.add).then_inc(r_step, 1)
            dve.scalar_tensor_tensor(out=mk[:, :, :], in0=mk[:, :, :], scalar=-2.0, in1=ew[:, :, :],
                                     op0=ALU.is_equal, op1=ALU.mult).then_inc(r_step, 1)
            dve.wait_ge(r_step, 10 * b + 7)
            dve.reciprocal(low[:, 6, :], low[:, 5, :]).then_inc(r_step, 1)
            dve.wait_ge(r_step, 10 * b + 9)
            dve.scalar_tensor_tensor(out=low[:, 7, :], in0=low[:, 6, :], scalar=ROUTE_SCALE, in1=low[:, 2, :],
                                     op0=ALU.mult, op1=ALU.mult).then_inc(r_step, 1)
            dve.wait_ge(r_step, 10 * b + 10)
            after(dve, x_ct, b)
            for t in range(TPB):
                ins = dve.tensor_scalar(cexp[:, t, :, :], mk[:, t, :].unsqueeze(2).broadcast_to([P, E, EQ]),
                                        low[:, 7, t:t + 1], None, ALU.mult)
            ins.then_inc(x_cexp, 1)

        def r_weights_pe(pe, b):
            pe.wait_ge(x_cexp, b + 1)
            after(pe, C.xt, blocks(b + LC + 1))
            for i in range(TPB):
                ins = pe.transpose(banks[0][:, i * P:(i + 1) * P],
                                   cexp[:, i, :, :].rearrange("p e q -> p (e q)"), ident)
            ins.then_inc(x_ct, 1)

        def r_weights_act(act, b, par):
            act.wait_ge(x_ct, b + 1)
            after(act, x_gc, JE * (b - 1))
            act.activation(cw[:, par, :], banks[0][:, :], ACT.Copy).then_inc(x_cw, 1)

        ORDER = list(range(JE, NJ)) + list(range(JE))
        LAG = 2
        sil = sb("sil", [P, 2, TB])
        gu = sb("gu", [P, 2, TB])
        gc = wstage[:, 0:3 * TB].rearrange("p (k t) -> p k t", k=3)
        yx = sb("yx", [P, TB])
        tmpx = sb("tmpx", [P, TB])
        x_g, x_u, x_sil, x_gu = sem("x_g"), sem("x_u"), sem("x_sil"), sem("x_gu")
        x_gc = sem("x_gc")
        x_d = sem("x_d")
        x_y = sem("x_yc")

        def gate_bank(k):
            return banks[1 + 2 * k % 3]

        def up_bank(k):
            return banks[1 + (2 * k + 1) % 3]

        def x_hidden_pe(pe, b, par, k):
            j = ORDER[k]
            m, c = rows(j), slice(j * P, j * P + rows(j))
            n = NJ * b + k
            if k == 0:
                pe.wait_ge(r_xl, b + 1)
                if first(b):
                    pe.wait_ge(l_down, 2 * 16)
                    pe.wait_ge(s_wsplit, 6)
                    pe.wait_ge(a_rot, 4 * LF)
                    pe.wait_ge(a_v, LF)
            after(pe, x_gu, n - 1 if k else n)
            if k == 1:
                after(pe, x_sil, n - 1)
            pe.matmul(gate_bank(k)[0:m, :], wg_lo[:, c], xh[:, par, :], start=True, stop=False)
            pe.matmul(gate_bank(k)[0:m, :], wg_hi[:, c], xl[:, par, :], start=False, stop=False)
            pe.matmul(gate_bank(k)[0:m, :], wg_hi[:, c], xh[:, par, :], start=False, stop=True).then_inc(x_g, 1)
            if k:
                pe.wait_ge(x_sil, n)
            pe.matmul(up_bank(k)[0:m, :], wu_lo[:, c], xh[:, par, :], start=True, stop=False)
            pe.matmul(up_bank(k)[0:m, :], wu_hi[:, c], xl[:, par, :], start=False, stop=False)
            pe.matmul(up_bank(k)[0:m, :], wu_hi[:, c], xh[:, par, :], start=False, stop=True).then_inc(x_u, 1)

        def x_down_pe(pe, b, k):
            j = ORDER[k]
            if j < JE:
                pe.wait_ge(x_gc, JE * b + j + 1)
            else:
                pe.wait_ge(x_gu, NJ * b + k + 1)
            if k == 0:
                after(pe, x_y, b)
            m = rows(j)
            src = gc[0:m, k % 3, :]
            for i in range(TPB):
                ins = pe.matmul(banks[4][:, i * P:(i + 1) * P], src[:, i * P:(i + 1) * P], wd_sb[0:m, j, :],
                                start=(k == 0 and i == 0), stop=True, skip_group_check=True)
            ins.then_inc(x_d, 1)

        def x_chunk_pe(pe, b, par, k):
            x_hidden_pe(pe, b, par, k)
            if k >= LAG:
                x_down_pe(pe, b, k - LAG)

        def x_tail_pe(pe, b):
            for k in range(NJ - LAG, NJ):
                x_down_pe(pe, b, k)

        def silu_table(act):
            act.activation(warm[:, :], mhalf[:, 0:1], ACT.Silu)

        def x_chunk_act(act, b, k):
            m = rows(ORDER[k])
            act.wait_ge(x_g, NJ * b + k + 1)
            after(act, x_gu, NJ * b + k - 1)
            act.activation(sil[0:m, k % 2, :], gate_bank(k)[0:m, :], ACT.Silu).then_inc(x_sil, 1)

        def x_chunk_dve(dve, b, k):
            j = ORDER[k]
            m = rows(j)
            dve.wait_ge(x_u, NJ * b + k + 1)
            dve.wait_ge(x_sil, NJ * b + k + 1)
            if j < JE:
                after(dve, x_gc, JE * b + j - 1 if j >= 2 else JE * b)
                dst = gu[0:m, j % 2, :]
            else:
                if first(b):
                    dve.wait_ge(s_wsplit, 4)
                after(dve, x_d, NJ * b)
                dst = gc[0:m, k, :]
            dve.tensor_tensor(dst, up_bank(k)[0:m, :], sil[0:m, k % 2, :], ALU.mult).then_inc(x_gu, 1)

        def x_chunk_pool(pool, b, par, k):
            j = ORDER[k]
            if j >= JE:
                return
            if j == 0:
                pool.wait_ge(x_cw, b + 1)
            pool.wait_ge(x_gu, NJ * b + k + 1)
            after(pool, x_d, NJ * b + k - 2)
            pool.tensor_tensor(gc[:, k % 3, :], gu[:, j % 2, :], cw[:, par, :], ALU.mult).then_inc(x_gc, 1)

        def x_y_act(act, b):
            act.wait_ge(x_d, NJ * (b + 1))
            after(act, X.tmp, b)
            act.activation(yx[:, :], banks[4][:, :], ACT.Copy).then_inc(x_y, 1)

        def x_ystats_dve(dve, b, par):
            dve.wait_ge(x_y, b + 1)
            stats(dve, nx, b, par, lambda i: yx[:, i * P:(i + 1) * P], X.ybn, X.ymv)

        def together(eng, iteration):
            start, stop = 2, (NB - LF) // 2 * 2
            for i in range(-LF, start):
                iteration(i, i % 2)
            with eng.Fori(start // 2, stop // 2) as s:
                iteration(s * 2, 0)
                iteration(s * 2 + 1, 1)
            for i in range(stop, NB + 1):
                iteration(i, i % 2)

        block = ctx.enter_context(nc.Block())

        @block.sync
        def _(sp):
            def load_x(b0, b1, done):
                sp.dma_start(xres[:, b0 * TB:b1 * TB].rearrange("p (c t d) -> p (c t) d", c=b1 - b0, t=TPB),
                             x[b0:b1].rearrange("c (t p) d -> p (c t) d", p=P)).then_inc(done, 16)

            load_x(0, 1, l_x[0])
            sp.dma_start(cst[:, 0:C_COS], consts[:, 0:C_COS]).then_inc(l_consts, 16)
            sp.dma_start(wqkv_sb[:, :], wqkv).then_inc(l_consts, 16)
            sp.dma_start(cst[:, C_COS:C_N], consts[:, C_COS:C_N]).then_inc(l_rope, 16)
            sp.dma_start(s23_sb[:, :, :], s23).then_inc(l_attn, 16)
            sp.dma_start(s1_sb[:, :], s1c).then_inc(l_attn, 16)
            sp.dma_start(scl_sb[:, :, :], scl).then_inc(l_attn, 16)
            load_x(1, 2, l_x[1])
            sp.dma_start(wout_sb[:, :], wout).then_inc(l_attn, 16)
            load_x(2, NB, l_x[2])
            for dst, src in ((wr_sb, wr), (wk_sb, wk), (wv_sb, wv), (mu_sb, mu)):
                sp.dma_start(dst[:, :], src).then_inc(l_mix, 16)
            for dst, src in ((wlb_sb, wlb), (bl_sb, bl), (wc_sb, wc), (dp_sb, dp), (gate_sb, gate)):
                sp.dma_start(dst[:, :], src).then_inc(l_rec, 16)
            sp.dma_start(wstage[:, :], wg).then_inc(l_gate, 16)
            sp.dma_start(wd_sb[:, 0:NJ - 1, :],
                         wd[0:(NJ - 1) * P, :].rearrange("(j p) d -> p j d", p=P)).then_inc(l_down, 16)
            sp.dma_start(wd_sb[0:LAST, NJ - 1, :], wd[(NJ - 1) * P:HF, :]).then_inc(l_down, 16)
            sp.wait_ge(s_wsplit, 2)
            sp.dma_start(wstage[:, :], wu).then_inc(l_up, 16)
            with sp.Fori(0, NB) as b:
                sp.wait_ge(X.xa, b + 1)
                sp.dma_start(out[bass.ds(b, 1), :, :].rearrange("c (t p) d -> p (c t) d", p=P),
                             blk(xres, b).rearrange("p (t d) -> p t d", t=TPB)).then_inc(s_out, 16)
            sp.wait_ge(s_out, 16 * NB)

        @block.gpsimd
        def _(pool):
            pool.memset(mhalf[:, :], -0.5).then_inc(s_prep, 1)
            pool.memset(vals[:, :, :, DH:VW], 1.0).then_inc(a_ones, 1)
            pool.wait_ge(s_prep, 1)
            pool.memset(xs[:, 0, 0:1], 0.0).then_inc(b_zero, 1)

            def iteration(i, par):
                odd, (out_b, x_b, route_b, rec_b, mix_b, query_b, key_b, front_b) = 1 - par, lags(i)
                if has(front_b) and early(front_b, LF - LQ):
                    root(pool, A.mv, A.rs, na.m, na.r, na.n, front_b, par)
                if has(mix_b) and not early(mix_b, LB):
                    root(pool, Bp.mv, Bp.rs, nb.m, nb.r, nb.n, mix_b, odd)
                if has(rec_b):
                    root(pool, C.mv, C.rs, ncx.m, ncx.r, ncx.n, rec_b, par)
                if has(front_b) and not early(front_b, LF - LQ):
                    root(pool, A.mv, A.rs, na.m, na.r, na.n, front_b, par)
                if has(x_b):
                    x_chunk_pool(pool, x_b, par, 0)
                if has(route_b):
                    root(pool, R.mv, R.rs, nr.m, nr.r, nr.n, route_b, odd)
                if has(x_b):
                    x_chunk_pool(pool, x_b, par, 1)
                if has(rec_b):
                    c_skip_pool(pool, rec_b)
                if has(x_b):
                    x_chunk_pool(pool, x_b, par, 2)
                if has(out_b):
                    root(pool, X.ymv, X.yrs, nx.m, nx.r, nx.n, out_b, odd)
                if has(x_b):
                    x_chunk_pool(pool, x_b, par, 3)
                if has(query_b):
                    root(pool, A.ymv, A.yrs, nya.m, nya.r, nya.n, query_b, par)
                if has(x_b):
                    x_chunk_pool(pool, x_b, par, 4)
                if has(out_b):
                    add_residual(pool, X, out_b, tmpx)
                if has(x_b):
                    x_chunk_pool(pool, x_b, par, 5)
                if has(query_b):
                    add_residual(pool, A, query_b, tmpa)
                if has(x_b):
                    x_chunk_pool(pool, x_b, par, 6)
                if has(x_b):
                    x_chunk_pool(pool, x_b, par, 7)
                if has(mix_b):
                    root(pool, Bp.ymv, Bp.yrs, nyb.m, nyb.r, nyb.n, mix_b, odd, 4 * LN_EPS)
                if has(x_b):
                    x_chunk_pool(pool, x_b, par, 8)
                if has(rec_b):
                    root(pool, C.ymv, C.yrs, nyc.m, nyc.r, nyc.n, rec_b, par)
                if has(query_b) and early(query_b, LB):
                    root(pool, Bp.mv, Bp.rs, nb.m, nb.r, nb.n, query_b, par)
                if has(x_b):
                    x_chunk_pool(pool, x_b, par, 9)
                if has(mix_b):
                    add_residual(pool, Bp, mix_b, tmpb)
                if has(x_b):
                    x_chunk_pool(pool, x_b, par, 10)
                if has(rec_b):
                    add_residual(pool, C, rec_b, tmpc)
                if has(x_b):
                    for k in range(11, NJ):
                        x_chunk_pool(pool, x_b, par, k)

            together(pool, iteration)

        @block.scalar
        def _(act):
            act.wait_ge(s_prep, 1)
            act.wait_ge(a_ones, 1)

            def iteration(i, par):
                odd, (out_b, x_b, route_b, rec_b, mix_b, query_b, key_b, front_b) = 1 - par, lags(i)
                if has(x_b):
                    r_exp_act(act, x_b)
                if has(key_b):
                    a_keys_act(act, key_b, range(2 if early(key_b, LK) else 0, TPB))
                if has(mix_b) and not late(i):
                    b_shift_act(act, mix_b, odd)
                if has(query_b):
                    a_query_act(act, query_b, range(0, 1))
                if has(rec_b) and not late(i):
                    c_front_act(act, rec_b)
                if has(query_b):
                    a_query_act(act, query_b, range(1, 3))
                if has(x_b) and not late(i):
                    r_weights_act(act, x_b, par)
                if has(query_b):
                    a_query_act(act, query_b, range(3, NG))
                if has(x_b):
                    silu_table(act)
                if has(x_b):
                    x_chunk_act(act, x_b, 0)
                if has(out_b):
                    x_y_act(act, out_b)
                if has(mix_b) and not late(i):
                    b_key_act(act, mix_b)
                if has(rec_b) and not late(i):
                    c_gates_act(act, rec_b)
                if has(mix_b) and late(i):
                    b_shift_act(act, mix_b, odd)
                if has(front_b) and early(front_b, LF - 1):
                    a_xt_act(act, front_b)
                if has(x_b):
                    x_chunk_act(act, x_b, 1)
                if has(rec_b) and late(i):
                    c_front_act(act, rec_b)
                if has(x_b) and late(i):
                    r_weights_act(act, x_b, par)
                if has(query_b):
                    a_back_act(act, query_b)
                if has(x_b):
                    x_chunk_act(act, x_b, 2)
                if has(front_b) and not early(front_b, LF - 1):
                    a_xt_act(act, front_b)
                if has(mix_b) and late(i):
                    b_key_act(act, mix_b)
                if has(rec_b) and late(i):
                    c_gates_act(act, rec_b)
                if has(x_b):
                    x_chunk_act(act, x_b, 3)
                if has(query_b):
                    a_y_act(act, query_b)
                if has(out_b):
                    apply(act, X, nx, out_b, odd, yx, tmpx)
                if has(x_b):
                    x_chunk_act(act, x_b, 4)
                if has(mix_b) and early(mix_b, LB - 1):
                    b_gate_act(act, mix_b)
                if has(front_b):
                    a_squares_k_act(act, front_b)
                if has(x_b):
                    x_chunk_act(act, x_b, 5)
                if has(front_b) and early(front_b, LF - 1):
                    a_values_act(act, front_b)
                if has(route_b):
                    r_hi_act(act, route_b, odd)
                if has(mix_b) and not early(mix_b, LB - 1):
                    b_gate_act(act, mix_b)
                if has(query_b):
                    apply(act, A, nya, query_b, par, ya, tmpa)
                if has(x_b):
                    x_chunk_act(act, x_b, 6)
                if has(front_b):
                    a_squares_q_act(act, front_b, par)
                if has(front_b) and not early(front_b, LF - 1):
                    a_values_act(act, front_b)
                if has(x_b):
                    x_chunk_act(act, x_b, 7)
                if has(x_b):
                    x_chunk_act(act, x_b, 8)
                if has(front_b):
                    a_keys_act(act, front_b, range(2 if early(front_b, LF - 1) else 0))
                if has(mix_b):
                    apply(act, Bp, nyb, mix_b, odd, yb, tmpb)
                if has(x_b):
                    x_chunk_act(act, x_b, 9)
                if has(rec_b):
                    apply(act, C, nyc, rec_b, par, yc, tmpc)
                if has(x_b):
                    for k in range(10, NJ):
                        x_chunk_act(act, x_b, k)

            together(act, iteration)

        @block.tensor
        def _(pe):
            pe.wait_ge(l_consts, 32)

            def sorf_map(b):
                if not first(b):
                    return
                for n in range(2):
                    pe.wait_ge(s_sorf_v, n + 1)
                    if n == 0:
                        pe.matmul(banks[1][0:PP, 0:P], had, sorf_a[:, :, :], start=True, stop=True).then_inc(s_sorf_p, 1)
                    else:
                        for h in range(2):
                            ins = pe.matmul(banks[2][0:PP, h * M:(h + 1) * M],
                                            sorf_b[:, h * HH:(h + 1) * HH, :].rearrange("p h d -> p (h d)"),
                                            had[:, 0:M], start=True, stop=True)
                        ins.then_inc(s_sorf_p, 1)

            def feature_weights(b):
                if first(b):
                    pe.wait_ge(s_sorf_v, 6)

            def iteration(i, par):
                odd, (out_b, x_b, route_b, rec_b, mix_b, query_b, key_b, front_b) = 1 - par, lags(i)
                if has(key_b):
                    feature_weights(key_b)
                    a_keys_pe(pe, key_b, range(0, 2))
                if has(out_b):
                    x_tail_pe(pe, out_b)
                if has(key_b):
                    a_keys_pe(pe, key_b, range(2, TPB))
                if has(mix_b) and not late(i):
                    b_front_pe(pe, mix_b)
                if has(key_b):
                    a_keys_pe(pe, key_b, range(TPB, TPB + 1))
                if has(query_b):
                    a_query_pe(pe, query_b, par, range(0, 1))
                if has(rec_b) and not late(i):
                    c_front_pe(pe, rec_b)
                if has(query_b):
                    a_query_pe(pe, query_b, par, range(1, 3))
                if has(x_b) and not late(i):
                    r_weights_pe(pe, x_b)
                if has(query_b):
                    a_query_pe(pe, query_b, par, range(3, NG + 1))
                if has(x_b):
                    x_chunk_pe(pe, x_b, par, 0)
                if has(mix_b) and not late(i):
                    b_key_pe(pe, mix_b)
                if has(rec_b) and not late(i):
                    c_in_pe(pe, rec_b)
                if has(mix_b) and late(i):
                    b_front_pe(pe, mix_b)
                if has(front_b) and early(front_b, LF - 1):
                    a_front_pe(pe, front_b)
                if has(x_b):
                    x_chunk_pe(pe, x_b, par, 1)
                if has(rec_b) and late(i):
                    c_front_pe(pe, rec_b)
                if has(x_b) and late(i):
                    r_weights_pe(pe, x_b)
                if has(query_b):
                    a_back_pe(pe, query_b)
                if has(x_b):
                    x_chunk_pe(pe, x_b, par, 2)
                if has(front_b) and not early(front_b, LF - 1):
                    a_front_pe(pe, front_b)
                if has(front_b):
                    sorf_map(front_b)
                if has(query_b):
                    a_out_pe(pe, query_b)
                if has(mix_b) and late(i):
                    b_key_pe(pe, mix_b)
                if has(rec_b) and late(i):
                    c_in_pe(pe, rec_b)
                if has(x_b):
                    x_chunk_pe(pe, x_b, par, 3)
                if has(front_b):
                    a_products_pe(pe, front_b, 0)
                if has(front_b) and early(front_b, LF - 1):
                    a_products_pe(pe, front_b, 1)
                if has(x_b):
                    x_chunk_pe(pe, x_b, par, 4)
                if has(front_b) and early(front_b, LF - 1):
                    a_values_pe(pe, front_b)
                if has(route_b):
                    r_front_pe(pe, route_b)
                if has(mix_b):
                    b_in_pe(pe, mix_b)
                if has(x_b):
                    x_chunk_pe(pe, x_b, par, 5)
                if has(front_b) and not early(front_b, LF - 1):
                    a_products_pe(pe, front_b, 1)
                if has(x_b):
                    x_chunk_pe(pe, x_b, par, 6)
                if has(front_b) and not early(front_b, LF - 1):
                    a_values_pe(pe, front_b)
                if has(mix_b):
                    b_value_pe(pe, mix_b)
                if has(x_b):
                    x_chunk_pe(pe, x_b, par, 7)
                if has(rec_b):
                    c_out_pe(pe, rec_b, par)
                if has(x_b):
                    x_chunk_pe(pe, x_b, par, 8)
                if has(route_b):
                    r_logits_pe(pe, route_b, odd)
                if has(x_b):
                    for k in range(9, NJ):
                        x_chunk_pe(pe, x_b, par, k)

            together(pe, iteration)

        @block.vector
        def _(dve):
            dve.wait_ge(l_consts, 32)
            dve.wait_ge(b_zero, 1)

            def sorf_map(b):
                if not first(b):
                    return
                dve.wait_ge(l_attn, 4 * 16)
                dve.tensor_tensor(sorf_a[:, :, :], had[:, 0:DH].unsqueeze(1).broadcast_to([PP, H, DH]),
                                  s23_sb[:, 0, :].unsqueeze(2).broadcast_to([PP, H, DH]), ALU.mult).then_inc(s_sorf_v, 1)
                dve.wait_ge(s_sorf_p, 1)
                dve.tensor_tensor(sorf_b[:, :, :], banks[1][0:PP, 0:P].rearrange("p (h d) -> p h d", h=H),
                                  s23_sb[:, 1, :].unsqueeze(2).broadcast_to([PP, H, DH]), ALU.mult).then_inc(s_sorf_v, 1)
                dve.wait_ge(s_sorf_p, 2)
                for h in range(2):
                    ins = dve.tensor_scalar(sorf_c[:, h, :], banks[2][0:PP, h * M:(h + 1) * M], s1_sb[:, h:h + 1],
                                            1.0 / PP ** 2, ALU.mult, ALU.mult)
                ins.then_inc(s_sorf_v, 1)
                dve.wait_ge(s_sorf_v, 3)
                dve.tensor_tensor(sorf_d[:, :, :], sorf_c[:, :, :], scl_sb[:, :, :], ALU.mult).then_inc(s_sorf_v, 1)
                dve.wait_ge(s_sorf_v, 4)
                m8 = cst[:, C_M8:C_M8 + HH]
                for h in range(2):
                    ins = dve.tensor_tensor(feat[0:PP, h, :, :], sorf_d[:, h, :].unsqueeze(1).broadcast_to([PP, HH, M]),
                                            m8[0:PP].unsqueeze(2).broadcast_to([PP, HH, M]), ALU.mult)
                ins.then_inc(s_sorf_v, 1)
                for h in range(2):
                    ins = dve.tensor_copy(feat[PP:P, h, :, :], m8[PP:P].unsqueeze(2).broadcast_to([PP, HH, M]))
                ins.then_inc(s_sorf_v, 1)

            def small_weights(b):
                if not first(b):
                    return
                dve.wait_ge(l_mix, 4 * 16)
                dve.wait_ge(l_rec, 5 * 16)
                dve.tensor_scalar(blh_sb[:, :], bl_sb[:, :], 0.5, None, ALU.mult).then_inc(s_blh, 1)

            def split_w(hi, lo, src, k):
                dve.tensor_copy(hi[:, :], src[:, :]).then_inc(s_wsplit, 1)
                dve.wait_ge(s_wsplit, k + 1)
                dve.tensor_tensor(lo[:, :], src[:, :], hi[:, :].bitcast(F32), ALU.subtract).then_inc(s_wsplit, 1)

            def split_router(b):
                if first(b):
                    split_w(gate_hi, gate_lo, gate_sb, 4)

            def split_gate(b):
                if first(b):
                    dve.wait_ge(l_gate, 16)
                    split_w(wg_hi, wg_lo, wstage, 0)

            def split_up(b):
                if first(b):
                    dve.wait_ge(l_up, 16)
                    split_w(wu_hi, wu_lo, wstage, 2)

            def a_stats(b, par):
                if isinstance(b, int) and b < 3:
                    dve.wait_ge(l_x[b], 16)
                stats(dve, na, b, par, lambda i: tile(xres, b, i), A.bn, A.mv)

            def iteration(i, par):
                odd, (out_b, x_b, route_b, rec_b, mix_b, query_b, key_b, front_b) = 1 - par, lags(i)
                if has(front_b) and early(front_b, LF - LQ):
                    a_stats(front_b, par)
                if has(mix_b):
                    b_stats_dve(dve, mix_b, odd)
                if has(rec_b) and not early(rec_b, LC):
                    c_stats_dve(dve, rec_b, par)
                if has(mix_b):
                    normalise(dve, Bp, nb, mix_b, odd, xnb)
                if has(front_b) and early(front_b, LF - LQ):
                    normalise(dve, A, na, front_b, par, xna)
                if has(rec_b) and early(rec_b, LC):
                    c_stats_dve(dve, rec_b, par)
                if has(x_b) and early(x_b, 0):
                    r_top_dve(dve, x_b)
                if has(rec_b):
                    normalise(dve, C, ncx, rec_b, par, xnc)
                if has(x_b) and not early(x_b, 0):
                    r_top_dve(dve, x_b)
                if has(key_b):
                    a_state_dve(dve, key_b, odd)
                if has(mix_b) and not late(i):
                    b_mix_dve(dve, mix_b, odd)
                if has(front_b) and not early(front_b, LF - LQ):
                    a_stats(front_b, par)
                if has(query_b):
                    a_divide_dve(dve, query_b, 0)
                    a_divide_dve(dve, query_b, 1)
                if has(front_b) and not early(front_b, LF - LQ):
                    normalise(dve, A, na, front_b, par, xna)
                if has(route_b):
                    split_router(route_b)
                if has(front_b):
                    sorf_map(front_b)
                if has(query_b):
                    small_weights(query_b)
                    split_gate(query_b)
                if has(mix_b):
                    split_up(mix_b)
                if has(x_b):
                    x_chunk_dve(dve, x_b, 0)
                if has(route_b):
                    r_stats_dve(dve, route_b, odd)
                if has(mix_b) and late(i):
                    b_mix_dve(dve, mix_b, odd)
                if has(x_b):
                    x_chunk_dve(dve, x_b, 1)
                if has(rec_b) and not late(i):
                    c_scan_dve(dve, rec_b, par)
                if has(out_b):
                    x_ystats_dve(dve, out_b, odd)
                if has(x_b):
                    x_chunk_dve(dve, x_b, 2)
                if has(route_b):
                    normalise(dve, R, nr, route_b, odd, xnr)
                if has(rec_b) and late(i):
                    c_scan_dve(dve, rec_b, par)
                if has(x_b):
                    x_chunk_dve(dve, x_b, 3)
                if has(query_b):
                    stats(dve, nya, query_b, par, lambda i: ya[:, i * P:(i + 1) * P], A.ybn, A.ymv, a_yc)
                if has(front_b):
                    a_cat_dve(dve, front_b, par, 0)
                if has(x_b):
                    x_chunk_dve(dve, x_b, 4)
                if has(x_b):
                    x_chunk_dve(dve, x_b, 5)
                if has(route_b):
                    r_lo_dve(dve, route_b, odd)
                if has(front_b):
                    a_cat_dve(dve, front_b, par, 1)
                if has(x_b):
                    x_chunk_dve(dve, x_b, 6)
                if has(x_b):
                    x_chunk_dve(dve, x_b, 7)
                if has(mix_b):
                    b_gate_dve(dve, mix_b, odd)
                if has(x_b):
                    x_chunk_dve(dve, x_b, 8)
                if has(rec_b):
                    c_y_dve(dve, rec_b)
                    c_ystats_dve(dve, rec_b, par)
                if has(x_b):
                    x_chunk_dve(dve, x_b, 9)
                if has(route_b):
                    r_scores_dve(dve, route_b)
                if has(x_b):
                    for k in range(10, NJ):
                        x_chunk_dve(dve, x_b, k)

            together(dve, iteration)


def constants():
    c = np.zeros((P, C_N), np.float32)
    freqs = np.float32(10000.0) ** (-np.arange(0, DH, 2, dtype=np.float32) / np.float32(DH))
    ang = np.arange(L - 1, dtype=np.float32)[:, None] * freqs.astype(np.float32)
    ang = np.concatenate([np.zeros((1, DH // 2), np.float32), ang]).astype(np.float64)
    ch = np.arange(P)
    pair = (ch % DH) // 2
    c[:, C_COS:C_COS + L] = np.cos(ang)[:, pair].T
    c[:, C_SIN:C_SIN + L] = np.sin(ang)[:, pair].T * np.where(ch % 2 == 0, -1.0, 1.0)[:, None]
    c[:, C_ID:C_ID + P] = np.eye(P)
    had = np.ones((1, 1))
    while had.shape[0] < PP:
        had = np.block([[had, had], [had, -had]])
    c[0:PP, C_HAD:C_HAD + PP] = had
    own = (np.arange(PP)[:, None] // DH) == np.arange(HH)[None, :]
    c[0:PP, C_M8:C_M8 + HH] = own
    c[PP:P, C_M8:C_M8 + HH] = -0.5 * own
    c[:, C_M4:C_M4 + GH] = ((ch[:, None] // M) == np.arange(GH)[None, :]) / float(M)
    return c


def kernel(L0_attn_x, L0_attn_w_qkv, L0_attn_w_out, L0_attn_sorf_signs, L0_attn_sorf_scales, L0_ffn_W_r, L0_ffn_W_k,
           L0_ffn_W_v, L0_ffn_mu_r, L0_ffn_mu_k, L1_attn_Wl, L1_attn_bl, L1_attn_Wb, L1_attn_Wc, L1_attn_Dp,
           L1_ffn_gate_w, L1_ffn_w_gate, L1_ffn_w_up, L1_ffn_w_down, L1_ffn_sw_gate, L1_ffn_sw_up, L1_ffn_sw_down):
    import concourse.bacc as bacc
    from concourse.bass_utils import run_bass_kernel_spmd

    swap = np.arange(D).reshape(-1, 2)[:, ::-1].reshape(-1)
    q, k, v = (np.asarray(L0_attn_w_qkv)[i * D:(i + 1) * D] for i in range(3))
    signs = np.asarray(L0_attn_sorf_signs)[:, 0]
    scales = np.asarray(L0_attn_sorf_scales)[:, 0, 0:M]

    def experts(w, shared):
        w = np.asarray(w).reshape(E, D, JE, EQ).transpose(1, 2, 0, 3).reshape(D, E * F)
        return np.concatenate([w, np.asarray(shared)], axis=1)

    arrays = {
        "x": np.asarray(L0_attn_x).reshape(NB, TB, D),
        "wqkv": np.concatenate([q, q[swap], k, k[swap], v]).T,
        "wout": np.asarray(L0_attn_w_out).T,
        "consts": constants(),
        "s1c": signs[:, 0, 0:DH].reshape(2, PP).T,
        "s23": signs[:, 1:3].transpose(2, 1, 0),
        "scl": np.broadcast_to(scales.reshape(2, HH, 1, M), (2, HH, DH, M)).transpose(1, 2, 0, 3).reshape(PP, 2, M),
        "wr": np.asarray(L0_ffn_W_r).T, "wk": np.asarray(L0_ffn_W_k).T, "wv": np.asarray(L0_ffn_W_v).T,
        "mu": np.stack([np.asarray(L0_ffn_mu_r), np.asarray(L0_ffn_mu_k)], axis=1),
        "wlb": np.concatenate([np.asarray(L1_attn_Wl), np.asarray(L1_attn_Wb)]).T,
        "bl": np.asarray(L1_attn_bl).reshape(NS, 1),
        "wc": np.asarray(L1_attn_Wc).T,
        "dp": np.broadcast_to(np.asarray(L1_attn_Dp).reshape(1, D), (P, D)),
        "gate": np.asarray(L1_ffn_gate_w).T,
        "wg": experts(L1_ffn_w_gate, L1_ffn_sw_gate),
        "wu": experts(L1_ffn_w_up, L1_ffn_sw_up),
        "wd": np.concatenate([np.asarray(L1_ffn_w_down).reshape(E, JE, EQ, D).transpose(1, 0, 2, 3).reshape(E * F, D),
                              np.asarray(L1_ffn_sw_down)]),
    }
    nc = bacc.Bacc("TRN2", target_bir_lowering=False, num_devices=1)
    arrays = {n: np.ascontiguousarray(a) for n, a in arrays.items()}
    args = [nc.dram_tensor(n, a.shape, F32, kind="ExternalInput").ap() for n, a in arrays.items()]
    args.append(nc.dram_tensor("out", (NB, TB, D), F32, kind="ExternalOutput").ap())
    build(nc, *args)
    r = run_bass_kernel_spmd(nc, [arrays], core_ids=[0])
    return r.results[0]["out"].reshape(B, L, D)
```
